# Optimizing a Trainium2 kernel written in Bass

```python
import numpy as np
import jax
import jax.numpy as jnp

def _softmax(x, axis=-1):
    return jax.nn.softmax(x, axis=axis)

def _gelu(x):
    return jax.nn.gelu(x, approximate=True)

def _silu(x):
    return jax.nn.silu(x)

def _sigmoid(x):
    return jax.nn.sigmoid(x)

def _layernorm(x, axis=-1, eps=1e-05):
    m = jnp.mean(x, axis=axis, keepdims=True)
    v = jnp.var(x, axis=axis, keepdims=True)
    return (x - m) / jnp.sqrt(v + eps)

def _scatter_add(tgt, idx, src, axis=0):
    return tgt.at[idx].add(src)

def _segment_sum(src, seg, n):
    return jax.ops.segment_sum(src, seg, n)
kernel_name = 'mk_early_fusion_embed_d1_tok_img768_r4_f2aedc'

def setup_inputs(seed: int=0):
    np.random.seed(seed)
    _w = jnp.asarray

    def _rec_inputs():
        import jax
        import jax.numpy as jnp
        _rk = jax.random.key(seed)
        x = -0.000348323 + 0.999952 * jax.random.normal(jax.random.fold_in(_rk, 1), (16, 3, 96, 96), jnp.float32)
        x_txt = jax.random.randint(jax.random.fold_in(_rk, 51), (16, 128), 0, 70, jnp.int32)
        return (x, x_txt)
    x, x_txt = _rec_inputs()

    def _L0_tok_setup():
        import jax, jax.numpy as jnp
        import numpy as np
        PATCH = 16

        def _shifted_concat(x):
            B, C, H, W = x.shape
            xp = jnp.pad(x, ((0, 0), (0, 0), (1, 1), (1, 1)))
            right = xp[:, :, 1:1 + H, 0:W]
            left = xp[:, :, 1:1 + H, 2:2 + W]
            down = xp[:, :, 0:H, 1:1 + W]
            up = xp[:, :, 2:2 + H, 1:1 + W]
            return jnp.concatenate([x, right, left, down, up], axis=1)

        def _patchify(x, p):
            B, C, H, W = x.shape
            h, w = (H // p, W // p)
            x = x.reshape(B, C, h, p, w, p)
            x = x.transpose(0, 2, 4, 3, 5, 1)
            return x.reshape(B, h * w, p * p * C)

        def _layernorm(x, gamma, beta, eps=1e-05):
            mu = jnp.mean(x, axis=-1, keepdims=True)
            var = jnp.var(x, axis=-1, keepdims=True)
            return (x - mu) * jax.lax.rsqrt(var + eps) * gamma + beta
        key = jax.random.key(seed)
        k1, k2 = jax.random.split(key)
        B, H, W = (32, 96, 96)
        patch_dim = PATCH * PATCH * 15
        d_hidn = 192
        x = jax.random.normal(k1, (B, 3, H, W), dtype=jnp.float32)
        gamma = jnp.ones((patch_dim,), dtype=jnp.float32)
        beta = jnp.zeros((patch_dim,), dtype=jnp.float32)
        W_ = jax.random.normal(k2, (patch_dim, d_hidn), dtype=jnp.float32) * patch_dim ** (-0.5)
        b = jnp.zeros((d_hidn,), dtype=jnp.float32)
        return {'x': x, 'gamma': gamma, 'beta': beta, 'W': W_, 'b': b}
    _L0_tok_all = _L0_tok_setup()
    _L0_tok_in = {k: v for k, v in _L0_tok_all.items() if k in ('gamma', 'beta', 'W', 'b')}
    del _L0_tok_all

    def _L0_txt_setup():
        import jax, jax.numpy as jnp
        import numpy as np
        import math
        D_MODEL = 192
        BASE = D_MODEL // 3

        def positional_encoding(seq_length, d_model, dtype=jnp.float32):
            pos = jnp.arange(seq_length, dtype=dtype)[:, None]
            i_even = jnp.arange(0, d_model, 2, dtype=dtype)
            inv = jnp.exp(-(i_even / d_model) * math.log(10000.0))
            ang = pos * inv
            pe = jnp.stack([jnp.sin(ang), jnp.cos(ang)], axis=-1)
            return pe.reshape(seq_length, d_model)
        key = jax.random.key(seed)
        k_tok, k_c, k_s, k_q, k_sp = jax.random.split(key, 5)
        tokens = jax.random.randint(k_tok, (64, 512), 0, 70, dtype=jnp.int64)
        scale = 1.0
        color_W = jax.random.normal(k_c, (4, BASE), dtype=jnp.float32) * scale
        shape_W = jax.random.normal(k_s, (4, BASE), dtype=jnp.float32) * scale
        quantity_W = jax.random.normal(k_q, (4, BASE), dtype=jnp.float32) * scale
        special_W = jax.random.normal(k_sp, (6, D_MODEL), dtype=jnp.float32) * scale
        return {'tokens': tokens, 'color_W': color_W, 'shape_W': shape_W, 'quantity_W': quantity_W, 'special_W': special_W}
    _L0_txt_all = _L0_txt_setup()
    _L0_txt_in = {k: v for k, v in _L0_txt_all.items() if k in ('color_W', 'shape_W', 'quantity_W', 'special_W')}
    del _L0_txt_all

    def _L0_attn_setup():
        import jax, jax.numpy as jnp
        import numpy as np
        import math
        H = 12

        def _ln(x, w, b, eps=1e-05):
            mu = x.mean(-1, keepdims=True)
            var = ((x - mu) ** 2).mean(-1, keepdims=True)
            return (x - mu) / jnp.sqrt(var + eps) * w + b

        def _reference_tuple_inner(x, Wqkv, bqkv, Wb1, Wb2, temperature, Wproj, bproj, ln_w, ln_b, mn_w, mn_b):
            B, L, D = x.shape
            d = D // H
            x_norm = _ln(x, ln_w, ln_b)
            qkv = x_norm @ Wqkv + bqkv
            q, k, v = jnp.split(qkv, 3, axis=-1)
            params = (jax.nn.silu(x @ Wb1) @ Wb2).reshape(B, L, H, 5)
            sem_amp = jax.nn.sigmoid(params[..., 0])
            sem_phase = jnp.tanh(params[..., 1]) * math.pi
            ctx_amp = jax.nn.sigmoid(params[..., 2])
            ctx_phase = jnp.tanh(params[..., 3]) * math.pi
            temp = jnp.clip(temperature, 0.1, 2.0)
            interference = jnp.tanh(sem_amp * ctx_amp * jnp.cos(sem_phase - ctx_phase)) * temp
            gate = jax.nn.sigmoid(interference)
            q_f = (jax.nn.elu(q) + 1.0).reshape(B, L, H, d)
            k_f = (jax.nn.elu(k) + 1.0).reshape(B, L, H, d)
            v_f = v.reshape(B, L, H, d)
            kv_gated = jnp.einsum('blhd,blhe->blhde', k_f, v_f) * (1.0 + gate)[..., None, None]
            kv_states = jnp.cumsum(kv_gated, axis=1)
            z_states = jnp.cumsum(k_f, axis=1)
            out_num = jnp.einsum('blhd,blhde->blhe', q_f, kv_states)
            den = jnp.sum(q_f * z_states, axis=-1, keepdims=True) + 1e-06
            out = _ln(out_num / den, mn_w, mn_b)
            attn_out = out.reshape(B, L, D)
            return (attn_out @ Wproj + bproj, gate)
        key = jax.random.key(seed)
        B, L, D, R = (2, 256, 192, 128)
        d_head = D // H
        ks = jax.random.split(key, 6)
        s = 0.02
        return {'x': jax.random.normal(ks[0], (B, L, D), jnp.float32), 'Wqkv': jax.random.normal(ks[1], (D, 3 * D), jnp.float32) * s, 'bqkv': jnp.zeros((3 * D,), jnp.float32), 'Wb1': jax.random.normal(ks[2], (D, R), jnp.float32) * s, 'Wb2': jax.random.normal(ks[3], (R, H * 5), jnp.float32) * s, 'temperature': jnp.ones((1,), jnp.float32) * 0.5, 'Wproj': jax.random.normal(ks[4], (D, D), jnp.float32) * s, 'bproj': jnp.zeros((D,), jnp.float32), 'ln_w': jnp.ones((D,), jnp.float32), 'ln_b': jnp.zeros((D,), jnp.float32), 'mn_w': jnp.ones((d_head,), jnp.float32), 'mn_b': jnp.zeros((d_head,), jnp.float32)}
    _L0_attn_all = _L0_attn_setup()
    _L0_attn_in = {k: v for k, v in _L0_attn_all.items() if k in ('Wqkv', 'bqkv', 'Wb1', 'Wb2', 'temperature', 'Wproj', 'bproj', 'ln_w', 'ln_b', 'mn_w', 'mn_b')}
    del _L0_attn_all

    def _L0_ffn_setup():
        import jax, jax.numpy as jnp
        import numpy as np
        B, N, D, E, F, K = (2, 512, 192, 8, 768, 2)
        V_MAX = 3.0
        FEAT_CLAMP = 10.0

        def bk_green_diag(a):
            aT = jnp.swapaxes(a, 0, 1)

            def step(c, ai):
                d = ai - 1.0 / c
                return (d, d)
            d0 = aT[0]
            _, d_rest = jax.lax.scan(step, d0, aT[1:])
            d = jnp.concatenate([d0[None], d_rest], axis=0)
            eN = aT[-1]
            _, e_rest = jax.lax.scan(step, eN, aT[:-1], reverse=True)
            e = jnp.concatenate([e_rest, eN[None]], axis=0)
            G = 1.0 / (d + e - aT)
            return jnp.swapaxes(G, 0, 1)
        key = jax.random.key(seed)
        ks = jax.random.split(key, 8)
        s = lambda k, shape, sc: jax.random.normal(k, shape, jnp.float32) * sc
        return {'x': s(ks[0], (B, N, D), 1.0), 'v_w': s(ks[1], (D,), 0.02), 'v_b': jnp.zeros((), jnp.float32), 'gate_w': s(ks[2], (D, E), 0.02), 'gate_b': jnp.zeros((E,), jnp.float32), 'w1': s(ks[3], (E, D, F), 0.02), 'b1': jnp.zeros((E, F), jnp.float32), 'w2': s(ks[4], (E, F, D), 0.02), 'b2': jnp.zeros((E, D), jnp.float32), 'out_w': s(ks[5], (2, D), 0.02), 'out_b': jnp.zeros((D,), jnp.float32), 'bk_scale': jnp.ones((D,), jnp.float32)}
    _L0_ffn_all = _L0_ffn_setup()
    _L0_ffn_in = {k: v for k, v in _L0_ffn_all.items() if k in ('v_w', 'v_b', 'gate_w', 'gate_b', 'w1', 'b1', 'w2', 'b2', 'out_w', 'out_b', 'bk_scale')}
    del _L0_ffn_all
    return {'x': x, 'x_txt': x_txt, 'L0_tok_gamma': _L0_tok_in['gamma'], 'L0_tok_beta': _L0_tok_in['beta'], 'L0_tok_W': _L0_tok_in['W'], 'L0_tok_b': _L0_tok_in['b'], 'L0_txt_color_W': _L0_txt_in['color_W'], 'L0_txt_shape_W': _L0_txt_in['shape_W'], 'L0_txt_quantity_W': _L0_txt_in['quantity_W'], 'L0_txt_special_W': _L0_txt_in['special_W'], 'L0_attn_Wqkv': _L0_attn_in['Wqkv'], 'L0_attn_bqkv': _L0_attn_in['bqkv'], 'L0_attn_Wb1': _L0_attn_in['Wb1'], 'L0_attn_Wb2': _L0_attn_in['Wb2'], 'L0_attn_temperature': _L0_attn_in['temperature'], 'L0_attn_Wproj': _L0_attn_in['Wproj'], 'L0_attn_bproj': _L0_attn_in['bproj'], 'L0_attn_ln_w': _L0_attn_in['ln_w'], 'L0_attn_ln_b': _L0_attn_in['ln_b'], 'L0_attn_mn_w': _L0_attn_in['mn_w'], 'L0_attn_mn_b': _L0_attn_in['mn_b'], 'L0_ffn_v_w': _L0_ffn_in['v_w'], 'L0_ffn_v_b': _L0_ffn_in['v_b'], 'L0_ffn_gate_w': _L0_ffn_in['gate_w'], 'L0_ffn_gate_b': _L0_ffn_in['gate_b'], 'L0_ffn_w1': _L0_ffn_in['w1'], 'L0_ffn_b1': _L0_ffn_in['b1'], 'L0_ffn_w2': _L0_ffn_in['w2'], 'L0_ffn_b2': _L0_ffn_in['b2'], 'L0_ffn_out_w': _L0_ffn_in['out_w'], 'L0_ffn_out_b': _L0_ffn_in['out_b'], 'L0_ffn_bk_scale': _L0_ffn_in['bk_scale']}

def reference(x, x_txt, L0_tok_gamma, L0_tok_beta, L0_tok_W, L0_tok_b, L0_txt_color_W, L0_txt_shape_W, L0_txt_quantity_W, L0_txt_special_W, L0_attn_Wqkv, L0_attn_bqkv, L0_attn_Wb1, L0_attn_Wb2, L0_attn_temperature, L0_attn_Wproj, L0_attn_bproj, L0_attn_ln_w, L0_attn_ln_b, L0_attn_mn_w, L0_attn_mn_b, L0_ffn_v_w, L0_ffn_v_b, L0_ffn_gate_w, L0_ffn_gate_b, L0_ffn_w1, L0_ffn_b1, L0_ffn_w2, L0_ffn_b2, L0_ffn_out_w, L0_ffn_out_b, L0_ffn_bk_scale):
    import jax
    import jax.numpy as jnp

    def _L0_tok_ref(x, gamma, beta, W, b):
        import jax, jax.numpy as jnp
        import numpy as np
        PATCH = 16

        def _shifted_concat(x):
            B, C, H, W = x.shape
            xp = jnp.pad(x, ((0, 0), (0, 0), (1, 1), (1, 1)))
            right = xp[:, :, 1:1 + H, 0:W]
            left = xp[:, :, 1:1 + H, 2:2 + W]
            down = xp[:, :, 0:H, 1:1 + W]
            up = xp[:, :, 2:2 + H, 1:1 + W]
            return jnp.concatenate([x, right, left, down, up], axis=1)

        def _patchify(x, p):
            B, C, H, W = x.shape
            h, w = (H // p, W // p)
            x = x.reshape(B, C, h, p, w, p)
            x = x.transpose(0, 2, 4, 3, 5, 1)
            return x.reshape(B, h * w, p * p * C)

        def _layernorm(x, gamma, beta, eps=1e-05):
            mu = jnp.mean(x, axis=-1, keepdims=True)
            var = jnp.var(x, axis=-1, keepdims=True)
            return (x - mu) * jax.lax.rsqrt(var + eps) * gamma + beta
        xs = _shifted_concat(x)
        tokens = _patchify(xs, PATCH)
        normed = _layernorm(tokens, gamma, beta)
        return jnp.einsum('bnd,de->bne', normed, W) + b

    def _L0_txt_ref(tokens, color_W, shape_W, quantity_W, special_W):
        import jax, jax.numpy as jnp
        import numpy as np
        import math
        D_MODEL = 192
        BASE = D_MODEL // 3

        def positional_encoding(seq_length, d_model, dtype=jnp.float32):
            pos = jnp.arange(seq_length, dtype=dtype)[:, None]
            i_even = jnp.arange(0, d_model, 2, dtype=dtype)
            inv = jnp.exp(-(i_even / d_model) * math.log(10000.0))
            ang = pos * inv
            pe = jnp.stack([jnp.sin(ang), jnp.cos(ang)], axis=-1)
            return pe.reshape(seq_length, d_model)
        B, S = tokens.shape
        d_model = special_W.shape[1]
        t = jnp.minimum(tokens, 63)
        color = t // 16
        shape = t % 16 // 4
        quantity = t % 4
        feat_emb = jnp.concatenate([color_W[color], shape_W[shape], quantity_W[quantity]], axis=-1)
        sp_idx = jnp.clip(tokens - 64, 0, special_W.shape[0] - 1)
        spec_emb = special_W[sp_idx]
        emb = jnp.where((tokens < 64)[..., None], feat_emb, spec_emb)
        pe = positional_encoding(S, d_model, dtype=emb.dtype)
        out = emb * jnp.asarray(math.sqrt(d_model), emb.dtype) + pe[None, :, :]
        return out

    def _L0_attn_ref(x, Wqkv, bqkv, Wb1, Wb2, temperature, Wproj, bproj, ln_w, ln_b, mn_w, mn_b):
        import jax, jax.numpy as jnp
        import numpy as np
        import math
        H = 12

        def _ln(x, w, b, eps=1e-05):
            mu = x.mean(-1, keepdims=True)
            var = ((x - mu) ** 2).mean(-1, keepdims=True)
            return (x - mu) / jnp.sqrt(var + eps) * w + b

        def _reference_tuple_inner(x, Wqkv, bqkv, Wb1, Wb2, temperature, Wproj, bproj, ln_w, ln_b, mn_w, mn_b):
            B, L, D = x.shape
            d = D // H
            x_norm = _ln(x, ln_w, ln_b)
            qkv = x_norm @ Wqkv + bqkv
            q, k, v = jnp.split(qkv, 3, axis=-1)
            params = (jax.nn.silu(x @ Wb1) @ Wb2).reshape(B, L, H, 5)
            sem_amp = jax.nn.sigmoid(params[..., 0])
            sem_phase = jnp.tanh(params[..., 1]) * math.pi
            ctx_amp = jax.nn.sigmoid(params[..., 2])
            ctx_phase = jnp.tanh(params[..., 3]) * math.pi
            temp = jnp.clip(temperature, 0.1, 2.0)
            interference = jnp.tanh(sem_amp * ctx_amp * jnp.cos(sem_phase - ctx_phase)) * temp
            gate = jax.nn.sigmoid(interference)
            q_f = (jax.nn.elu(q) + 1.0).reshape(B, L, H, d)
            k_f = (jax.nn.elu(k) + 1.0).reshape(B, L, H, d)
            v_f = v.reshape(B, L, H, d)
            kv_gated = jnp.einsum('blhd,blhe->blhde', k_f, v_f) * (1.0 + gate)[..., None, None]
            kv_states = jnp.cumsum(kv_gated, axis=1)
            z_states = jnp.cumsum(k_f, axis=1)
            out_num = jnp.einsum('blhd,blhde->blhe', q_f, kv_states)
            den = jnp.sum(q_f * z_states, axis=-1, keepdims=True) + 1e-06
            out = _ln(out_num / den, mn_w, mn_b)
            attn_out = out.reshape(B, L, D)
            return (attn_out @ Wproj + bproj, gate)
        return _reference_tuple_inner(x, Wqkv, bqkv, Wb1, Wb2, temperature, Wproj, bproj, ln_w, ln_b, mn_w, mn_b)[0]

    def _L0_ffn_ref(x, v_w, v_b, gate_w, gate_b, w1, b1, w2, b2, out_w, out_b, bk_scale):
        import jax, jax.numpy as jnp
        import numpy as np
        B, N, D, E, F, K = (2, 512, 192, 8, 768, 2)
        V_MAX = 3.0
        FEAT_CLAMP = 10.0

        def bk_green_diag(a):
            aT = jnp.swapaxes(a, 0, 1)

            def step(c, ai):
                d = ai - 1.0 / c
                return (d, d)
            d0 = aT[0]
            _, d_rest = jax.lax.scan(step, d0, aT[1:])
            d = jnp.concatenate([d0[None], d_rest], axis=0)
            eN = aT[-1]
            _, e_rest = jax.lax.scan(step, eN, aT[:-1], reverse=True)
            e = jnp.concatenate([e_rest, eN[None]], axis=0)
            G = 1.0 / (d + e - aT)
            return jnp.swapaxes(G, 0, 1)
        v = jnp.clip(x @ v_w + v_b, -V_MAX, V_MAX)
        a = (-2.0 + v).astype(jnp.complex64) - 1j
        G = bk_green_diag(a)
        feats = jnp.stack([G.real, G.imag], axis=-1)
        logits = x @ gate_w + gate_b
        probs = jax.nn.softmax(logits, axis=-1)
        topv, topi = jax.lax.top_k(probs, K)
        topv = topv / jnp.sum(topv, axis=-1, keepdims=True)
        comb = jnp.sum(topv[..., None] * jax.nn.one_hot(topi, E, dtype=x.dtype), axis=2)
        h = jax.nn.gelu(jnp.einsum('bnd,edf->bnef', x, w1) + b1)
        y = jnp.einsum('bnef,efd->bned', h, w2) + b2
        ffn_out = jnp.einsum('bne,bned->bnd', comb, y)
        feats_c = jnp.clip(feats, -FEAT_CLAMP, FEAT_CLAMP)
        spec_out = feats_c @ out_w + out_b
        return ffn_out + bk_scale * spec_out
    h = _L0_tok_ref(x, L0_tok_gamma, L0_tok_beta, L0_tok_W, L0_tok_b)
    h = jnp.concatenate([h, _L0_txt_ref(x_txt, L0_txt_color_W, L0_txt_shape_W, L0_txt_quantity_W, L0_txt_special_W)], axis=1)
    h = h + _L0_attn_ref(_layernorm(h, axis=-1), L0_attn_Wqkv, L0_attn_bqkv, L0_attn_Wb1, L0_attn_Wb2, L0_attn_temperature, L0_attn_Wproj, L0_attn_bproj, L0_attn_ln_w, L0_attn_ln_b, L0_attn_mn_w, L0_attn_mn_b)
    h = h + _L0_ffn_ref(_layernorm(h, axis=-1), L0_ffn_v_w, L0_ffn_v_b, L0_ffn_gate_w, L0_ffn_gate_b, L0_ffn_w1, L0_ffn_b1, L0_ffn_w2, L0_ffn_b2, L0_ffn_out_w, L0_ffn_out_b, L0_ffn_bk_scale)
    return h

_drawn_inputs = setup_inputs


def setup_inputs(seed=0):
    import zlib

    import numpy as np

    out = dict(_drawn_inputs(seed))
    spreads = {'L0_tok_gamma': (1.0, 0.6),
     'L0_tok_beta': (0.0, 0.8),
     'L0_tok_b': (0.0, 0.8),
     'L0_attn_bqkv': (0.0, 0.369),
     'L0_attn_bproj': (0.0, 0.8),
     'L0_attn_ln_w': (1.0, 0.6),
     'L0_attn_ln_b': (0.0, 0.8),
     'L0_attn_mn_w': (1.0, 0.6),
     'L0_attn_mn_b': (0.0, 0.8),
     'L0_ffn_gate_b': (0.0, 0.8),
     'L0_ffn_b1': (0.0, 0.8),
     'L0_ffn_b2': (0.0, 0.8),
     'L0_ffn_out_b': (0.0, 0.8),
     'L0_ffn_bk_scale': (1.0, 0.6)}
    factors = {'L0_attn_Wqkv': 3.502,
     'L0_attn_Wb1': 64.0,
     'L0_attn_Wb2': 64.0,
     'L0_ffn_v_w': 64.0,
     'L0_ffn_gate_w': 8.0,
     'L0_ffn_w1': 8.0,
     'L0_ffn_w2': 8.0,
     'L0_ffn_out_w': 54.64}
    for name, (base, spread) in spreads.items():
        noise = np.random.default_rng([zlib.crc32(name.encode()), seed]).standard_normal(out[name].shape)
        drawn = base * np.exp(spread * noise) if base else spread * noise
        out[name] = jnp.asarray(drawn.astype(out[name].dtype))
    for name, factor in factors.items():
        out[name] = (out[name] * factor).astype(out[name].dtype)
    return out
```

```python
import concourse.bass as bass
from concourse import mybir
from contextlib import ExitStack

B, CH, IMG, PATCH = 16, 3, 96, 16
SIDE = IMG // PATCH
NI = SIDE * SIDE
NT = 128
L = NI + NT
D = 192
DH = D // 2
NH, HD = 12, 16
HH = NH // 2
VE = HD + 1
RANK = 128
TW = D + RANK
NE, FF = 8, 768
FC = FF // 128
SHIFTS = 5
PDIM = PATCH * PATCH * CH * SHIFTS
WIN = PATCH + 2
KP = 2 * CH * WIN
NK = WIN // 2
PAIRS = B // 2
SLOTS = 3 * PAIRS
PC = 2 * L
PT = 128 * PAIRS
TILES = NE + (2 * B * L - NE) // 128
SROWS = TILES * 128
ROW = D + 2
PLANE = B * L
GSTEP = 4
GLEN = TILES * GSTEP + 1
EPS = 1e-5

CW, NCONST = {}, 0
for _name, _n in (("pe", D), ("ident", 128), ("causal", 128), ("icausal", NI), ("before", 128), ("blk", HH * VE),
                  ("hmask", HH), ("mult", NK), ("iota8", NE), ("valid", SLOTS), ("trash", 2 * SLOTS),
                  ("place", 2 * SLOTS), ("tile8", (TILES + 2) * NE), ("tok", 1), ("steps", 2 * SLOTS), ("fill", ROW), ("sign", GLEN)):
    CW[_name] = (NCONST, NCONST + _n)
    NCONST += _n


class Chain:

    def __init__(self, eng, sem):
        self.eng, self.sem, self.base, self.k, self.i, self.per = eng, sem, 0, 0, None, 0

    def done(self, ins):
        ins.then_inc(self.sem, 1)
        self.k += 1

    def enter(self, per):
        self.base, self.k, self.i, self.per = self.base + self.k, 0, 0, per

    def leave(self, trips):
        assert self.k == self.per, (self.k, self.per)
        self.base, self.k, self.i = self.base + self.per * trips, 0, None

    def at(self, i):
        self.i = i

    def sync(self):
        value = self.base + self.k
        self.eng.wait_ge(self.sem, value if self.i is None else self.i * self.per + value)


def early_fusion_block(nc, a, out):
    F, BF = mybir.dt.float32, mybir.dt.bfloat16
    I32, U32 = mybir.dt.int32, mybir.dt.uint32
    ALU, ACT, AX = mybir.AluOpType, mybir.ActivationFunctionType, mybir.AxisListType
    ds = bass.ds

    sorted_rows = nc.dram_tensor("sorted_rows", (SROWS + 2 * PAIRS * 128, ROW), F, kind="Internal").ap()
    planes = nc.dram_tensor("planes", (2 * PLANE + 128, D), F, kind="Internal").ap()
    v_dram = nc.dram_tensor("v_dram", (B, L), F, kind="Internal").ap()
    g_dram = nc.dram_tensor("g_dram", (B, L, 2), F, kind="Internal").ap()

    ctx = ExitStack()
    with ctx:
        def sb(name, shape, dt=F):
            return ctx.enter_context(nc.sbuf_tensor(name, shape, dt))

        cst = sb("cst", [128, NCONST])

        def C(name, p=128):
            return cst[0:p, CW[name][0]:CW[name][1]]

        arena1 = sb("arena1", [128, NE * 2 * FF])
        xwin = arena1[0:KP, 0:NK * PT].rearrange("p (k n) -> p k n", k=NK)
        w1 = arena1[0:DH + 1, :].rearrange("p (h n) -> p h n", h=2)
        plane_in = arena1[:, 0:2 * SLOTS * D].rearrange("p (k s n) -> p k s n", k=2, n=D)
        arena2 = sb("arena2", [128, 4 * B * L])
        wpatch = arena2[0:KP, 0:SHIFTS * NK * D].rearrange("p (k n) -> p k n", n=D)
        qk = arena2[0:DH, :].rearrange("p (c n) -> p c n", c=4)
        w2 = arena2[:, 0:NE * FC * D].rearrange("p (f n) -> p f n", f=FC)
        rows = sb("rows", [128, 2, SLOTS, ROW])
        u = rows[:, 0, :, 2:ROW]
        p0 = rows[:, :, :, :].rearrange("p k s n -> p (k s n)")
        XS = NK * 128
        xsq = p0[0:KP, 0:2 * XS].rearrange("p (u k n) -> p u k n", u=2, k=NK)
        tok_f = p0[0:70, 2 * XS:2 * XS + B * NT]
        tokneg = p0[0:70, 2 * XS + B * NT:2 * XS + 2 * B * NT]

        h = sb("h", [128, SLOTS, D])
        vx = sb("vx", [128, SLOTS, NH, HD])
        vflat = vx[:, :, :, :].rearrange("p s h e -> p (s h e)")
        usq = vx[:, :, :, :].rearrange("p s h e -> p s (h e)")
        tok_i = vflat[0:70, 0:B * NT].bitcast(I32)

        used = {}

        def carve(phase, p, n, start=0):
            at = used.get(phase, start)
            used[phase] = at + n
            assert at + n <= NE * 2 * FF, (phase, at + n)
            return arena1[0:p, at:at + n]

        weff = carve("patch", KP, NK * (D + 1), NK * PT).rearrange("p (k n) -> p k n", k=NK)
        gb = carve("patch", KP, 2 * SHIFTS * NK)
        gsum = carve("patch", 128, D)
        tokb = carve("patch", 128, D)
        tb = carve("patch", 128, D)
        table = carve("patch", 70, D)
        istat = carve("patch", 128, 8 * PAIRS).rearrange("p (k g) -> p k g", k=8)

        xn = carve("attn", 128, 6 * D).rearrange("p (u s n) -> p u s n", u=2, s=3)
        xnT = carve("attn", DH, 4 * PC).rearrange("p (u h n) -> p u h n", u=2, h=2)
        ek = carve("attn", DH, 2 * PC).rearrange("p (u n) -> p u n", u=2)
        rk = carve("attn", DH, 2 * PC).rearrange("p (u n) -> p u n", u=2)
        th = carve("attn", 128, 2 * RANK).rearrange("p (u n) -> p u n", u=2)
        sg = carve("attn", 128, 2 * RANK).rearrange("p (u n) -> p u n", u=2)
        sgT = carve("attn", 128, 256).rearrange("p (u n) -> p u n", u=2)
        ximg = carve("attn", DH, 4 * 128).rearrange("p (u h n) -> p u h n", u=2, h=2)
        kimg = carve("attn", DH, 4 * 128).rearrange("p (u h n) -> p u h n", u=2, h=2)
        kst = carve("attn", DH, 4 * PC).rearrange("p (u h n) -> p u h n", u=2, h=2)
        qst = carve("attn", DH, 4 * PC).rearrange("p (u h n) -> p u h n", u=2, h=2)
        qbd = carve("attn", DH, 2 * HH * PC).rearrange("p (u h n) -> p u h n", u=2, h=HH)
        used["attn2"] = 0
        sm = carve("attn2", 128, 2 * 384).rearrange("p (u n) -> p u n", u=2)
        si = carve("attn2", 128, NH * NI + 64)
        kft = carve("attn2", 128, D)
        sbd = carve("attn2", DH, 4 * HH * VE).rearrange("p (b h n) -> p b h n", b=2, h=2)
        vst = carve("attn2", 128, 6 * NH * VE).rearrange("p (u s h e) -> p u s h e", u=2, s=3, h=NH)
        assert used["attn2"] <= 6 * D + 8 * PC + 6 * RANK

        ones = sb("ones", [128, 128])
        eps_t = sb("eps_t", [128, 1])
        st = sb("st", [128, SLOTS, 6])
        mv = sb("mv", [128, SLOTS, 2])
        ln = sb("ln", [128, 6, SLOTS])
        place_a = sb("place_a", [128, SLOTS * NH * 10])
        place_b = sb("place_b", [128, 2 * (4 * DH + TW)])
        place_c = sb("place_c", [128, 2 * (4 * DH + TW)])

        def within(place, start, p, n):
            assert start + n <= place.shape[1]
            return place[0:p, start:start + n]

        wraw = within(place_b, 0, DH, 2 * (4 * DH + TW)).rearrange("p (h n) -> p h n", h=2)
        wqk = within(place_c, 0, DH, 8 * DH).rearrange("p (h n) -> p h n", h=2)
        wtok = within(place_c, 8 * DH, DH, 2 * TW).rearrange("p (h n) -> p h n", h=2)
        lnwb = sb("lnwb", [DH, 4])
        bqk0 = sb("bqk0", [DH, 4])
        bqk = sb("bqk", [DH, 4])
        bv0 = sb("bv0", [128, D])
        bv = sb("bv", [128, D])
        wb2 = sb("wb2", [RANK, 5 * NH])
        temp = sb("temp", [128, 2])
        wp_raw = sb("wp_raw", [DH, 2, D])
        wp = sb("wp", [DH + 1, 2, D])
        mnwb = sb("mnwb", [DH, 2])
        bproj = sb("bproj", [128, D])
        gw = sb("gw", [DH + 1, 2, NE + 1])
        par = within(place_a, 0, 128, SLOTS * NH * 5).rearrange("p (s n) -> p s n", s=SLOTS)
        gt = within(place_a, SLOTS * NH * 5, 128, SLOTS * NH * 5).rearrange("p (k n) -> p k n", k=5)
        rden = sb("rden", [128, 3, NH])
        lnr = sb("lnr", [128, 3, SLOTS * NH])
        vat = [0]

        def carve_v(p, n):
            vat[0] += n
            assert vat[0] <= SLOTS * D
            return vflat[0:p, vat[0] - n:vat[0]]

        uh = carve_v(128, 6 * D).rearrange("p (u s n) -> p u s n", u=2, s=3)
        x2 = carve_v(128, 6 * D).rearrange("p (u s n) -> p u s n", u=2, s=3)
        oT = carve_v(DH + 1, 512).rearrange("p (u n) -> p u n", u=2)
        x2T = carve_v(DH + 1, 512).rearrange("p (u n) -> p u n", u=2)
        vat[0] = 0
        hid = carve_v(128, 2 * FF).rearrange("p (u n) -> p u n", u=2)
        hT = carve_v(128, 2 * FF).rearrange("p (u n) -> p u n", u=2)
        xgT = carve_v(DH + 1, 512).rearrange("p (u n) -> p u n", u=2)
        b2b = within(place_a, 0, 128, NE * D)
        xg = within(place_a, NE * D, 128, 2 * ROW).rearrange("p (u n) -> p u n", u=2)
        y1 = within(place_a, NE * D + 2 * ROW, 128, 2 * D).rearrange("p (u n) -> p u n", u=2)
        y2 = within(place_a, NE * D + 2 * ROW + 2 * D, 128, 2 * D).rearrange("p (u n) -> p u n", u=2)
        meta_w = sb("meta_w", [128, 4])
        meta_i = sb("meta_i", [128, 4], I32)
        spec = sb("spec", [128, 4, D])
        tail2 = NE * FC * D
        lg = within(arena2, tail2, 128, SLOTS * (NE + 1)).rearrange("p (s n) -> p s n", s=SLOTS)
        m8 = within(arena2, tail2 + SLOTS * 9, 128, SLOTS * 8).rearrange("p (s n) -> p s n", s=SLOTS)
        ix = within(arena2, tail2 + SLOTS * 17, 128, SLOTS * 8).bitcast(U32).rearrange("p (s n) -> p s n", s=SLOTS)
        ixf = sb("ixf", [128, 2, SLOTS])
        wk = sb("wk", [128, 2, SLOTS])
        beforeb = sb("beforeb", [128, 128], BF)
        onesb = sb("onesb", [128, 128], BF)
        ohf = within(place_b, 0, 128, 2 * SLOTS * NE).rearrange("p (s e) -> p s e", e=NE)
        ohb = sb("ohb", [128, 2 * SLOTS, NE], BF)
        tot = within(place_b, 2 * SLOTS * NE, 128, 2 * SLOTS * NE).rearrange("p (e s) -> p e s", e=NE)
        inc = within(place_b, 4 * SLOTS * NE, 128, 2 * SLOTS * NE).rearrange("p (e s) -> p e s", e=NE)
        cnt = sb("cnt", [128, 4, NE])
        pos = sb("pos", [128, 2 * SLOTS])
        sidx = sb("sidx", [128, 2 * SLOTS], I32)
        ecmp = within(place_c, 0, 1, (TILES + 2) * NE).rearrange("p (t e) -> p t e", e=NE)
        eidf = sb("eidf", [1, TILES + 2])
        eid = sb("eid", [1, TILES + 2], I32)
        vtok = sb("vtok", [128, SLOTS])
        ga = within(place_c, 0, 32, 2 * GLEN).rearrange("p (t c) -> p t c", c=2)
        gs = within(place_c, 2 * GLEN, 32, 2 * GLEN).rearrange("p (t c) -> p t c", c=2)
        ge = within(place_c, 4 * GLEN, B, 2 * L).rearrange("p (t c) -> p t c", c=2)
        vv = within(place_c, 4 * GLEN + 2 * L, 32, L)
        gq = sb("gq", [32, 4])
        gg = within(place_b, 0, B, 4 * L).rearrange("p (k n) -> p k n", k=4)
        g2 = within(place_b, 4 * L, B, 2 * L).rearrange("p (n k) -> p n k", k=2)
        pool_turn = sb("pool_turn", [1, TILES])
        gtok = sb("gtok", [128, SLOTS, 2])

        bank = [ctx.enter_context(nc.psum_tensor(f"bank{n}", [128, 512], F)) for n in range(8)]
        pbank = [bank[0], bank[1], bank[2], bank[5]]

        class Sems(dict):
            def __missing__(self, name):
                self[name] = ctx.enter_context(nc.semaphore(name))
                return self[name]

        s = Sems()
        for n in ("constants_in", "dve_chain", "act_chain", "pool_chain"):
            s[n]
        ctx.enter_context(nc.allow_non_contiguous_dma(reason="one value of every token"))
        block = ctx.enter_context(nc.Block())
        TXT = [(0, NI), (1, L + NI)]

        def slot_cols(t, k):
            if k < 2:
                return t[:, k * L + NI:(k + 1) * L]
            return t.rearrange("p (b n) -> p b n", b=2)[:, :, 0:64]

        SMALL = 14

        @block.sync
        def _(sp):
            sp.dma_start(cst[:, :], a["consts"]).then_inc(s["constants_in"], 16)
            sp.dma_start(tok_i, a["tokens"].partition_broadcast(70)).then_inc(s["tokens_in"], 16)
            sp.dma_start(wpatch, a["wpatch"]).then_inc(s["patch_weights_in"], 16)
            sp.dma_start(xwin, a["xwin"]).then_inc(s["windows_in"], 16)
            sp.wait_ge(s["constants_in"], 16)
            sp.dma_start(sorted_rows[0:SROWS + 256].rearrange("(t p) n -> p t n", p=128),
                         C("fill").unsqueeze(1).to_broadcast([128, TILES + 2, ROW])).then_inc(s["list_filled"], 16)
            sp.wait_ge(s["out_taken"], 1 + PAIRS)
            sp.dma_start(w1, a["w1"]).then_inc(s["w1_in"], 16)
            sp.dma_start(w2, a["w2"]).then_inc(s["w2_in"], 16)
            sp.dma_start(b2b, a["b2"]).then_inc(s["b2_in"], 16)
            def by_token(dram):
                return dram

            sp.wait_ge(s["v_ready"], 1)
            vt = vtok[:, :].rearrange("p (i k) -> p k i", k=3)
            vd = v_dram.rearrange("(i b) l -> b l i", b=2)
            for b in range(2):
                sp.dma_start(vd[b, NI:L], vt[:, b]).then_inc(s["v_out"], 16)
                sp.dma_start(vd[b, 0:NI], vt[64 * b:64 * b + NI, 2]).then_inc(s["v_out"], 16)
            sp.wait_ge(s["v_out"], 64)
            sp.dma_start(vv[0:B, :], v_dram).then_inc(s["v_in"], 16)
            sp.dma_start(vv[B:2 * B, :], v_dram[:, ::-1]).then_inc(s["v_in"], 16)

            sp.wait_ge(s["list_written"], 16 * 2 * SLOTS)
            for t in range(2):
                sp.dma_start(xg[:, t, :], sorted_rows[128 * t:128 * (t + 1)]).then_inc(s[f"xg_in{t}"], 16)
            with sp.Fori(0, TILES // 4) as it:
                for j in range(4):
                    t = it * 4 + j
                    sp.wait_ge(s["xgT_taken"], t + 1)
                    sp.dma_start(xg[:, j % 2, :], sorted_rows[ds(128 * (t + 2), 128), :]).then_inc(s[f"xg_in{j % 2}"], 16)
            sp.wait_ge(s["recurrence_done"], 1)
            sp.dma_start(ge[:, :, :], gs[B:2 * B, 0:L, :]).then_inc(s["ge_in"], 16)
            sp.wait_ge(s["green_ready"], 1)
            sp.dma_start(g_dram, g2[:, :, :]).then_inc(s["g_out"], 16)
            sp.wait_ge(s["g_out"], 16)
            gd = g_dram.rearrange("(i b) l c -> b l i c", b=2)
            gv = gtok[:, :, :].rearrange("p (i k) c -> p k i c", k=3)
            for b in range(2):
                sp.dma_start(gv[:, b], gd[b, NI:L]).then_inc(s["gtok_in"], 16)
                sp.dma_start(gv[64 * b:64 * b + NI, 2], gd[b, 0:NI]).then_inc(s["gtok_in"], 16)
            sp.wait_ge(s["l1_psum"], 2 + TILES + 1)
            for k in range(2):
                sp.wait_ge(s[f"plane_written{k}"], 8 * TILES)
            pd = planes[0:2 * PLANE].rearrange("(k i b l) n -> k b l i n", k=2, b=2, l=L)
            pv_ = plane_in.rearrange("p k (i j) n -> p k j i n", j=3)
            for k in range(2):
                for b in range(2):
                    sp.dma_start(pv_[:, k, b], pd[k, b, NI:L]).then_inc(s["planes_in"], 16)
                    sp.dma_start(pv_[64 * b:64 * b + NI, k, 2], pd[k, b, 0:NI]).then_inc(s["planes_in"], 16)
            sp.wait_ge(s["total_ready"], 1)
            od = out.rearrange("(i b) l n -> b l i n", b=2)
            hv = h[:, :, :].rearrange("p (i j) n -> p j i n", j=3)
            for b in range(2):
                sp.dma_start(od[b, NI:L], hv[:, b]).then_inc(s["out_written"], 16)
                sp.dma_start(od[b, 0:NI], hv[64 * b:64 * b + NI, 2]).then_inc(s["out_written"], 16)
            sp.wait_ge(s["out_written"], 64)

        @block.gpsimd
        def _(pool):
            nc.gpsimd.memset(ones[:, :], 1.0)
            nc.gpsimd.memset(eps_t[:, :], EPS).then_inc(s["filled"], 1)
            P = nc.gpsimd
            pool.sem_inc(s["x2_copied"], 2)
            with pool.Fori(0, PAIRS // 2) as it:
                for w in range(2):
                    i = it * 2 + w
                    pool.wait_ge(s["x2_ready"], i + 1)
                    P.tensor_copy(rows[:, 0, ds(3 * i, 3), 2:ROW], x2[:, w])
                    P.tensor_copy(rows[:, 1, ds(3 * i, 3), 2:ROW], x2[:, w]).then_inc(s["x2_copied"], 1)
            pool.wait_ge(s["x2_copied"], 2 + PAIRS)
            pool.wait_ge(s["list_filled"], 16)
            pool.wait_ge(s["places_ready"], 1)
            for k in range(2):
                for n in range(SLOTS):
                    pool.indirect_dma_start(out=sorted_rows,
                                            out_offset=bass.IndirectOffsetOnAxis(ap=sidx[:, k * SLOTS + n:k * SLOTS + n + 1].bitcast(U32), axis=0),
                                            in_=rows[:, k, n, :], in_offset=None).then_inc(s["list_written"], 16)
            pool.sem_inc(s["turn_taken"], 1)

            def write_tiles(it, first):
                for j in range(4):
                    t = it * 4 + j
                    pool.wait_ge(s["y2_ready"], 2 + t + 1)
                    if not (first and j == 0):
                        pool.wait_ge(s[f"plane_written{(j + 1) % 2}"], 32 * it + 16 * ((j + 1) // 2))
                    P.tensor_copy(pool_turn[:, ds(t, 1)], eps_t[0:1, :]).then_inc(s["turn_taken"], 1)
                    pool.indirect_dma_start(out=planes,
                                            out_offset=bass.IndirectOffsetOnAxis(ap=meta_i[:, j:j + 1].bitcast(U32), axis=0),
                                            in_=y2[:, j % 2, :], in_offset=None).then_inc(s[f"plane_written{j % 2}"], 16)

            write_tiles(0, True)
            with pool.Fori(1, TILES // 4) as it:
                write_tiles(it, False)

        @block.scalar
        def _(act):
            for dst, src in ((gb, "patch_gb"), (table, "table"), (tb, "tok_b"), (wraw[:, :, :], "wattn"),
                             (lnwb[:, :], "lnwb"), (bqk0[:, :], "bqk"), (bv0[:, :], "bv"), (wb2[:, :], "wb2"),
                             (wp_raw[:, :, :], "wproj"), (mnwb[:, :], "mnwb"), (bproj[:, :], "bproj"),
                             (temp[:, 0:1], "temp"), (gw[:, :, :], "gate_w"),
                             (spec[:, :, :], "spec")):
                act.dma_start(dst, a[src]).then_inc(s["small_in"], 16)
            act.wait_ge(s["windows_in"], 16)
            act.wait_ge(s["onehot_ready"], 1)
            for g in range(PAIRS):
                if g >= 2:
                    act.wait_ge(s["patch_sums"], g - 1)
                nc.scalar.activation(xsq[:, g % 2], xwin[:, :, 128 * g:128 * (g + 1)], ACT.Square).then_inc(s["squares_ready"], 1)
            act.wait_ge(s["filled"], 1)
            act.wait_ge(s["ivar_ready"], 1)
            nc.scalar.activation(istat[:, 4, :], istat[:, 3, :], ACT.Sqrt, bias=eps_t[:, :]).then_inc(s["isd_ready"], 1)
            act.wait_ge(s["stats_ready"], 1)
            nc.scalar.activation(ln[:, 0, :], mv[:, :, 1], ACT.Sqrt, bias=eps_t[:, :]).then_inc(s["sd_ready"], 1)
            act.wait_ge(s["varx_ready"], 1)
            nc.scalar.activation(ln[:, 3, :], ln[:, 2, :], ACT.Sqrt, bias=eps_t[:, :]).then_inc(s["sd_ready"], 1)

            A = nc.scalar
            act.sem_inc(s["xnT_taken"], 2)
            act.sem_inc(s["qk_taken"], 2)
            act.sem_inc(s["th_ready"], 2)
            act.sem_inc(s["sgT_taken"], 1)
            act.wait_ge(s["ln_ready"], 1)
            act.wait_ge(s["attn_weights_ready"], 1)
            with act.Fori(0, PAIRS // 2) as it:
                for par_i in range(2):
                    i, w = it * 2 + par_i, par_i
                    for k in range(3):
                        n, b = 3 * i + k, (w + k) % 2
                        act.wait_ge(s["xnT_psum"], 6 + n + 1)
                        if k == 0:
                            act.wait_ge(s["tok_psum"], 3 * i + 3)
                            act.wait_ge(s["qk_done"], 4 * i + 2)
                        src = bank[b][0:DH, 0:256].rearrange("p (h n) -> p h n", h=2)
                        if k < 2:
                            A.activation(xnT[:, w, :, k * L + NI:(k + 1) * L], src, ACT.Copy).then_inc(s["xnT_taken"], 1)
                        else:
                            A.activation(ximg[:, w], src, ACT.Copy)
                            for f in range(2):
                                last = A.activation(xnT[:, w, f, :].rearrange("p (b n) -> p b n", b=2)[:, :, 0:NI],
                                                    src[:, f, :].rearrange("p (b n) -> p b n", b=2)[:, :, 0:NI], ACT.Copy)
                            last.then_inc(s["xnT_taken"], 1)
                    for k in range(3):
                        n, b = 3 * i + k, (w + k) % 2
                        act.wait_ge(s["tok_psum"], 6 + n + 1)
                        act.wait_ge(s["tok_taken"], n + 1)
                        A.activation(th[:, b, :], bank[4 + b][:, D:TW], ACT.Tanh,
                                     scale=ln[:, 5, ds(n, 1)]).then_inc(s["th_ready"], 1)

                    def qk_take(c):
                        m = 4 * i + c
                        act.wait_ge(s["qk_psum"], m + 1)
                        act.wait_ge(s["qk_done"], 4 + m + 1)
                        A.activation(ek[:, c % 2, :], bank[2 + c % 2][0:DH, 0:PC], ACT.Exp, bias=bqk[:, c:c + 1])
                        A.activation(rk[:, c % 2, :], bank[2 + c % 2][0:DH, 0:PC], ACT.Relu,
                                     bias=bqk[:, c:c + 1]).then_inc(s["qk_taken"], 1)

                    def hidden_take(k):
                        n = 3 * i + k
                        act.wait_ge(s["sgT_psum"], 2 + n + 1)
                        act.wait_ge(s["par_psum"], n + 1)
                        A.activation(sgT[:, (w + k) % 2, :], bank[6][:, 0:128], ACT.Copy).then_inc(s["sgT_taken"], 1)

                    for c in range(4):
                        qk_take(c)
                        if c < 3:
                            hidden_take(c)

            act.wait_ge(s["par_taken"], 1 + SLOTS)
            pv = par[:, :, :].rearrange("p s (h k) -> p (s h) k", k=5)
            for k in range(4):
                last = A.activation(gt[:, k, :], pv[:, :, k], ACT.Tanh, scale=0.5 if k % 2 == 0 else 1.0)
            last.then_inc(s["gate_tanh"], 1)
            act.wait_ge(s["phase_ready"], 1)
            HALF_PI = 1.5707962
            A.activation(gt[:, 3, :], gt[:, 1, :], ACT.Sin, scale=HALF_PI).then_inc(s["sin_ready"], 1)
            act.wait_ge(s["inter_ready"], 1)
            A.activation(gt[:, 1, :], gt[:, 0, :], ACT.Tanh, scale=0.25).then_inc(s["inter_tanh"], 1)
            act.wait_ge(s["inter_tanh"], 1)
            A.activation(gt[:, 2, :], gt[:, 1, :], ACT.Tanh, scale=temp[:, 1:2]).then_inc(s["gate_ready"], 1)

            act.sem_inc(s["kft_taken"], 1)
            with act.Fori(0, PAIRS // 2) as it:
                for par_i in range(2):
                    i, w = it * 2 + par_i, par_i
                    act.wait_ge(s["qk_done"], 6 + 4 * PAIRS)
                    act.wait_ge(s["out_psum"], i + 1)
                    src = qk[:, :, ds(i * PC, PC)]
                    A.activation(kst[:, w], src[:, 2:4, :], ACT.Copy)
                    for f in range(2):
                        A.activation(kimg[:, w, f, :].rearrange("p (b n) -> p b n", b=2),
                                     src[:, 2 + f, :].rearrange("p (b n) -> p b n", b=2)[:, :, 0:64], ACT.Copy)
                    A.activation(qst[:, w], src[:, 0:2, :], ACT.Copy).then_inc(s["staged"], 1)
                    act.wait_ge(s["kft_psum"], i + 1)
                    act.wait_ge(s["state_psum"], i + 1)
                    A.activation(kft, bank[6][:, 0:D], ACT.Copy).then_inc(s["kft_taken"], 1)
                    act.wait_ge(s["uc_ready"], i + 1)
                    A.activation(usq[:, ds(3 * i, 3), :], u[:, ds(3 * i, 3), :], ACT.Square).then_inc(s["usq_ready"], 1)

            act.wait_ge(s["hvar_ready"], 1)
            A.activation(lnr[:, 2, :], lnr[:, 1, :], ACT.Sqrt, scale=1.0 / HD, bias=eps_t[:, :]).then_inc(s["hsd_ready"], 1)
            act.sem_inc(s["uhT_taken"], 2)
            act.sem_inc(s["x2T_taken"], 2)
            for psum, taken, used, dst in (("uhT_psum", "uhT_taken", "proj_psum", oT), ("x2T_psum", "x2T_taken", "logit_psum", x2T)):
                if dst is x2T:
                    act.wait_ge(s["means2_ready"], 1)
                    A.activation(ln[:, 0, :], mv[:, :, 1], ACT.Sqrt, bias=eps_t[:, :]).then_inc(s["sd2_ready"], 1)
                with act.Fori(0, PAIRS // 2) as it:
                    for j in range(6):
                        n = it * 6 + j
                        act.wait_ge(s[psum], 6 + n + 1)
                        act.wait_ge(s[used], n + 1)
                        A.activation(dst[0:DH, j % 2, :], bank[j % 2][0:DH, 0:256], ACT.Copy).then_inc(s[taken], 1)
            act.wait_ge(s["gap_ready"], 1)
            A.activation(wk[:, 1, :], wk[:, 0, :], ACT.Exp).then_inc(s["ratio_ready"], 1)

            act.sem_inc(s["hid_ready"], 2)
            act.sem_inc(s["y2_ready"], 2)

            def gelu(t, w):
                for f in range(2):
                    act.wait_ge(s["l1_psum"], 2 + t + 1)
                    act.wait_ge(s["hT_psum"], t + 1)
                    ins = A.activation(hid[:, w, 384 * f:384 * (f + 1)], bank[1 + 2 * w + f][:, 0:384], ACT.Gelu_apprx_tanh)
                ins.then_inc(s["hid_ready"], 1)

            gelu(0, 0)
            with act.Fori(0, TILES // 4) as it:
                for j in range(4):
                    t = it * 4 + j
                    gelu(t + 1, (j + 1) % 2)
                    act.wait_ge(s["y1_ready"], 1 + t + 1)
                    act.wait_ge(s["turn_taken"], t + 1)
                    A.activation(y2[:, j % 2, :], y1[:, j % 2, :], ACT.Copy, scale=meta_w[:, j:j + 1]).then_inc(s["y2_ready"], 1)

        @block.tensor
        def _(pe):
            pe.wait_ge(s["constants_in"], 16)
            pe.wait_ge(s["small_in"], 16 * SMALL)
            pe.wait_ge(s["filled"], 1)
            for c in range(4):
                for f in range(2):
                    last = nc.tensor.matmul(bank[3][0:DH, 100 + c:101 + c], wraw[:, f, DH * c:DH * (c + 1)],
                                            lnwb[:, 2 + f:3 + f], start=f == 0, stop=f == 1)
            for f in range(2):
                last = nc.tensor.matmul(bank[7][:, D:2 * D], lnwb[:, 2 + f:3 + f].to_broadcast([DH, 128]),
                                        wraw[:, f, 4 * DH:4 * DH + D], start=f == 0, stop=f == 1)
            for f in range(2):
                last = nc.tensor.matmul(bank[6][:, D:2 * D], mnwb[:, 1:2].to_broadcast([DH, 128]), wp_raw[:, f, :],
                                        start=f == 0, stop=f == 1)
            last.then_inc(s["attn_bias_sums"], 1)
            pe.wait_ge(s["onehot_ready"], 1)
            for b in range(B):
                if b >= 2:
                    pe.wait_ge(s["text_taken"], b - 1)
                nc.tensor.matmul(bank[4 + b % 2][:, 0:D], tok_f[:, NT * b:NT * (b + 1)], table, start=True,
                                 stop=True).then_inc(s["text_psum"], 1)
            pe.wait_ge(s["patch_weights_in"], 16)
            for c in range(SHIFTS * NK):
                last = nc.tensor.matmul(bank[6][:, 0:D], gb[:, SHIFTS * NK + c:SHIFTS * NK + c + 1].to_broadcast([KP, 128]),
                                        wpatch[:, c, :], start=c == 0, stop=c == SHIFTS * NK - 1)
            last.then_inc(s["beta_sums"], 1)
            pe.wait_ge(s["weff_ready"], 1)
            for k in range(NK):
                last = nc.tensor.matmul(bank[7][:, 0:D], ones[0:KP, :], weff[:, k, 0:D], start=k == 0, stop=k == NK - 1)
            last.then_inc(s["gain_sums"], 1)
            pe.wait_ge(s["windows_in"], 16)
            for g in range(PAIRS):
                if g == PAIRS - 2:
                    pe.wait_ge(s["text_taken"], B)
                for k in range(NK):
                    nc.tensor.matmul(pbank[g // 2][:, (D + 1) * (g % 2):(D + 1) * (g % 2 + 1)],
                                     xwin[:, k, 128 * g:128 * (g + 1)], weff[:, k, :], start=k == 0, stop=k == NK - 1)
                pe.wait_ge(s["squares_ready"], g + 1)
                for k in range(NK):
                    last = nc.tensor.matmul(bank[3][:, g:g + 1], xsq[:, g % 2, k, :], weff[:, k, D:D + 1],
                                            start=k == 0, stop=k == NK - 1)
                last.then_inc(s["patch_sums"], 1)

            pe.sem_inc(s["xnT_psum"], 6)
            pe.sem_inc(s["tok_psum"], 6)
            pe.sem_inc(s["sgT_psum"], 2)
            pe.sem_inc(s["par_psum"], 2)
            pe.wait_ge(s["attn_weights_ready"], 1)
            with pe.Fori(0, PAIRS // 2) as it:
                for par_i in range(2):
                    i, w = it * 2 + par_i, par_i
                    for k in range(3):
                        n, b = 3 * i + k, (w + k) % 2
                        pe.wait_ge(s["xn_ready"], n + 1)
                        pe.wait_ge(s["xnT_taken"], n + 1)
                        for f in range(2):
                            last = nc.tensor.transpose(bank[b][0:DH, 128 * f:128 * (f + 1)],
                                                       xn[:, w, k, DH * f:DH * (f + 1)], C("ident"))
                        last.then_inc(s["xnT_psum"], 1)

                    def token_product(k):
                        n, b = 3 * i + k, 4 + (w + k) % 2
                        pe.wait_ge(s["xnT_taken"], 2 + n + 1)
                        pe.wait_ge(s["tok_taken"], n + 1)
                        for f in range(2):
                            lhsT = xnT[:, w, f, k * L + NI:(k + 1) * L] if k < 2 else ximg[:, w, f, :]
                            last = nc.tensor.matmul(bank[b][:, 0:TW], lhsT, wtok[:, f, :], start=f == 0, stop=f == 1)
                        last.then_inc(s["tok_psum"], 1)

                    def qk_product(c):
                        m = 4 * i + c
                        pe.wait_ge(s["qk_taken"], m + 1)
                        for f in range(2):
                            last = nc.tensor.matmul(bank[2 + c % 2][0:DH, 0:PC], wqk[:, f, DH * c:DH * (c + 1)],
                                                    xnT[:, w, f, :], start=f == 0, stop=f == 1)
                        last.then_inc(s["qk_psum"], 1)

                    def hidden_transpose(k):
                        n = 3 * i + k
                        pe.wait_ge(s["tok_taken"], 2 + n + 1)
                        pe.wait_ge(s["sgT_taken"], n + 1)
                        nc.tensor.transpose(bank[6][:, 0:128], sg[:, (w + k) % 2, :], C("ident")).then_inc(s["sgT_psum"], 1)

                    def gate_product(k):
                        n = 3 * i + k
                        pe.wait_ge(s["sgT_taken"], 1 + n + 1)
                        pe.wait_ge(s["par_taken"], n + 1)
                        nc.tensor.matmul(bank[7][:, 0:5 * NH], sgT[:, (w + k) % 2, :], wb2[:, :], start=True,
                                         stop=True).then_inc(s["par_psum"], 1)

                    token_product(0)
                    token_product(1)
                    token_product(2)
                    qk_product(0)
                    hidden_transpose(0)
                    qk_product(1)
                    hidden_transpose(1)
                    gate_product(0)
                    qk_product(2)
                    hidden_transpose(2)
                    gate_product(1)
                    qk_product(3)
                    gate_product(2)

            pe.sem_inc(s["scores_psum"], 2)
            pe.sem_inc(s["state_psum"], 1)
            pe.sem_inc(s["text_out_done"], 2)
            pe.sem_inc(s["out_psum"], 2)
            with pe.Fori(0, PAIRS // 2) as it:
                for par_i in range(2):
                    i, w = it * 2 + par_i, par_i
                    pe.wait_ge(s["staged"], i + 1)
                    pe.wait_ge(s["kft_taken"], i + 1)
                    for f in range(2):
                        last = nc.tensor.transpose(bank[6][:, DH * f:DH * (f + 1)], kimg[:, w, f, :],
                                                   C("ident", DH)[:, 0:DH])
                    last.then_inc(s["kft_psum"], 1)

                    def scores(t):
                        f, b, tri = t // 4, t // 2 % 2, t % 2
                        if b == 0 and tri == 0:
                            pe.wait_ge(s["qbd_ready"], 2 * i + f + 1)
                            if f == 0:
                                pe.wait_ge(s["si_taken"], i + 1)
                            for b2 in range(2):
                                last = nc.tensor.matmul(bank[2][64 * b2:64 * b2 + 64, HH * NI * f:HH * NI * (f + 1)],
                                                        kimg[:, w, f, 64 * b2:64 * b2 + 64],
                                                        qbd[:, f, :, b2 * L:b2 * L + NI], start=True, stop=True)
                            if f == 1:
                                last.then_inc(s["img_scores_psum"], 1)
                        pe.wait_ge(s["scores_taken"], 8 * i + t + 1)
                        nc.tensor.matmul(bank[tri][:, 0:384], kst[:, w, f, b * L + NI:(b + 1) * L],
                                         qbd[:, f, 3 * tri:3 * tri + 3, b * L + NI:(b + 1) * L],
                                         start=True, stop=True).then_inc(s["scores_psum"], 1)

                    def text_out(t):
                        f, b, tri = t // 4, t // 2 % 2, t % 2
                        pe.wait_ge(s["scores_taken"], 2 + 8 * i + t + 1)
                        for k in range(3):
                            hd = HH * f + 3 * tri + k
                            last = nc.tensor.matmul(bank[3 + b][:, VE * hd:VE * (hd + 1)], sm[:, tri, 128 * k:128 * (k + 1)],
                                                    vst[:, w, b, hd, :],
                                                    start=t in (0, 2) and k == 0, stop=False, skip_group_check=True)
                        last.then_inc(s["text_out_done"], 1)

                    scores(0)
                    pe.wait_ge(s["kft_taken"], 1 + i + 1)
                    pe.wait_ge(s["vg_ready"], i + 1)
                    pe.wait_ge(s["sbd_taken"], i + 1)
                    for b in range(2):
                        for f in range(2):
                            last = nc.tensor.matmul(bank[7 - b][0:DH, HH * VE * f:HH * VE * (f + 1)],
                                                    kft[64 * b:64 * b + NI, DH * f:DH * (f + 1)],
                                                    vst[64 * b:64 * b + NI, w, 2, HH * f:HH * (f + 1), :].rearrange("p h e -> p (h e)"),
                                                    start=True, stop=True)
                    last.then_inc(s["state_psum"], 1)
                    scores(1)
                    pe.wait_ge(s["out_taken"], i + 1)
                    for t in range(2, 8):
                        text_out(t - 2)
                        scores(t)
                    text_out(6)
                    text_out(7)
                    pe.wait_ge(s["sbd_taken"], 1 + i + 1)
                    pe.wait_ge(s["si_taken"], 1 + i + 1)
                    for b in range(2):
                        for f in range(2):
                            nc.tensor.matmul(bank[3 + b][:, HH * VE * f:HH * VE * (f + 1)],
                                             qst[:, w, f, b * L + NI:(b + 1) * L], sbd[:, b, f, :],
                                             start=False, stop=f == 1, skip_group_check=True)
                    for b in range(2):
                        for hd in range(NH):
                            last = nc.tensor.matmul(bank[5][64 * b:64 * b + 64, VE * hd:VE * (hd + 1)],
                                                    si[64 * b:64 * b + 64, NI * hd:NI * hd + 64],
                                                    vst[64 * b:64 * b + 64, w, 2, hd, :],
                                                    start=hd == 0, stop=hd == NH - 1, skip_group_check=True)
                    last.then_inc(s["out_psum"], 1)

            pe.sem_inc(s["uhT_psum"], 6)
            pe.sem_inc(s["proj_psum"], 2)
            pe.sem_inc(s["x2T_psum"], 6)
            pe.sem_inc(s["logit_psum"], 2)
            for src, ready, psum, taken, dst, used, done, wgt, cols in (
                    (uh, "uh_ready", "uhT_psum", "uhT_taken", oT, "proj_taken", "proj_psum", wp, D),
                    (x2, "x2_ready", "x2T_psum", "x2T_taken", x2T, "logit_taken", "logit_psum", gw, NE + 1)):
                with pe.Fori(0, PAIRS // 2) as it:
                    for w in range(2):
                        i = it * 2 + w
                        pe.wait_ge(s[ready], i + 1)

                        def rows_out(k):
                            n, b = 3 * i + k, (w + k) % 2
                            pe.wait_ge(s[taken], n + 1)
                            for f in range(2):
                                last = nc.tensor.transpose(bank[b][0:DH, 128 * f:128 * (f + 1)],
                                                           src[:, w, k, DH * f:DH * (f + 1)], C("ident"))
                            last.then_inc(s[psum], 1)

                        def rows_in(k):
                            n, b = 3 * i + k, (w + k) % 2
                            pe.wait_ge(s[taken], 2 + n + 1)
                            pe.wait_ge(s[used], n + 1)
                            nc.tensor.matmul(bank[2 + b][:, 0:cols], dst[0:DH, b, 0:128], wgt[0:DH, 0, :], start=True, stop=False)
                            nc.tensor.matmul(bank[2 + b][:, 0:cols], dst[0:DH + 1, b, 128:256], wgt[0:DH + 1, 1, :], start=False,
                                             stop=True).then_inc(s[done], 1)

                        rows_out(0)
                        rows_out(1)
                        rows_in(0)
                        rows_out(2)
                        rows_in(1)
                        rows_in(2)
            pe.wait_ge(s["choices_ready"], 1)
            nc.tensor.matmul(bank[4][:, 0:2 * SLOTS * NE], beforeb[:, :], ohb[:, :, :].rearrange("p s e -> p (s e)"),
                             start=True, stop=True)
            nc.tensor.matmul(bank[5][:, 0:2 * SLOTS * NE], onesb[:, :], ohb[:, :, :].rearrange("p s e -> p (s e)"),
                             start=True, stop=True).then_inc(s["ranks_psum"], 1)

            pe.sem_inc(s["l1_psum"], 2)
            pe.sem_inc(s["hT_psum"], 2)
            pe.sem_inc(s["xgT_psum"], 1)
            pe.sem_inc(s["y_psum"], 1)

            def token_transpose(t, w, count):
                pe.wait_ge(s[f"xg_in{w}"], 16 * count)
                pe.wait_ge(s["xgT_taken"], t + 0) if isinstance(t, int) and t > 0 else None
                if not isinstance(t, int):
                    pe.wait_ge(s["xgT_taken"], t)
                for f in range(2):
                    last = nc.tensor.transpose(bank[0][0:DH, 128 * f:128 * (f + 1)], xg[:, w, 2 + DH * f:2 + DH * (f + 1)],
                                               C("ident"))
                last.then_inc(s["xgT_psum"], 1)

            def layer1(t, w):
                e = pe.value_load(eid[0:1, ds(t, 1)], min_val=0, max_val=NE - 1)
                pe.wait_ge(s["xgT_taken"], t + 1)
                pe.wait_ge(s["hid_ready"], t + 1)
                for f in range(2):
                    for q in range(2):
                        m = DH + q
                        last = nc.tensor.matmul(bank[1 + 2 * w + f][:, 0:384], xgT[0:m, w, 128 * q:128 * (q + 1)],
                                                w1[0:m, q, ds(e * FF + 384 * f, 384)], start=q == 0, stop=q == 1)
                last.then_inc(s["l1_psum"], 1)

            pe.wait_ge(s["w1_in"], 16)
            pe.wait_ge(s["w2_in"], 16)
            pe.wait_ge(s["eid_ready"], 1)
            token_transpose(0, 0, 1)
            token_transpose(1, 1, 1)
            layer1(0, 0)
            with pe.Fori(0, TILES // 4) as it:
                for j in range(4):
                    t, w = it * 4 + j, j % 2
                    layer1(t + 1, 1 - w)
                    e0 = pe.value_load(eid[0:1, ds(t, 1)], min_val=0, max_val=NE - 1)
                    pe.wait_ge(s["hid_ready"], 2 + t + 1)
                    for f in range(2):
                        pe.wait_ge(s["hT_taken"], 2 * t + f + 1)
                        for q in range(3):
                            last = nc.tensor.transpose(bank[5 + f][:, 128 * q:128 * (q + 1)],
                                                       hid[:, w, 384 * f + 128 * q:384 * f + 128 * (q + 1)], C("ident"))
                        last.then_inc(s["hT_psum"] if f else s["hT_half"], 1)
                    token_transpose(t + 2, w, 2 * it + j // 2 + 2)
                    for c in range(FC):
                        if c % 3 == 0:
                            pe.wait_ge(s["hT_taken"], 2 + 2 * t + c // 3 + 1)
                        if c == 0:
                            pe.wait_ge(s["y1_ready"], t + 1)
                        last = nc.tensor.matmul(bank[7][:, 0:D], hT[:, w, 128 * c:128 * (c + 1)], w2[:, c, ds(e0 * D, D)],
                                                start=c == 0, stop=c == FC - 1)
                    last.then_inc(s["y_psum"], 1)

        @block.vector
        def _(dve):
            ch = Chain(dve, s["dve_chain"])
            V = nc.vector
            dve.wait_ge(s["constants_in"], 16)
            dve.wait_ge(s["tokens_in"], 16)
            ch.done(V.tensor_scalar(tokneg, tok_i, 0, 64.0, ALU.is_lt, ALU.mult))
            ch.sync()
            ch.done(V.tensor_tensor(tok_f, tokneg, tok_i, ALU.add))
            ch.sync()
            V.tensor_scalar(tok_f, tok_f, 69.0, C("tok", 70), ALU.min, ALU.is_equal).then_inc(s["onehot_ready"], 1)
            dve.wait_ge(s["small_in"], 16 * SMALL)
            for f in range(2):
                V.tensor_scalar(wqk[:, f, :], wraw[:, f, 0:4 * DH], lnwb[:, f:f + 1], None, ALU.mult)
                V.tensor_scalar(wtok[:, f, 0:D], wraw[:, f, 4 * DH:4 * DH + D], lnwb[:, f:f + 1], None, ALU.mult)
                V.tensor_copy(wtok[:, f, D:TW], wraw[:, f, 4 * DH + D:])
                V.tensor_scalar(wp[0:DH, f, :], wp_raw[:, f, :], mnwb[:, 0:1], None, ALU.mult)
            V.tensor_scalar(temp[:, 1:2], temp[:, 0:1], 0.1, 2.0, ALU.max, ALU.min)
            dve.wait_ge(s["attn_bias_sums"], 1)
            V.tensor_tensor(bqk[:, :], bank[3][0:DH, 100:104], bqk0[:, :], ALU.add)
            V.tensor_tensor(bv[:, :], bank[7][:, D:2 * D], bv0[:, :], ALU.add)
            V.tensor_tensor(wp[DH:DH + 1, 1, :], bank[6][DH:DH + 1, D:2 * D], bproj[DH:DH + 1, :],
                            ALU.add).then_inc(s["attn_weights_ready"], 1)
            text = [3 * (b // 2) + b % 2 for b in range(B)]
            for b in range(B):
                dve.wait_ge(s["text_psum"], b + 1)
                V.scalar_tensor_tensor(h[:, text[b], :], bank[4 + b % 2][:, 0:D], float(D) ** 0.5, C("pe"),
                                       ALU.mult, ALU.add).then_inc(s["text_taken"], 1)
            dve.wait_ge(s["text_taken"], B)
            for b in range(B):
                ch.done(V.bn_stats(st[:, text[b], :], h[:, text[b], :]))
            ch.sync()
            for b in range(B):
                V.bn_aggr(mv[:, text[b], :], st[:, text[b], :])
            dve.wait_ge(s["beta_sums"], 1)
            NW = SHIFTS * NK
            for q in range(SHIFTS):
                ch.done(V.tensor_tensor(wpatch[:, NK * q:NK * (q + 1), :], wpatch[:, NK * q:NK * (q + 1), :],
                                        gb[:, NK * q:NK * (q + 1)].unsqueeze(2).to_broadcast([KP, NK, D]), ALU.mult))
            ch.done(V.tensor_tensor(tokb, bank[6][:, 0:D], tb, ALU.add))
            ch.sync()
            wq = [wpatch[:, NK * q:NK * (q + 1), :] for q in range(SHIFTS)]
            ch.done(V.tensor_tensor(wq[0], wq[0], wq[1], ALU.add))
            ch.done(V.tensor_tensor(wq[2], wq[2], wq[3], ALU.add))
            ch.sync()
            ch.done(V.tensor_tensor(wq[0], wq[0], wq[2], ALU.add))
            V.tensor_copy(weff[:, :, D], C("mult", KP))
            ch.sync()
            V.tensor_tensor(weff[:, :, 0:D], wq[0], wq[4], ALU.add).then_inc(s["weff_ready"], 1)
            dve.wait_ge(s["gain_sums"], 1)
            ch.done(V.tensor_copy(gsum, bank[7][:, 0:D]))
            dve.wait_ge(s["patch_sums"], PAIRS)
            for g in range(PAIRS):
                V.tensor_scalar(istat[:, 0, g:g + 1], pbank[g // 2][:, (D + 1) * (g % 2) + D:(D + 1) * (g % 2 + 1)],
                                1.0 / PDIM, None, ALU.mult)
                ch.done(V.tensor_scalar(istat[:, 1, g:g + 1], bank[3][:, g:g + 1], 1.0 / PDIM, None, ALU.mult))
            ch.sync()
            ch.done(V.tensor_tensor(istat[:, 2, :], istat[:, 0, :], istat[:, 0, :], ALU.mult))
            ch.sync()
            ch.done(V.tensor_tensor(istat[:, 3, :], istat[:, 1, :], istat[:, 2, :], ALU.subtract))
            ch.sync()
            V.tensor_scalar(istat[:, 3, :], istat[:, 3, :], 0.0, None, ALU.max).then_inc(s["ivar_ready"], 1)
            ch.done(V.tensor_scalar(istat[:, 6, :], istat[:, 0, :], -1.0, None, ALU.mult))
            dve.wait_ge(s["isd_ready"], 1)
            ch.done(V.reciprocal(istat[:, 5, :], istat[:, 4, :]))
            ch.sync()
            img = lambda g: h[:, 3 * g + 2, :]
            for g in range(PAIRS):
                ch.done(V.scalar_tensor_tensor(img(g), gsum, istat[:, 6, g:g + 1],
                                               pbank[g // 2][:, (D + 1) * (g % 2):(D + 1) * (g % 2) + D], ALU.mult, ALU.add))
            ch.sync()
            for g in range(PAIRS):
                ch.done(V.scalar_tensor_tensor(img(g), img(g), istat[:, 5, g:g + 1], tokb, ALU.mult, ALU.add))
            ch.sync()
            for g in range(PAIRS):
                ch.done(V.bn_stats(st[:, 3 * g + 2, :], img(g)))
            ch.sync()
            for g in range(PAIRS):
                last = V.bn_aggr(mv[:, 3 * g + 2, :], st[:, 3 * g + 2, :])
            last.then_inc(s["stats_ready"], 1)
            dve.wait_ge(s["sd_ready"], 1)
            ch.done(V.reciprocal(ln[:, 1, :], ln[:, 0, :]))
            ch.sync()
            ch.done(V.tensor_tensor(ln[:, 2, :], mv[:, :, 1], ln[:, 1, :], ALU.mult))
            ch.sync()
            V.tensor_tensor(ln[:, 2, :], ln[:, 2, :], ln[:, 1, :], ALU.mult).then_inc(s["varx_ready"], 1)
            dve.wait_ge(s["sd_ready"], 2)
            ch.done(V.reciprocal(ln[:, 4, :], ln[:, 3, :]))
            ch.sync()
            V.tensor_scalar(ln[:, 5, :], ln[:, 3, :], 0.5, None, ALU.mult)
            V.tensor_tensor(ln[:, 4, :], ln[:, 4, :], ln[:, 1, :], ALU.mult).then_inc(s["ln_ready"], 1)

            dve.sem_inc(s["qk_done"], 6)
            dve.sem_inc(s["tok_taken"], 2)
            dve.sem_inc(s["par_taken"], 1)
            dve.wait_ge(s["ln_ready"], 1)
            dve.wait_ge(s["attn_weights_ready"], 1)
            with dve.Fori(0, PAIRS // 2) as it:
                for par_i in range(2):
                    i, w = it * 2 + par_i, par_i
                    dve.wait_ge(s["xnT_psum"], 3 * i + 3)
                    for k in range(3):
                        n = 3 * i + k
                        V.tensor_scalar(xn[:, w, k, :], h[:, ds(n, 1), :].rearrange("p a n -> p (a n)"), mv[:, ds(n, 1), 0],
                                        ln[:, 4, ds(n, 1)], ALU.subtract, ALU.mult).then_inc(s["xn_ready"], 1)
                    for k in range(3):
                        n, b = 3 * i + k, (w + k) % 2
                        dve.wait_ge(s["tok_psum"], 6 + n + 1)
                        dve.wait_ge(s["th_ready"], 2 + n + 1)
                        V.tensor_tensor(vx[:, ds(n, 1), :, :].rearrange("p a h e -> p (a h) e"),
                                        bank[4 + b][:, 0:D].rearrange("p (h e) -> p h e", h=NH),
                                        bv[:, :].rearrange("p (h e) -> p h e", h=NH), ALU.add)
                        dve.wait_ge(s["sgT_psum"], n + 1)
                        V.scalar_tensor_tensor(sg[:, b, :], th[:, b, :], 1.0, bank[4 + b][:, D:TW], ALU.add,
                                               ALU.mult).then_inc(s["tok_taken"], 1)

                    def qk_finish(c):
                        m = 4 * i + c
                        dve.wait_ge(s["qk_taken"], 2 + m + 1)
                        V.scalar_tensor_tensor(qk[:, c, ds(i * PC, PC)], ek[:, c % 2, :], 1.0, rk[:, c % 2, :], ALU.min,
                                               ALU.add).then_inc(s["qk_done"], 1)

                    def gate_take(k):
                        n = 3 * i + k
                        dve.wait_ge(s["par_psum"], 2 + n + 1)
                        V.tensor_scalar(par[:, ds(n, 1), :].rearrange("p a n -> p (a n)"), bank[7][:, 0:5 * NH],
                                        ln[:, 5, ds(n, 1)], None, ALU.mult).then_inc(s["par_taken"], 1)

                    qk_finish(0)
                    qk_finish(1)
                    gate_take(0)
                    qk_finish(2)
                    gate_take(1)
                    qk_finish(3)
                    gate_take(2)

            dve.wait_ge(s["gate_tanh"], 1)
            ch.done(V.tensor_scalar(gt[:, 0, :], gt[:, 0, :], 1.0, None, ALU.add))
            V.tensor_tensor(gt[:, 1, :], gt[:, 1, :], gt[:, 3, :], ALU.subtract).then_inc(s["phase_ready"], 1)
            ch.sync()
            ch.done(V.scalar_tensor_tensor(gt[:, 0, :], gt[:, 2, :], 1.0, gt[:, 0, :], ALU.add, ALU.mult))
            dve.wait_ge(s["sin_ready"], 1)
            ch.done(V.tensor_tensor(gt[:, 4, :], gt[:, 3, :], gt[:, 3, :], ALU.mult))
            ch.sync()
            ch.done(V.tensor_scalar(gt[:, 4, :], gt[:, 4, :], -2.0, 1.0, ALU.mult, ALU.add))
            ch.done(V.tensor_scalar(temp[:, 1:2], temp[:, 1:2], 0.5, None, ALU.mult))
            ch.sync()
            V.tensor_tensor(gt[:, 0, :], gt[:, 0, :], gt[:, 4, :], ALU.mult).then_inc(s["inter_ready"], 1)
            dve.wait_ge(s["gate_ready"], 1)
            ch.done(V.tensor_scalar(gt[:, 4, :], gt[:, 2, :], 0.5, 1.5, ALU.mult, ALU.add))
            ch.done(V.memset(si[:, NH * NI:], 0.0))
            ch.done(V.memset(vst[:, :, :, :, HD:VE], 1.0))
            ch.sync()

            dve.sem_inc(s["si_taken"], 1)
            dve.sem_inc(s["scores_taken"], 2)
            dve.sem_inc(s["sbd_taken"], 1)
            dve.sem_inc(s["out_taken"], 1)
            ch.enter(3)
            with dve.Fori(0, PAIRS // 2) as it:
                for par_i in range(2):
                    i, w = it * 2 + par_i, par_i
                    if par_i:
                        ch.k = 0
                    ch.at(i)

                    def expand(f):
                        if f == 0:
                            dve.wait_ge(s["scores_psum"], 8 * i + 2)
                        for k in range(HH):
                            last = V.tensor_scalar(qbd[:, f, k, :], qk[:, f, ds(i * PC, PC)], C("hmask", DH)[:, k:k + 1],
                                                   None, ALU.mult)
                        last.then_inc(s["qbd_ready"], 1)

                    def mask(t):
                        f, b, tri = t // 4, t // 2 % 2, t % 2
                        dve.wait_ge(s["scores_psum"], 2 + 8 * i + t + 1)
                        dve.wait_ge(s["text_out_done"], 8 * i + t + 1)
                        V.tensor_tensor(sm[:, tri, :].rearrange("p (h n) -> p h n", h=3),
                                        bank[tri][:, 0:384].rearrange("p (h n) -> p h n", h=3),
                                        C("causal").unsqueeze(1).to_broadcast([128, 3, 128]), ALU.mult).then_inc(s["scores_taken"], 1)

                    expand(0)
                    expand(1)
                    vrow = vx[:, ds(3 * i, 3), :, :].rearrange("p s h e -> p (s h) e")
                    dve.wait_ge(s["out_psum"], i + 1)
                    V.tensor_tensor(vst[:, w, :, :, 0:HD].rearrange("p s h e -> p (s h) e"), vrow, gt[:, 4, ds(3 * NH * i, 3 * NH)].unsqueeze(2).to_broadcast([128, 3 * NH, HD]),
                                    ALU.mult).then_inc(s["vg_ready"], 1)
                    mask(0)
                    mask(1)
                    dve.wait_ge(s["state_psum"], 1 + i + 1)
                    for b in range(2):
                        last = V.tensor_tensor(sbd[:, b], bank[7 - b][0:DH, 0:2 * HH * VE].rearrange("p (c n) -> p c n", c=2),
                                               C("blk", DH).unsqueeze(1).to_broadcast([DH, 2, HH * VE]), ALU.mult)
                    last.then_inc(s["sbd_taken"], 1)
                    for t in range(2, 8):
                        mask(t)
                        if t == 4:
                            dve.wait_ge(s["img_scores_psum"], i + 1)
                            V.tensor_tensor(si[:, 0:NH * NI].rearrange("p (h n) -> p h n", h=NH),
                                            bank[2][:, 0:NH * NI].rearrange("p (h n) -> p h n", h=NH),
                                            C("icausal").unsqueeze(1).to_broadcast([128, NH, NI]), ALU.mult).then_inc(s["si_taken"], 1)
                    dve.wait_ge(s["out_psum"], 2 + i + 1)
                    o = [bank[3 + k][:, 0:NH * VE].rearrange("p (h e) -> p h e", h=NH) for k in range(3)]
                    for k in range(3):
                        last = V.tensor_scalar(rden[:, k, :], o[k][:, :, HD], 1e-6, None, ALU.add)
                    ch.done(last)
                    ch.sync()
                    ch.done(V.reciprocal(rden[:, :, :], rden[:, :, :]))
                    ch.sync()
                    uh3 = [u[:, ds(3 * i + k, 1), :].rearrange("p a (h e) -> p (a h) e", h=NH) for k in range(3)]
                    for k in range(3):
                        last = V.tensor_tensor(uh3[k], o[k][:, :, 0:HD],
                                               rden[:, k, :].unsqueeze(2).to_broadcast([128, NH, HD]), ALU.mult)
                    last.then_inc(s["out_taken"], 1)
                    dve.wait_ge(s["out_taken"], 1 + i + 1)
                    hm = lnr[:, 0, ds(3 * NH * i, 3 * NH)]
                    for k in range(3):
                        last = V.tensor_reduce(lnr[:, 0, ds(3 * NH * i + NH * k, NH)], uh3[k], AX.X, ALU.add)
                    ch.done(last)
                    ch.sync()
                    for k in range(3):
                        last = V.scalar_tensor_tensor(uh3[k], lnr[:, 0, ds(3 * NH * i + NH * k, NH)].unsqueeze(2).to_broadcast([128, NH, HD]),
                                                      -1.0 / HD, uh3[k], ALU.mult, ALU.add)
                    last.then_inc(s["uc_ready"], 1)
            ch.leave(PAIRS)

            dve.wait_ge(s["usq_ready"], PAIRS)
            V.tensor_reduce(lnr[:, 1, :], usq.rearrange("p s (h e) -> p (s h) e", h=NH), AX.X, ALU.add).then_inc(s["hvar_ready"], 1)
            dve.wait_ge(s["hvar_ready"], 1)
            ch.done(V.memset(oT[DH:DH + 1], 1.0))
            ch.done(V.memset(x2T[DH:DH + 1], 1.0))
            ch.sync()
            dve.wait_ge(s["hsd_ready"], 1)
            ch.done(V.reciprocal(lnr[:, 2, :], lnr[:, 2, :]))
            ch.sync()
            dve.sem_inc(s["proj_taken"], 2)
            dve.sem_inc(s["logit_taken"], 2)

            def head_norm(i, w):
                dve.wait_ge(s["uhT_psum"], 3 * i + 3)
                uv = u[:, ds(3 * i, 3), :]
                for k in range(3):
                    last = V.tensor_tensor(uh[:, w, k].rearrange("p (h e) -> p h e", h=NH),
                                           u[:, ds(3 * i + k, 1), :].rearrange("p a (h e) -> p (a h) e", h=NH),
                                           lnr[:, 2, ds(3 * NH * i + NH * k, NH)].unsqueeze(2).to_broadcast([128, NH, HD]), ALU.mult)
                last.then_inc(s["uh_ready"], 1)

            def residual(i):
                for k in range(3):
                    hr = h[:, ds(3 * i + k, 1), :].rearrange("p a n -> p (a n)")
                    dve.wait_ge(s["proj_psum"], 2 + 3 * i + k + 1)
                    V.tensor_tensor(hr, hr, bank[2 + (i_par(i) + k) % 2][:, 0:D], ALU.add).then_inc(s["proj_taken"], 1)
                dve.wait_ge(s["proj_taken"], 2 + 3 * i + 3)
                for k in range(3):
                    last = V.bn_stats(st[:, ds(3 * i + k, 1), :].rearrange("p a n -> p (a n)"), h[:, ds(3 * i + k, 1), :].rearrange("p a n -> p (a n)"))
                last.then_inc(s["stats2_done"], 1)

            par_now = [0]
            i_par = lambda i: par_now[0]
            head_norm(0, 0)
            with dve.Fori(0, PAIRS // 2 - 1) as it:
                for w in range(2):
                    par_now[0] = w
                    head_norm(it * 2 + w + 1, 1 - w)
                    residual(it * 2 + w)
            for i in (PAIRS - 2, PAIRS - 1):
                par_now[0] = i % 2
                if i == PAIRS - 2:
                    head_norm(i + 1, 1)
                residual(i)
            dve.wait_ge(s["stats2_done"], PAIRS)
            for n in range(SLOTS):
                last = V.bn_aggr(mv[:, n, :], st[:, n, :])
            last.then_inc(s["means2_ready"], 1)
            dve.wait_ge(s["sd2_ready"], 1)
            ch.done(V.reciprocal(ln[:, 1, :], ln[:, 0, :]))
            ch.sync()

            def token_norm(i, w):
                dve.wait_ge(s["x2T_psum"], 3 * i + 3)
                dve.wait_ge(s["x2_copied"], i + 1)
                for k in range(3):
                    last = V.tensor_scalar(x2[:, w, k], h[:, ds(3 * i + k, 1), :].rearrange("p a n -> p (a n)"), mv[:, ds(3 * i + k, 1), 0],
                                           ln[:, 1, ds(3 * i + k, 1)], ALU.subtract, ALU.mult)
                last.then_inc(s["x2_ready"], 1)

            def choose(i):
                for k in range(3):
                    dve.wait_ge(s["logit_psum"], 2 + 3 * i + k + 1)
                    V.tensor_copy(lg[:, ds(3 * i + k, 1), :].rearrange("p a n -> p (a n)"),
                                  bank[2 + (par_now[0] + k) % 2][:, 0:NE + 1]).then_inc(s["logit_taken"], 1)

            token_norm(0, 0)
            with dve.Fori(0, PAIRS // 2 - 1) as it:
                for w in range(2):
                    par_now[0] = w
                    token_norm(it * 2 + w + 1, 1 - w)
                    choose(it * 2 + w)
            for i in (PAIRS - 2, PAIRS - 1):
                par_now[0] = i % 2
                if i == PAIRS - 2:
                    token_norm(i + 1, 1)
                choose(i)
            dve.wait_ge(s["logit_taken"], 2 + SLOTS)
            for n in range(SLOTS):
                ch.done(V.max(m8[:, n, :], lg[:, n, 0:NE]))
            ch.sync()
            for n in range(SLOTS):
                ch.done(V.max_index(ix[:, n, :], m8[:, n, :], lg[:, n, 0:NE]))
            ch.sync()
            V.tensor_scalar(vtok[:, :], lg[:, :, NE], -3.0, 3.0, ALU.max, ALU.min).then_inc(s["v_ready"], 1)
            V.tensor_tensor(wk[:, 0, :], m8[:, :, 1], m8[:, :, 0], ALU.subtract).then_inc(s["gap_ready"], 1)
            for k in range(2):
                ch.done(V.tensor_copy(ixf[:, k, :], ix[:, :, k]))
            V.tensor_copy(beforeb[:, :], C("before"))
            ch.done(V.memset(onesb[:, :], 1.0))
            ch.sync()
            ch.done(V.tensor_tensor(ohf[:, :, :], ixf[:, :, :].rearrange("p k s -> p (k s)").unsqueeze(2).to_broadcast([128, 2 * SLOTS, NE]),
                                    C("iota8").unsqueeze(1).to_broadcast([128, 2 * SLOTS, NE]), ALU.is_equal))
            ch.sync()
            for k in range(2):
                last = V.tensor_tensor(ohb[:, k * SLOTS:(k + 1) * SLOTS, :], ohf[:, k * SLOTS:(k + 1) * SLOTS, :],
                                       C("valid").unsqueeze(2).to_broadcast([128, SLOTS, NE]), ALU.mult)
            last.then_inc(s["choices_ready"], 1)
            dve.wait_ge(s["ratio_ready"], 1)
            ch.done(V.tensor_scalar(wk[:, 0, :], wk[:, 1, :], 1.0, None, ALU.add))
            ch.sync()
            ch.done(V.reciprocal(wk[:, 0, :], wk[:, 0, :]))
            ch.sync()
            dve.wait_ge(s["x2_copied"], 2 + PAIRS)
            V.tensor_copy(rows[:, 0, :, 0], wk[:, 0, :])
            V.tensor_tensor(rows[:, 1, :, 0], wk[:, 0, :], wk[:, 1, :], ALU.mult)
            V.tensor_copy(rows[:, :, :, 1], C("place").rearrange("p (k s) -> p k s", k=2))
            dve.wait_ge(s["ranks_psum"], 1)
            ch.done(V.tensor_copy(tot[:, :, :], bank[5][:, 0:2 * SLOTS * NE].rearrange("p (s e) -> p e s", e=NE)))
            ch.sync()
            for e in range(NE):
                ch.done(V.tensor_tensor_scan(inc[:, e, :], ones[:, 0:2 * SLOTS], tot[:, e, :], 0.0, ALU.mult, ALU.add))
            ch.sync()
            ch.done(V.tensor_tensor(ohf[:, :, :].rearrange("p s e -> p (s e)").rearrange("p (e s) -> p e s", e=NE),
                                    inc[:, :, 2 * SLOTS - 1:2 * SLOTS].to_broadcast([128, NE, 2 * SLOTS]),
                                    C("steps").unsqueeze(1).to_broadcast([128, NE, 2 * SLOTS]), ALU.is_gt))
            ch.sync()
            ch.done(V.tensor_reduce(cnt[:, 0, :], ohf[:, :, :].rearrange("p s e -> p (s e)").rearrange("p (e s) -> p e s", e=NE), AX.X, ALU.add))
            ch.sync()
            ch.done(V.tensor_tensor_scan(cnt[:, 1, :], ones[:, 0:NE], cnt[:, 0, :], 0.0, ALU.mult, ALU.add))
            ch.sync()
            ch.done(V.tensor_tensor(cnt[:, 2, :], cnt[:, 1, :], cnt[:, 0, :], ALU.subtract))
            ch.done(V.tensor_tensor(inc[:, :, :], inc[:, :, :], tot[:, :, :], ALU.subtract))
            ch.done(V.tensor_tensor(ecmp[:, :, :], cnt[0:1, 1, :].unsqueeze(1).to_broadcast([1, TILES + 2, NE]),
                                    C("tile8", 1).rearrange("p (t e) -> p t e", e=NE), ALU.is_le))
            ch.sync()
            ch.done(V.tensor_scalar(cnt[:, 3, :], cnt[:, 2, :], 128.0, None, ALU.mult))
            ch.done(V.tensor_reduce(eidf[:, :], ecmp[:, :, :], AX.X, ALU.add))
            ch.sync()
            V.tensor_scalar(eid[:, :], eidf[:, :], NE - 1.0, None, ALU.min).then_inc(s["eid_ready"], 1)
            ch.done(V.tensor_tensor(inc[:, :, :], inc[:, :, :], cnt[:, 3, :].unsqueeze(2).to_broadcast([128, NE, 2 * SLOTS]), ALU.add))
            ch.sync()
            ch.done(V.tensor_tensor(ohf[:, :, :], bank[4][:, 0:2 * SLOTS * NE].rearrange("p (s e) -> p s e", e=NE),
                                    inc[:, :, :].rearrange("p e s -> p s e"), ALU.add))
            ch.sync()
            ch.done(V.tensor_tensor(ohf[:, :, :], ohf[:, :, :], ohb[:, :, :], ALU.mult))
            ch.sync()
            ch.done(V.tensor_reduce(pos[:, :], ohf[:, :, :], AX.X, ALU.add))
            ch.sync()
            V.tensor_tensor(sidx[:, :], pos[:, :], C("trash"), ALU.add).then_inc(s["places_ready"], 1)
            ch.done(V.memset(ga[:, :, 0], 0.0))
            ch.done(V.memset(ga[:, :, 1], -1.0))
            ch.done(V.memset(gtok[:, :, :], 0.0))
            ch.done(V.memset(xgT[DH:DH + 1], 1.0))
            for k in range(3):
                ch.done(V.tensor_tensor(spec[:, k, :], spec[:, k, :], spec[:, 3, :], ALU.mult))
            ch.sync()
            dve.wait_ge(s["v_in"], 32)
            ch.done(V.scalar_tensor_tensor(ga[:, 0:L, 0], vv[:, :], -2.0, C("sign", 32)[:, 0:L], ALU.add, ALU.mult))
            ch.sync()
            ch.done(V.tensor_copy(gs[:, 0, :], ga[:, 0, :]))
            ch.sync()

            dve.sem_inc(s["hT_taken"], 2)
            dve.sem_inc(s["y1_ready"], 1)

            def take_tokens(t, w, j):
                dve.wait_ge(s["xgT_psum"], 1 + t + 1)
                V.tensor_copy(meta_w[:, j:j + 1], xg[:, w, 0:1])
                V.tensor_copy(meta_i[:, j:j + 1], xg[:, w, 1:2])
                V.tensor_copy(xgT[0:DH, w, :], bank[0][0:DH, 0:256]).then_inc(s["xgT_taken"], 1)

            dve.wait_ge(s["eid_ready"], 1)
            dve.wait_ge(s["b2_in"], 16)
            take_tokens(0, 0, 0)
            take_tokens(1, 1, 1)
            ch.enter(3 * GSTEP)
            with dve.Fori(0, TILES // 4) as it:
                for j in range(4):
                    t, w = it * 4 + j, j % 2
                    ch.k = 0
                    ch.at(t)
                    e = dve.value_load(eid[0:1, ds(t, 1)], min_val=0, max_val=NE - 1)
                    for f in range(2):
                        if f:
                            dve.wait_ge(s["hT_psum"], 2 + t + 1)
                        else:
                            dve.wait_ge(s["hT_half"], t + 1)
                            dve.wait_ge(s["y_psum"], t + 1)
                        V.tensor_copy(hT[:, w, 384 * f:384 * (f + 1)], bank[5 + f][:, 0:384]).then_inc(s["hT_taken"], 1)
                    dve.wait_ge(s["turn_taken"], t + 1)
                    take_tokens(t + 2, w, (j + 2) % 4)
                    for g in range(GSTEP):
                        now = gs[:, ds(t * GSTEP + g, 1), :].rearrange("p a c -> p (a c)")
                        nxt = gs[:, ds(t * GSTEP + g + 1, 1), :].rearrange("p a c -> p (a c)")
                        ch.done(V.scalar_tensor_tensor(gq[:, 2:4], now, 1.0, now, ALU.mult, ALU.mult, accum_out=gq[:, 0:1]))
                        ch.sync()
                        ch.done(V.reciprocal(gq[:, 1:2], gq[:, 0:1]))
                        ch.sync()
                        ch.done(V.scalar_tensor_tensor(nxt, now, gq[:, 1:2], ga[:, ds(t * GSTEP + g + 1, 1), :].rearrange("p a c -> p (a c)"),
                                                       ALU.mult, ALU.add))
                        ch.sync()
                    dve.wait_ge(s["y_psum"], 1 + t + 1)
                    dve.wait_ge(s["y2_ready"], t + 1)
                    V.tensor_tensor(y1[:, w, :], bank[7][:, 0:D], b2b[:, ds(e * D, D)], ALU.add).then_inc(s["y1_ready"], 1)
            ch.leave(TILES)

            V.tensor_tensor(gg[:, 0, :], gs[0:B, 0:L, 0], C("sign", B)[:, 0:L], ALU.mult).then_inc(s["recurrence_done"], 1)
            dve.wait_ge(s["recurrence_done"], 1)
            dve.wait_ge(s["ge_in"], 16)
            ch.done(V.tensor_tensor(gg[:, 1, :], ge[:, :, 0], C("sign", B)[:, 0:L], ALU.mult))
            ch.sync()
            ch.done(V.tensor_tensor(gg[:, 0, :], gg[:, 0, :], gg[:, 1, ::-1], ALU.add))
            ch.done(V.tensor_tensor(gg[:, 2, :], gs[0:B, 0:L, 1], ge[:, ::-1, 1], ALU.add))
            ch.sync()
            ch.done(V.scalar_tensor_tensor(gg[:, 0, :], vv[0:B, :], -2.0, gg[:, 0, :], ALU.add, ALU.subtract))
            ch.done(V.tensor_scalar(gg[:, 2, :], gg[:, 2, :], 1.0, None, ALU.add))
            ch.sync()
            ch.done(V.tensor_tensor(gg[:, 1, :], gg[:, 0, :], gg[:, 0, :], ALU.mult))
            ch.done(V.tensor_tensor(gg[:, 3, :], gg[:, 2, :], gg[:, 2, :], ALU.mult))
            ch.sync()
            ch.done(V.tensor_tensor(gg[:, 1, :], gg[:, 1, :], gg[:, 3, :], ALU.add))
            ch.sync()
            ch.done(V.reciprocal(gg[:, 1, :], gg[:, 1, :]))
            ch.sync()
            for k in range(2):
                ch.done(V.scalar_tensor_tensor(gg[:, 2 * k, :], gg[:, 2 * k, :], -1.0, gg[:, 1, :], ALU.mult, ALU.mult))
            ch.sync()
            for k in range(2):
                last = V.tensor_scalar(g2[:, :, k], gg[:, 2 * k, :], -10.0, 10.0, ALU.max, ALU.min)
            last.then_inc(s["green_ready"], 1)
            dve.wait_ge(s["gtok_in"], 64)
            for n in range(SLOTS):
                ch.done(V.scalar_tensor_tensor(h[:, n, :], spec[:, 0, :], gtok[:, n, 0:1], h[:, n, :], ALU.mult, ALU.add))
            ch.sync()
            for n in range(SLOTS):
                ch.done(V.scalar_tensor_tensor(h[:, n, :], spec[:, 1, :], gtok[:, n, 1:2], h[:, n, :], ALU.mult, ALU.add))
            ch.sync()
            ch.done(V.tensor_tensor(h[:, :, :], h[:, :, :], spec[:, 2, :].unsqueeze(1).to_broadcast([128, SLOTS, D]), ALU.add))
            ch.sync()
            dve.wait_ge(s["planes_in"], 16 * 8)
            hv = h[:, :, :].rearrange("p (i j) n -> p j i n", j=3)
            pin = plane_in.rearrange("p k (i j) n -> p k j i n", j=3)
            parts = [(0, 128, 0), (0, 128, 1), (0, NI, 2), (64, 64 + NI, 2)]
            for k in range(2):
                for lo, hi, j in parts:
                    last = V.tensor_tensor(hv[lo:hi, j], hv[lo:hi, j], pin[lo:hi, k, j], ALU.add)
                    if k == 0:
                        ch.done(last)
                ch.sync()
            last.then_inc(s["total_ready"], 1)


def laid_out(inp):
    import numpy as np

    f = {k: np.asarray(v) for k, v in inp.items()}
    arr = {}
    x = f["x"]
    pad = np.pad(x, ((0, 0), (0, 0), (1, 1), (1, 1)))
    win = np.stack([pad[:, :, PATCH * p:PATCH * p + WIN, :] for p in range(SIDE)], 2)
    win = np.stack([win[..., PATCH * p:PATCH * p + WIN] for p in range(SIDE)], 3)
    win = win.reshape(B, CH, SIDE, SIDE, WIN, NK, 2).transpose(6, 1, 4, 5, 0, 2, 3).reshape(KP, NK, B, NI)
    arr["xwin"] = np.pad(win, ((0, 0), (0, 0), (0, 0), (0, 64 - NI))).reshape(KP, NK, PT)

    def windowed(t):
        n = t.shape[1]
        t = t.reshape(PATCH, PATCH, SHIFTS, CH, n)
        o = np.zeros((2, CH, WIN, SHIFTS, NK, n), t.dtype)
        for sft, (dr, dc) in enumerate(((1, 1), (1, 0), (1, 2), (0, 1), (2, 1))):
            for par in range(2):
                js = [j for j in range(PATCH) if (j + dc) % 2 == par]
                ks = [(j + dc) // 2 for j in js]
                o[par, :, dr:dr + PATCH, sft, ks[0]:ks[-1] + 1] = t[:, js, sft].transpose(2, 0, 1, 3)
        return o.reshape(KP, SHIFTS * NK, n)

    arr["wpatch"] = windowed(f["L0_tok_W"])
    arr["patch_gb"] = np.concatenate([windowed(f[k][:, None])[..., 0] for k in ("L0_tok_gamma", "L0_tok_beta")], 1)
    arr["tokens"] = f["x_txt"].reshape(B * NT)
    cw, sw, qw = f["L0_txt_color_W"], f["L0_txt_shape_W"], f["L0_txt_quantity_W"]
    t = np.arange(64)
    arr["table"] = np.concatenate([np.concatenate([cw[t // 16], sw[t % 16 // 4], qw[t % 4]], 1), f["L0_txt_special_W"]], 0)
    rep = lambda v: np.ascontiguousarray(np.broadcast_to(v, (128,) + v.shape))
    halved = lambda w: w.reshape(2, DH, -1).transpose(1, 0, 2)
    arr["tok_b"] = rep(f["L0_tok_b"])
    arr["wattn"] = np.concatenate([halved(f["L0_attn_Wqkv"]), halved(f["L0_attn_Wb1"])], 2)
    arr["lnwb"] = np.concatenate([f["L0_attn_ln_w"].reshape(2, DH).T, f["L0_attn_ln_b"].reshape(2, DH).T], 1)
    arr["bqk"] = f["L0_attn_bqkv"][0:4 * DH].reshape(4, DH).T
    arr["bv"] = rep(f["L0_attn_bqkv"][4 * DH:])
    arr["wb2"] = f["L0_attn_Wb2"]
    arr["temp"] = rep(f["L0_attn_temperature"])
    arr["wproj"] = halved(f["L0_attn_Wproj"])
    arr["mnwb"] = np.stack([np.tile(f["L0_attn_mn_w"], HH), np.tile(f["L0_attn_mn_b"], HH)], 1)
    arr["bproj"] = rep(f["L0_attn_bproj"])

    arr["gate_w"] = np.zeros((DH + 1, 2, NE + 1), np.float32)
    arr["gate_w"][0:DH] = halved(np.concatenate([f["L0_ffn_gate_w"], f["L0_ffn_v_w"][:, None]], 1))
    arr["gate_w"][DH, 1, 0:NE] = f["L0_ffn_gate_b"]
    arr["gate_w"][DH, 1, NE] = f["L0_ffn_v_b"]
    arr["w1"] = np.zeros((DH + 1, 2, NE * FF), np.float32)
    arr["w1"][0:DH] = f["L0_ffn_w1"].reshape(NE, 2, DH, FF).transpose(2, 1, 0, 3).reshape(DH, 2, NE * FF)
    arr["w1"][DH, 1] = f["L0_ffn_b1"].reshape(NE * FF)
    arr["w2"] = f["L0_ffn_w2"].reshape(NE, FC, 128, D).transpose(2, 1, 0, 3).reshape(128, FC, NE * D)
    arr["b2"] = rep(f["L0_ffn_b2"].reshape(NE * D))
    arr["spec"] = rep(np.stack([f["L0_ffn_out_w"][0], f["L0_ffn_out_w"][1], f["L0_ffn_out_b"], f["L0_ffn_bk_scale"]], 0))

    c = {}
    p = np.arange(128)
    pos = np.arange(NT, dtype=np.float32)[:, None]
    inv = np.exp(-(np.arange(0, D, 2, dtype=np.float32) / np.float32(D)) * np.float32(np.log(10000.0))).astype(np.float32)
    ang = pos * inv
    c["pe"] = np.stack([np.sin(ang), np.cos(ang)], -1).reshape(NT, D)
    c["ident"] = np.eye(128)
    c["causal"] = p[:, None] <= p[None, :]
    c["icausal"] = (p[:, None] % 64) <= np.arange(NI)[None, :]
    c["before"] = p[:, None] < p[None, :]
    c["blk"] = (p[:, None] // HD) == (np.arange(HH * VE)[None, :] // VE)
    c["hmask"] = (p[:, None] // HD) == np.arange(HH)[None, :]
    ones = np.ones((PDIM, 1), np.float32)
    mult = windowed(ones)[..., 0].reshape(KP, SHIFTS, NK).sum(1)
    c["mult"] = np.concatenate([mult, np.zeros((128 - KP, NK))], 0)
    c["iota8"] = np.tile(np.arange(NE), (128, 1))
    valid = np.array([[k % 3 < 2 or q % 64 < NI for k in range(SLOTS)] for q in range(128)])
    c["valid"] = valid
    image = np.array([k // 3 for k in range(SLOTS)])
    c["trash"] = np.concatenate([np.where(valid, 0, SROWS + (k * PAIRS + image[None, :]) * 128 + p[:, None]) for k in range(2)], 1)
    seq = np.array([[2 * (k // 3) + (k % 3 if k % 3 < 2 else q // 64) for k in range(SLOTS)] for q in range(128)])
    tok = np.array([[NI + q if k % 3 < 2 else q % 64 for k in range(SLOTS)] for q in range(128)])
    c["place"] = np.concatenate([np.where(valid, k * PLANE + seq * L + tok, 0) for k in range(2)], 1)
    c["tile8"] = np.tile(np.repeat(np.arange(TILES + 2), NE), (128, 1))
    c["tok"] = p[:, None]
    c["steps"] = np.tile(128 * np.arange(2 * SLOTS), (128, 1))
    c["fill"] = np.concatenate([np.zeros((128, 1)), 2 * PLANE + p[:, None], np.zeros((128, D))], 1)
    c["sign"] = np.tile(1 - 2 * (np.arange(GLEN) % 2), (128, 1))
    packed = np.zeros((128, NCONST), np.float32)
    for k, (lo, hi) in CW.items():
        packed[:, lo:hi] = c[k]
    arr["consts"] = packed
    return {k: np.ascontiguousarray(v) for k, v in arr.items()}


def kernel(**inputs):
    import numpy as _np
    import concourse.bacc as _bacc
    from concourse import mybir as _mybir
    from concourse.bass_utils import run_bass_kernel_spmd as _run

    nc = _bacc.Bacc("TRN2", target_bir_lowering=False, num_devices=1)
    arrays = {f"in_{k}_dram": v for k, v in laid_out(inputs).items()}
    args = {k[3:-5]: nc.dram_tensor(k, v.shape, _mybir.dt.from_np(v.dtype), kind="ExternalInput").ap()
            for k, v in arrays.items()}
    out = nc.dram_tensor("out_0_dram", (B, L, D), _mybir.dt.float32, kind="ExternalOutput").ap()
    early_fusion_block(nc, args, out)
    r = _run(nc, [arrays], core_ids=[0])
    return r.results[0]["out_0_dram"]
```

```python
import concourse.bass as bass
from concourse import mybir
from contextlib import ExitStack

B, CH, IMG, PATCH = 16, 3, 96, 16
SIDE = IMG // PATCH
NI = SIDE * SIDE
NT = 128
L = NI + NT
D = 192
DH = D // 2
NH, HD = 12, 16
HH = NH // 2
VE = HD + 1
RANK = 128
TW = D + RANK
NE, FF = 8, 768
FC = FF // 128
SHIFTS = 5
PDIM = PATCH * PATCH * CH * SHIFTS
WIN = PATCH + 2
KP = 2 * CH * WIN
NK = WIN // 2
PAIRS = B // 2
SLOTS = 3 * PAIRS
PC = 2 * L
PT = 128 * PAIRS
TILES = NE + (2 * B * L - NE) // 128
SROWS = TILES * 128
ROW = D + 2
PLANE = B * L
GFIRST = 52
GSTEP = 4
GTILES = -(-(L - GFIRST) // (4 * GSTEP)) * 4
GLEN = GFIRST + GTILES * GSTEP + 1
EPS = 1e-5

CW, NCONST = {}, 0
for _name, _n in (("pe", D), ("ident", 128), ("causal", 128), ("icausal", NI), ("before", 128), ("blk", HH * VE),
                  ("hmask", HH), ("mult", NK), ("iota8", NE), ("valid", SLOTS), ("trash", 2 * SLOTS),
                  ("place", 2 * SLOTS), ("tile8", (TILES + 2) * NE), ("tok", 1), ("steps", 2 * SLOTS), ("fill", ROW), ("sign", GLEN)):
    CW[_name] = (NCONST, NCONST + _n)
    NCONST += _n


class Chain:

    def __init__(self, eng, sem):
        self.eng, self.sem, self.base, self.k, self.i, self.per = eng, sem, 0, 0, None, 0

    def done(self, ins):
        ins.then_inc(self.sem, 1)
        self.k += 1

    def enter(self, per):
        self.base, self.k, self.i, self.per = self.base + self.k, 0, 0, per

    def leave(self, trips):
        assert self.k == self.per, (self.k, self.per)
        self.base, self.k, self.i = self.base + self.per * trips, 0, None

    def at(self, i):
        self.i = i

    def sync(self):
        value = self.base + self.k
        self.eng.wait_ge(self.sem, value if self.i is None else self.i * self.per + value)


def early_fusion_block(nc, a, out):
    F, BF = mybir.dt.float32, mybir.dt.bfloat16
    I32, U32 = mybir.dt.int32, mybir.dt.uint32
    ALU, ACT, AX = mybir.AluOpType, mybir.ActivationFunctionType, mybir.AxisListType
    ds = bass.ds

    sorted_rows = nc.dram_tensor("sorted_rows", (SROWS + 2 * PAIRS * 128, ROW), F, kind="Internal").ap()
    planes = nc.dram_tensor("planes", (2 * PLANE + 128, D), F, kind="Internal").ap()
    v_dram = nc.dram_tensor("v_dram", (B, L), F, kind="Internal").ap()
    g_dram = nc.dram_tensor("g_dram", (B, L, 2), F, kind="Internal").ap()

    ctx = ExitStack()
    with ctx:
        def sb(name, shape, dt=F):
            return ctx.enter_context(nc.sbuf_tensor(name, shape, dt))

        cst = sb("cst", [128, NCONST])

        def C(name, p=128):
            return cst[0:p, CW[name][0]:CW[name][1]]

        arena1 = sb("arena1", [128, NE * 2 * FF])
        xwin = arena1[0:KP, 0:NK * PT].rearrange("p (k n) -> p k n", k=NK)
        w1 = arena1[0:DH + 1, :].rearrange("p (h n) -> p h n", h=2)
        plane_in = arena1[:, 0:2 * SLOTS * D].rearrange("p (k s n) -> p k s n", k=2, n=D)
        arena2 = sb("arena2", [128, 4 * B * L])
        wpatch = arena2[0:KP, 0:SHIFTS * NK * D].rearrange("p (k n) -> p k n", n=D)
        qk = arena2[0:DH, :].rearrange("p (c n) -> p c n", c=4)
        w2 = arena2[:, 0:NE * FC * D].rearrange("p (f n) -> p f n", f=FC)
        rows = sb("rows", [128, 2, SLOTS, ROW])
        u = rows[:, 0, :, 2:ROW]
        p0 = rows[:, :, :, :].rearrange("p k s n -> p (k s n)")
        XS = NK * 128
        xsq = p0[0:KP, 0:2 * XS].rearrange("p (u k n) -> p u k n", u=2, k=NK)
        xss = p0[0:KP, 2 * XS + 2 * B * NT:2 * XS + 2 * B * NT + PT]
        tok_f = p0[0:70, 2 * XS:2 * XS + B * NT]
        tokneg = p0[0:70, 2 * XS + B * NT:2 * XS + 2 * B * NT]

        h = sb("h", [128, SLOTS, D])
        vx = sb("vx", [128, SLOTS, NH, HD])
        vflat = vx[:, :, :, :].rearrange("p s h e -> p (s h e)")
        usq = vx[:, :, :, :].rearrange("p s h e -> p s (h e)")
        tok_i = vflat[0:70, 0:B * NT].bitcast(I32)

        used = {}

        def carve(phase, p, n, start=0):
            at = used.get(phase, start)
            used[phase] = at + n
            assert at + n <= NE * 2 * FF, (phase, at + n)
            return arena1[0:p, at:at + n]

        weff = carve("patch", KP, NK * (D + 1), NK * PT).rearrange("p (k n) -> p k n", k=NK)
        gb = carve("patch", KP, 2 * SHIFTS * NK)
        gsum = carve("patch", 128, D)
        tokb = carve("patch", 128, D)
        tb = carve("patch", 128, D)
        table = carve("patch", 70, D)
        istat = carve("patch", 128, 8 * PAIRS).rearrange("p (k g) -> p k g", k=8)

        xn = carve("attn", 128, 6 * D).rearrange("p (u s n) -> p u s n", u=2, s=3)
        xnT = carve("attn", DH, 4 * PC).rearrange("p (u h n) -> p u h n", u=2, h=2)
        ek = carve("attn", DH, 2 * PC).rearrange("p (u n) -> p u n", u=2)
        rk = carve("attn", DH, 2 * PC).rearrange("p (u n) -> p u n", u=2)
        th = carve("attn", 128, 2 * RANK).rearrange("p (u n) -> p u n", u=2)
        sg = carve("attn", 128, 2 * RANK).rearrange("p (u n) -> p u n", u=2)
        sgT = carve("attn", 128, 256).rearrange("p (u n) -> p u n", u=2)
        ximg = carve("attn", DH, 4 * 128).rearrange("p (u h n) -> p u h n", u=2, h=2)
        kimg = carve("attn", DH, 4 * 128).rearrange("p (u h n) -> p u h n", u=2, h=2)
        kst = carve("attn", DH, 4 * PC).rearrange("p (u h n) -> p u h n", u=2, h=2)
        qst = carve("attn", DH, 4 * PC).rearrange("p (u h n) -> p u h n", u=2, h=2)
        qbd = carve("attn", DH, 2 * HH * PC).rearrange("p (u h n) -> p u h n", u=2, h=HH)
        used["attn2"] = 0
        sm = carve("attn2", 128, 2 * 384).rearrange("p (u n) -> p u n", u=2)
        si = carve("attn2", 128, NH * NI + 64)
        kft = carve("attn2", 128, D)
        sbd = carve("attn2", DH, 4 * HH * VE).rearrange("p (b h n) -> p b h n", b=2, h=2)
        vst = carve("attn2", 128, 6 * NH * VE).rearrange("p (u s h e) -> p u s h e", u=2, s=3, h=NH)
        assert used["attn2"] <= 6 * D + 8 * PC + 6 * RANK

        ones = sb("ones", [128, 128])
        eps_t = sb("eps_t", [128, 1])
        st = sb("st", [128, SLOTS, 6])
        mv = sb("mv", [128, SLOTS, 2])
        ln = sb("ln", [128, 6, SLOTS])
        place_a = sb("place_a", [128, SLOTS * NH * 10])
        place_b = sb("place_b", [128, 2 * (4 * DH + TW)])
        place_c = sb("place_c", [128, 2 * (4 * DH + TW)])

        def within(place, start, p, n):
            assert start + n <= place.shape[1]
            return place[0:p, start:start + n]

        wraw = within(place_b, 0, DH, 2 * (4 * DH + TW)).rearrange("p (h n) -> p h n", h=2)
        wqk = within(place_c, 0, DH, 8 * DH).rearrange("p (h n) -> p h n", h=2)
        wtok = within(place_c, 8 * DH, DH, 2 * TW).rearrange("p (h n) -> p h n", h=2)
        lnwb = sb("lnwb", [DH, 4])
        bqk0 = sb("bqk0", [DH, 4])
        bqk = sb("bqk", [DH, 4])
        bv0 = sb("bv0", [128, D])
        bv = sb("bv", [128, D])
        wb2 = sb("wb2", [RANK, 5 * NH])
        temp = sb("temp", [128, 2])
        wp_raw = sb("wp_raw", [DH, 2, D])
        wp = sb("wp", [DH + 1, 2, D])
        mnwb = sb("mnwb", [DH, 2])
        bproj = sb("bproj", [128, D])
        gw = sb("gw", [DH + 1, 2, NE + 1])
        par = within(place_a, 0, 128, SLOTS * NH * 5).rearrange("p (s n) -> p s n", s=SLOTS)
        gt = within(place_a, SLOTS * NH * 5, 128, SLOTS * NH * 5).rearrange("p (k n) -> p k n", k=5)
        rden = sb("rden", [128, 3, NH])
        lnr = sb("lnr", [128, 3, SLOTS * NH])
        vat = [0]

        def carve_v(p, n):
            vat[0] += n
            assert vat[0] <= SLOTS * D
            return vflat[0:p, vat[0] - n:vat[0]]

        uh = carve_v(128, 6 * D).rearrange("p (u s n) -> p u s n", u=2, s=3)
        x2 = carve_v(128, 6 * D).rearrange("p (u s n) -> p u s n", u=2, s=3)
        oT = carve_v(DH + 1, 512).rearrange("p (u n) -> p u n", u=2)
        x2T = carve_v(DH + 1, 512).rearrange("p (u n) -> p u n", u=2)
        vat[0] = 0
        hid = carve_v(128, 2 * FF).rearrange("p (u n) -> p u n", u=2)
        hT = carve_v(128, 2 * FF).rearrange("p (u n) -> p u n", u=2)
        xgT = carve_v(DH + 1, 512).rearrange("p (u n) -> p u n", u=2)
        b2b = within(place_a, 0, 128, NE * D)
        xg = within(place_a, NE * D, 128, 2 * ROW).rearrange("p (u n) -> p u n", u=2)
        y1 = within(place_a, NE * D + 2 * ROW, 128, 2 * D).rearrange("p (u n) -> p u n", u=2)
        y2 = within(place_a, NE * D + 2 * ROW + 2 * D, 128, 2 * D).rearrange("p (u n) -> p u n", u=2)
        meta_w = sb("meta_w", [128, 4])
        meta_i = sb("meta_i", [128, 4], I32)
        spec = sb("spec", [128, 4, D])
        tail2 = NE * FC * D
        lg = within(arena2, tail2, 128, SLOTS * (NE + 1)).rearrange("p (s n) -> p s n", s=SLOTS)
        m8 = within(arena2, tail2 + SLOTS * 9, 128, SLOTS * 8).rearrange("p (s n) -> p s n", s=SLOTS)
        ix = within(arena2, tail2 + SLOTS * 17, 128, SLOTS * 8).bitcast(U32).rearrange("p (s n) -> p s n", s=SLOTS)
        ixf = sb("ixf", [128, 2, SLOTS])
        wk = sb("wk", [128, 2, SLOTS])
        beforeb = sb("beforeb", [128, 128], BF)
        onesb = sb("onesb", [128, 128], BF)
        ohf = within(place_b, 0, 128, 2 * SLOTS * NE).rearrange("p (s e) -> p s e", e=NE)
        ohb = sb("ohb", [128, 2 * SLOTS, NE], BF)
        tot = within(place_b, 2 * SLOTS * NE, 128, 2 * SLOTS * NE).rearrange("p (e s) -> p e s", e=NE)
        inc = within(place_b, 4 * SLOTS * NE, 128, 2 * SLOTS * NE).rearrange("p (e s) -> p e s", e=NE)
        cnt = sb("cnt", [128, 4, NE])
        pos = sb("pos", [128, 2 * SLOTS])
        sidx = sb("sidx", [128, 2 * SLOTS], I32)
        ecmp = within(place_c, 0, 1, (TILES + 2) * NE).rearrange("p (t e) -> p t e", e=NE)
        eidf = sb("eidf", [1, TILES + 2])
        eid = sb("eid", [1, TILES + 2], I32)
        vtok = sb("vtok", [128, SLOTS])
        ga = within(place_c, 0, 32, 2 * GLEN).rearrange("p (t c) -> p t c", c=2)
        gs = within(place_c, 2 * GLEN, 32, 2 * GLEN).rearrange("p (t c) -> p t c", c=2)
        ge = within(place_c, 4 * GLEN, B, 2 * L).rearrange("p (t c) -> p t c", c=2)
        vv = within(place_c, 4 * GLEN + 2 * L, 32, L)
        gq = sb("gq", [32, 4])
        gg = within(place_b, 0, B, 4 * L).rearrange("p (k n) -> p k n", k=4)
        g2 = within(place_b, 4 * L, B, 2 * L).rearrange("p (n k) -> p n k", k=2)
        pool_turn = sb("pool_turn", [1, TILES])
        gtok = sb("gtok", [128, SLOTS, 2])

        bank = [ctx.enter_context(nc.psum_tensor(f"bank{n}", [128, 512], F)) for n in range(8)]
        pbank = [bank[0], bank[1], bank[2], bank[5]]

        class Sems(dict):
            def __missing__(self, name):
                self[name] = ctx.enter_context(nc.semaphore(name))
                return self[name]

        s = Sems()
        for n in ("constants_in", "dve_chain", "act_chain", "pool_chain"):
            s[n]
        ctx.enter_context(nc.allow_non_contiguous_dma(reason="one value of every token"))
        block = ctx.enter_context(nc.Block())
        TXT = [(0, NI), (1, L + NI)]

        def slot_cols(t, k):
            if k < 2:
                return t[:, k * L + NI:(k + 1) * L]
            return t.rearrange("p (b n) -> p b n", b=2)[:, :, 0:64]

        SMALL = 14
        GROUPS = ((0, PAIRS - 2), (PAIRS - 2, PAIRS))

        @block.sync
        def _(sp):
            sp.dma_start(cst[:, :], a["consts"]).then_inc(s["constants_in"], 16)
            sp.dma_start(tok_i, a["tokens"].partition_broadcast(70)).then_inc(s["tokens_in"], 16)
            sp.wait_ge(s["small_in"], 16 * SMALL)
            for q in range(SHIFTS):
                sp.dma_start(wpatch[:, NK * q:NK * (q + 1), :],
                             a["wpatch"][:, NK * q:NK * (q + 1), :]).then_inc(s[f"patch_weights_in{q}"], 16)
            sp.dma_start(xwin, a["xwin"]).then_inc(s["windows_in"], 16)
            sp.wait_ge(s["constants_in"], 16)
            sp.wait_ge(s["windows_in"], 16)
            sp.dma_start(sorted_rows[0:SROWS + 256].rearrange("(t p) n -> p t n", p=128),
                         C("fill").unsqueeze(1).to_broadcast([128, TILES + 2, ROW])).then_inc(s["list_filled"], 16)
            sp.wait_ge(s["out_taken"], 1 + PAIRS)
            sp.dma_start(w1, a["w1"]).then_inc(s["w1_in"], 16)
            sp.dma_start(w2, a["w2"]).then_inc(s["w2_in"], 16)
            sp.dma_start(b2b, a["b2"]).then_inc(s["b2_in"], 16)
            def by_token(dram):
                return dram

            sp.wait_ge(s["v_ready"], 1)
            vt = vtok[:, :].rearrange("p (i k) -> p k i", k=3)
            vd = v_dram.rearrange("(i b) l -> b l i", b=2)
            for b in range(2):
                sp.dma_start(vd[b, NI:L], vt[:, b]).then_inc(s["v_out"], 16)
                sp.dma_start(vd[b, 0:NI], vt[64 * b:64 * b + NI, 2]).then_inc(s["v_out"], 16)
            sp.wait_ge(s["v_out"], 64)
            sp.dma_start(vv[0:B, :], v_dram).then_inc(s["v_in"], 16)
            sp.dma_start(vv[B:2 * B, :], v_dram[:, ::-1]).then_inc(s["v_in"], 16)

            sp.wait_ge(s["list_written"], 16 * 2 * SLOTS)
            for t in range(2):
                sp.dma_start(xg[:, t, :], sorted_rows[128 * t:128 * (t + 1)]).then_inc(s[f"xg_in{t}"], 16)

            def load_tile(t, w):
                sp.wait_ge(s["xgT_taken"], t + 1)
                sp.dma_start(xg[:, w, :], sorted_rows[ds(128 * (t + 2), 128), :]).then_inc(s[f"xg_in{w}"], 16)

            with sp.Fori(0, GTILES // 4) as it:
                for j in range(4):
                    load_tile(it * 4 + j, j % 2)
            load_tile(GTILES, 0)
            sp.wait_ge(s["recurrence_done"], 1)
            sp.dma_start(ge[:, :, :], gs[B:2 * B, 0:L, :]).then_inc(s["ge_in"], 16)
            load_tile(GTILES + 1, 1)
            sp.wait_ge(s["green_ready"], 1)
            sp.dma_start(g_dram, g2[:, :, :]).then_inc(s["g_out"], 16)
            load_tile(GTILES + 2, 0)
            sp.wait_ge(s["g_out"], 16)
            gd = g_dram.rearrange("(i b) l c -> b l i c", b=2)
            gv = gtok[:, :, :].rearrange("p (i k) c -> p k i c", k=3)
            for b in range(2):
                sp.dma_start(gv[:, b], gd[b, NI:L]).then_inc(s["gtok_in"], 16)
                sp.dma_start(gv[64 * b:64 * b + NI, 2], gd[b, 0:NI]).then_inc(s["gtok_in"], 16)
            load_tile(GTILES + 3, 1)
            with sp.Fori(GTILES // 4 + 1, TILES // 4) as it:
                for j in range(4):
                    load_tile(it * 4 + j, j % 2)
            sp.wait_ge(s["l1_psum"], 2 + TILES + 1)
            for k in range(2):
                sp.wait_ge(s[f"plane_written{k}"], 8 * TILES)
            pd = planes[0:2 * PLANE].rearrange("(k i b l) n -> k b l i n", k=2, b=2, l=L)
            pv_ = plane_in.rearrange("p k (i j) n -> p k j i n", j=3)
            for k in range(2):
                for b in range(2):
                    sp.dma_start(pv_[:, k, b], pd[k, b, NI:L]).then_inc(s["planes_in"], 16)
                    sp.dma_start(pv_[64 * b:64 * b + NI, k, 2], pd[k, b, 0:NI]).then_inc(s["planes_in"], 16)
            sp.wait_ge(s["total_ready"], 1)
            od = out.rearrange("(i b) l n -> b l i n", b=2)
            hv = h[:, :, :].rearrange("p (i j) n -> p j i n", j=3)
            for b in range(2):
                sp.dma_start(od[b, NI:L], hv[:, b]).then_inc(s["out_written"], 16)
                sp.dma_start(od[b, 0:NI], hv[64 * b:64 * b + NI, 2]).then_inc(s["out_written"], 16)
            sp.wait_ge(s["out_written"], 64)

        @block.gpsimd
        def _(pool):
            nc.gpsimd.memset(ones[:, :], 1.0)
            nc.gpsimd.memset(eps_t[:, :], EPS).then_inc(s["filled"], 1)
            P = nc.gpsimd
            pool.sem_inc(s["x2_copied"], 2)
            with pool.Fori(0, PAIRS // 2) as it:
                for w in range(2):
                    i = it * 2 + w
                    pool.wait_ge(s["x2_ready"], i + 1)
                    P.tensor_copy(rows[:, 0, ds(3 * i, 3), 2:ROW], x2[:, w])
                    P.tensor_copy(rows[:, 1, ds(3 * i, 3), 2:ROW], x2[:, w]).then_inc(s["x2_copied"], 1)
            pool.wait_ge(s["x2_copied"], 2 + PAIRS)
            pool.wait_ge(s["list_filled"], 16)
            pool.wait_ge(s["places_ready"], 1)
            for k in range(2):
                for n in range(SLOTS):
                    pool.indirect_dma_start(out=sorted_rows,
                                            out_offset=bass.IndirectOffsetOnAxis(ap=sidx[:, k * SLOTS + n:k * SLOTS + n + 1].bitcast(U32), axis=0),
                                            in_=rows[:, k, n, :], in_offset=None).then_inc(s["list_written"], 16)
            pool.sem_inc(s["turn_taken"], 1)

            def write_tiles(it, first):
                for j in range(4):
                    t = it * 4 + j
                    pool.wait_ge(s["y2_ready"], 2 + t + 1)
                    if not (first and j == 0):
                        pool.wait_ge(s[f"plane_written{(j + 1) % 2}"], 32 * it + 16 * ((j + 1) // 2))
                    P.tensor_copy(pool_turn[:, ds(t, 1)], eps_t[0:1, :]).then_inc(s["turn_taken"], 1)
                    pool.indirect_dma_start(out=planes,
                                            out_offset=bass.IndirectOffsetOnAxis(ap=meta_i[:, j:j + 1].bitcast(U32), axis=0),
                                            in_=y2[:, j % 2, :], in_offset=None).then_inc(s[f"plane_written{j % 2}"], 16)

            write_tiles(0, True)
            with pool.Fori(1, TILES // 4) as it:
                write_tiles(it, False)

        @block.scalar
        def _(act):
            for dst, src in ((gb, "patch_gb"), (table, "table"), (tb, "tok_b"), (wraw[:, :, :], "wattn"),
                             (lnwb[:, :], "lnwb"), (bqk0[:, :], "bqk"), (bv0[:, :], "bv"), (wb2[:, :], "wb2"),
                             (wp_raw[:, :, :], "wproj"), (mnwb[:, :], "mnwb"), (bproj[:, :], "bproj"),
                             (temp[:, 0:1], "temp"), (gw[:, :, :], "gate_w"),
                             (spec[:, :, :], "spec")):
                act.dma_start(dst, a[src]).then_inc(s["small_in"], 16)
            act.wait_ge(s["windows_in"], 16)
            act.wait_ge(s["onehot_ready"], 1)
            for g in range(PAIRS):
                if g >= 2:
                    act.wait_ge(s["squares_folded"], g - 1)
                nc.scalar.activation(xsq[:, g % 2], xwin[:, :, 128 * g:128 * (g + 1)], ACT.Square).then_inc(s["squares_ready"], 1)
            act.wait_ge(s["filled"], 1)
            for n, (g0, g1) in enumerate(GROUPS):
                act.wait_ge(s["ivar_ready"], n + 1)
                nc.scalar.activation(istat[:, 4, g0:g1], istat[:, 3, g0:g1], ACT.Sqrt, bias=eps_t[:, :]).then_inc(s["isd_ready"], 1)
            act.wait_ge(s["stats_ready"], len(GROUPS))
            nc.scalar.activation(ln[:, 0, :], mv[:, :, 1], ACT.Sqrt, bias=eps_t[:, :]).then_inc(s["sd_ready"], 1)
            act.wait_ge(s["varx_ready"], 1)
            nc.scalar.activation(ln[:, 3, :], ln[:, 2, :], ACT.Sqrt, bias=eps_t[:, :]).then_inc(s["sd_ready"], 1)

            A = nc.scalar
            act.sem_inc(s["xnT_taken"], 2)
            act.sem_inc(s["qk_taken"], 2)
            act.sem_inc(s["th_ready"], 2)
            act.sem_inc(s["sgT_taken"], 1)
            act.wait_ge(s["ln_ready"], 1)
            act.wait_ge(s["attn_weights_ready"], 1)

            def rows_take(i, w, k):
                n, b = 3 * i + k, (w + k) % 2
                act.wait_ge(s["xnT_psum"], 6 + n + 1)
                if k == 0:
                    act.wait_ge(s["tok_psum"], 3 * i + 3)
                    act.wait_ge(s["qk_done"], 4 * i + 2)
                src = bank[b][0:DH, 0:256].rearrange("p (h n) -> p h n", h=2)
                if k < 2:
                    A.activation(xnT[:, w, :, k * L + NI:(k + 1) * L], src, ACT.Copy).then_inc(s["xnT_taken"], 1)
                else:
                    A.activation(ximg[:, w], src, ACT.Copy)
                    for f in range(2):
                        last = A.activation(xnT[:, w, f, :].rearrange("p (b n) -> p b n", b=2)[:, :, 0:NI],
                                            src[:, f, :].rearrange("p (b n) -> p b n", b=2)[:, :, 0:NI], ACT.Copy)
                    last.then_inc(s["xnT_taken"], 1)

            def take_products(i, w, final=False):
                for k in range(3):
                    n, b = 3 * i + k, (w + k) % 2
                    act.wait_ge(s["tok_psum"], 6 + n + 1)
                    act.wait_ge(s["tok_taken"], n + 1)
                    A.activation(th[:, b, :], bank[4 + b][:, D:TW], ACT.Tanh,
                                 scale=ln[:, 5, ds(n, 1)]).then_inc(s["th_ready"], 1)
                for c in range(4):
                    m = 4 * i + c
                    act.wait_ge(s["qk_psum"], m + 1)
                    act.wait_ge(s["qk_done"], 4 + m + 1)
                    A.activation(ek[:, c % 2, :], bank[2 + c % 2][0:DH, 0:PC], ACT.Exp, bias=bqk[:, c:c + 1])
                    A.activation(rk[:, c % 2, :], bank[2 + c % 2][0:DH, 0:PC], ACT.Relu,
                                 bias=bqk[:, c:c + 1]).then_inc(s["qk_taken"], 1)
                    if c < 3:
                        n = 3 * i + c
                        act.wait_ge(s["sgT_psum"], 2 + n + 1)
                        act.wait_ge(s["par_psum"], n + 1)
                        A.activation(sgT[:, (w + c) % 2, :], bank[6][:, 0:128], ACT.Copy).then_inc(s["sgT_taken"], 1)
                        if not final:
                            rows_take(i + 1, 1 - w, c)

            for k in range(3):
                rows_take(0, 0, k)
            with act.Fori(0, PAIRS // 2 - 1) as it:
                take_products(it * 2, 0)
                take_products(it * 2 + 1, 1)
            take_products(PAIRS - 2, 0)
            take_products(PAIRS - 1, 1, final=True)

            act.wait_ge(s["par_taken"], 1 + SLOTS)
            pv = par[:, :, :].rearrange("p s (h k) -> p (s h) k", k=5)
            for k in range(4):
                last = A.activation(gt[:, k, :], pv[:, :, k], ACT.Tanh, scale=0.5 if k % 2 == 0 else 1.0)
            last.then_inc(s["gate_tanh"], 1)
            act.wait_ge(s["phase_ready"], 1)
            HALF_PI = 1.5707962
            A.activation(gt[:, 3, :], gt[:, 1, :], ACT.Sin, scale=HALF_PI).then_inc(s["sin_ready"], 1)
            act.wait_ge(s["inter_ready"], 1)
            A.activation(gt[:, 1, :], gt[:, 0, :], ACT.Tanh, scale=0.25).then_inc(s["inter_tanh"], 1)
            act.wait_ge(s["inter_tanh"], 1)
            A.activation(gt[:, 2, :], gt[:, 1, :], ACT.Tanh, scale=temp[:, 1:2]).then_inc(s["gate_ready"], 1)

            act.sem_inc(s["kft_taken"], 1)
            act.wait_ge(s["qk_done"], 6 + 4 * PAIRS)

            def stage(i, w):
                act.wait_ge(s["out_psum"], i + 1)
                src = qk[:, :, ds(i * PC, PC)]
                A.activation(kst[:, w], src[:, 2:4, :], ACT.Copy)
                for f in range(2):
                    A.activation(kimg[:, w, f, :].rearrange("p (b n) -> p b n", b=2),
                                 src[:, 2 + f, :].rearrange("p (b n) -> p b n", b=2)[:, :, 0:64], ACT.Copy)
                A.activation(qst[:, w], src[:, 0:2, :], ACT.Copy).then_inc(s["staged"], 1)

            def squares(i):
                act.wait_ge(s["uc_ready"], i + 1)
                A.activation(usq[:, ds(3 * i, 3), :], u[:, ds(3 * i, 3), :], ACT.Square).then_inc(s["usq_ready"], 1)

            def attention_copies(i, w, first=False, final=False):
                act.wait_ge(s["kft_psum"], i + 1)
                act.wait_ge(s["state_psum"], i + 1)
                A.activation(kft, bank[6][:, 0:D], ACT.Copy).then_inc(s["kft_taken"], 1)
                if not final:
                    stage(i + 1, 1 - w)
                if not first:
                    squares(i - 1)

            stage(0, 0)
            attention_copies(0, 0, first=True)
            with act.Fori(0, PAIRS // 2 - 1) as it:
                attention_copies(it * 2 + 1, 1)
                attention_copies(it * 2 + 2, 0)
            attention_copies(PAIRS - 1, 1, final=True)
            squares(PAIRS - 1)

            act.wait_ge(s["hvar_ready"], 1)
            A.activation(lnr[:, 2, :], lnr[:, 1, :], ACT.Sqrt, scale=1.0 / HD, bias=eps_t[:, :]).then_inc(s["hsd_ready"], 1)
            act.sem_inc(s["uhT_taken"], 2)
            act.sem_inc(s["x2T_taken"], 2)
            for psum, taken, used, dst in (("uhT_psum", "uhT_taken", "proj_psum", oT), ("x2T_psum", "x2T_taken", "logit_psum", x2T)):
                if dst is x2T:
                    act.wait_ge(s["means2_ready"], 1)
                    A.activation(ln[:, 0, :], mv[:, :, 1], ACT.Sqrt, bias=eps_t[:, :]).then_inc(s["sd2_ready"], 1)
                with act.Fori(0, PAIRS // 2) as it:
                    for j in range(6):
                        n = it * 6 + j
                        act.wait_ge(s[psum], 6 + n + 1)
                        act.wait_ge(s[used], n + 1)
                        A.activation(dst[0:DH, j % 2, :], bank[j % 2][0:DH, 0:256], ACT.Copy).then_inc(s[taken], 1)
            act.wait_ge(s["gap_ready"], 1)
            A.activation(wk[:, 1, :], wk[:, 0, :], ACT.Exp).then_inc(s["ratio_ready"], 1)

            act.sem_inc(s["hid_ready"], 2)
            act.sem_inc(s["y2_ready"], 2)

            def gelu(t, w):
                for f in range(2):
                    act.wait_ge(s["l1_psum"], 2 + t + 1)
                    act.wait_ge(s["hT_psum"], t + 1)
                    ins = A.activation(hid[:, w, 384 * f:384 * (f + 1)], bank[1 + 2 * w + f][:, 0:384], ACT.Gelu_apprx_tanh)
                ins.then_inc(s["hid_ready"], 1)

            gelu(0, 0)
            with act.Fori(0, TILES // 4) as it:
                for j in range(4):
                    t = it * 4 + j
                    gelu(t + 1, (j + 1) % 2)
                    act.wait_ge(s["y1_ready"], 1 + t + 1)
                    act.wait_ge(s["turn_taken"], t + 1)
                    A.activation(y2[:, j % 2, :], y1[:, j % 2, :], ACT.Copy, scale=meta_w[:, j:j + 1]).then_inc(s["y2_ready"], 1)

        @block.tensor
        def _(pe):
            pe.wait_ge(s["constants_in"], 16)
            pe.wait_ge(s["small_in"], 16 * SMALL)
            pe.wait_ge(s["filled"], 1)
            for c in range(4):
                for f in range(2):
                    last = nc.tensor.matmul(bank[3][0:DH, 100 + c:101 + c], wraw[:, f, DH * c:DH * (c + 1)],
                                            lnwb[:, 2 + f:3 + f], start=f == 0, stop=f == 1)
            for f in range(2):
                last = nc.tensor.matmul(bank[7][:, D:2 * D], lnwb[:, 2 + f:3 + f].to_broadcast([DH, 128]),
                                        wraw[:, f, 4 * DH:4 * DH + D], start=f == 0, stop=f == 1)
            for f in range(2):
                last = nc.tensor.matmul(bank[7][:, 0:D], mnwb[:, 1:2].to_broadcast([DH, 128]), wp_raw[:, f, :],
                                        start=f == 0, stop=f == 1)
            last.then_inc(s["attn_bias_sums"], 1)
            for c in range(SHIFTS * NK):
                if c % NK == 0:
                    pe.wait_ge(s[f"patch_weights_in{c // NK}"], 16)
                last = nc.tensor.matmul(bank[6][:, 0:D], gb[:, SHIFTS * NK + c:SHIFTS * NK + c + 1].to_broadcast([KP, 128]),
                                        wpatch[:, c, :], start=c == 0, stop=c == SHIFTS * NK - 1)
                if c % NK == NK - 1:
                    last.then_inc(s["beta_sums"], 1)
            pe.wait_ge(s["onehot_ready"], 1)
            for b in range(B):
                if b >= 2:
                    pe.wait_ge(s["text_taken"], b - 1)
                nc.tensor.matmul(bank[4 + b % 2][:, 0:D], tok_f[:, NT * b:NT * (b + 1)], table, start=True,
                                 stop=True).then_inc(s["text_psum"], 1)
            pe.wait_ge(s["weff_ready"], 1)
            for k in range(NK):
                last = nc.tensor.matmul(bank[7][:, 0:D], ones[0:KP, :], weff[:, k, 0:D], start=k == 0, stop=k == NK - 1)
            last.then_inc(s["gain_sums"], 1)
            pe.wait_ge(s["windows_in"], 16)
            for g in range(PAIRS):
                if g == PAIRS - 2:
                    pe.wait_ge(s["text_taken"], B)
                    pe.wait_ge(s["squares_folded"], PAIRS)
                    for m in range(PAIRS):
                        last = nc.tensor.matmul(bank[3][:, m:m + 1], xss[:, 128 * m:128 * (m + 1)], ones[0:KP, 0:1],
                                                start=True, stop=True)
                    last.then_inc(s["square_sums"], 1)
                for k in range(NK):
                    last = nc.tensor.matmul(pbank[g // 2][:, (D + 1) * (g % 2):(D + 1) * (g % 2 + 1)],
                                            xwin[:, k, 128 * g:128 * (g + 1)], weff[:, k, :], start=k == 0, stop=k == NK - 1)
                last.then_inc(s["patch_sums"], 1)

            pe.sem_inc(s["xnT_psum"], 6)
            pe.sem_inc(s["tok_psum"], 6)
            pe.sem_inc(s["sgT_psum"], 2)
            pe.sem_inc(s["par_psum"], 2)
            pe.wait_ge(s["attn_weights_ready"], 1)

            def row_transpose(i, w, k):
                n, b = 3 * i + k, (w + k) % 2
                pe.wait_ge(s["xn_ready"], n + 1)
                pe.wait_ge(s["xnT_taken"], n + 1)
                for f in range(2):
                    last = nc.tensor.transpose(bank[b][0:DH, 128 * f:128 * (f + 1)],
                                               xn[:, w, k, DH * f:DH * (f + 1)], C("ident"))
                last.then_inc(s["xnT_psum"], 1)

            def products(i, w, final=False):
                def token_product(k):
                    n, b = 3 * i + k, 4 + (w + k) % 2
                    pe.wait_ge(s["xnT_taken"], 2 + n + 1)
                    pe.wait_ge(s["tok_taken"], n + 1)
                    for f in range(2):
                        lhsT = xnT[:, w, f, k * L + NI:(k + 1) * L] if k < 2 else ximg[:, w, f, :]
                        last = nc.tensor.matmul(bank[b][:, 0:TW], lhsT, wtok[:, f, :], start=f == 0, stop=f == 1)
                    last.then_inc(s["tok_psum"], 1)

                def qk_product(c):
                    m = 4 * i + c
                    pe.wait_ge(s["xnT_taken"], 2 + 3 * i + 3)
                    pe.wait_ge(s["qk_taken"], m + 1)
                    for f in range(2):
                        last = nc.tensor.matmul(bank[2 + c % 2][0:DH, 0:PC], wqk[:, f, DH * c:DH * (c + 1)],
                                                xnT[:, w, f, :], start=f == 0, stop=f == 1)
                    last.then_inc(s["qk_psum"], 1)

                def hidden_transpose(k):
                    n = 3 * i + k
                    pe.wait_ge(s["tok_taken"], 2 + n + 1)
                    pe.wait_ge(s["sgT_taken"], n + 1)
                    nc.tensor.transpose(bank[6][:, 0:128], sg[:, (w + k) % 2, :], C("ident")).then_inc(s["sgT_psum"], 1)

                def gate_product(k):
                    n = 3 * i + k
                    pe.wait_ge(s["sgT_taken"], 1 + n + 1)
                    pe.wait_ge(s["par_taken"], n + 1)
                    nc.tensor.matmul(bank[7][:, 0:5 * NH], sgT[:, (w + k) % 2, :], wb2[:, :], start=True,
                                     stop=True).then_inc(s["par_psum"], 1)

                def next_rows(k):
                    if not final:
                        row_transpose(i + 1, 1 - w, k)

                token_product(0)
                token_product(1)
                qk_product(0)
                token_product(2)
                hidden_transpose(0)
                next_rows(0)
                qk_product(1)
                hidden_transpose(1)
                next_rows(1)
                gate_product(0)
                qk_product(2)
                hidden_transpose(2)
                next_rows(2)
                gate_product(1)
                qk_product(3)
                gate_product(2)

            for k in range(3):
                row_transpose(0, 0, k)
            with pe.Fori(0, PAIRS // 2 - 1) as it:
                products(it * 2, 0)
                products(it * 2 + 1, 1)
            products(PAIRS - 2, 0)
            products(PAIRS - 1, 1, final=True)

            pe.sem_inc(s["scores_psum"], 2)
            pe.sem_inc(s["state_psum"], 1)
            pe.sem_inc(s["text_out_done"], 2)
            pe.sem_inc(s["out_psum"], 2)
            with pe.Fori(0, PAIRS // 2) as it:
                for par_i in range(2):
                    i, w = it * 2 + par_i, par_i
                    pe.wait_ge(s["staged"], i + 1)
                    pe.wait_ge(s["kft_taken"], i + 1)
                    for f in range(2):
                        last = nc.tensor.transpose(bank[6][:, DH * f:DH * (f + 1)], kimg[:, w, f, :],
                                                   C("ident", DH)[:, 0:DH])
                    last.then_inc(s["kft_psum"], 1)

                    def scores(t):
                        f, b, tri = t // 4, t // 2 % 2, t % 2
                        if b == 0 and tri == 0:
                            pe.wait_ge(s["qbd_ready"], 2 * i + f + 1)
                            if f == 0:
                                pe.wait_ge(s["si_taken"], i + 1)
                            for b2 in range(2):
                                last = nc.tensor.matmul(bank[2][64 * b2:64 * b2 + 64, HH * NI * f:HH * NI * (f + 1)],
                                                        kimg[:, w, f, 64 * b2:64 * b2 + 64],
                                                        qbd[:, f, :, b2 * L:b2 * L + NI], start=True, stop=True)
                            if f == 1:
                                last.then_inc(s["img_scores_psum"], 1)
                        pe.wait_ge(s["scores_taken"], 8 * i + t + 1)
                        nc.tensor.matmul(bank[tri][:, 0:384], kst[:, w, f, b * L + NI:(b + 1) * L],
                                         qbd[:, f, 3 * tri:3 * tri + 3, b * L + NI:(b + 1) * L],
                                         start=True, stop=True).then_inc(s["scores_psum"], 1)

                    def text_out(t):
                        f, b, tri = t // 4, t // 2 % 2, t % 2
                        pe.wait_ge(s["scores_taken"], 2 + 8 * i + t + 1)
                        for k in range(3):
                            hd = HH * f + 3 * tri + k
                            last = nc.tensor.matmul(bank[3 + b][:, VE * hd:VE * (hd + 1)], sm[:, tri, 128 * k:128 * (k + 1)],
                                                    vst[:, w, b, hd, :],
                                                    start=t in (0, 2) and k == 0, stop=False, skip_group_check=True)
                        last.then_inc(s["text_out_done"], 1)

                    scores(0)
                    pe.wait_ge(s["kft_taken"], 1 + i + 1)
                    pe.wait_ge(s["vg_ready"], i + 1)
                    pe.wait_ge(s["sbd_taken"], i + 1)
                    for b in range(2):
                        for f in range(2):
                            last = nc.tensor.matmul(bank[7 - b][0:DH, HH * VE * f:HH * VE * (f + 1)],
                                                    kft[64 * b:64 * b + NI, DH * f:DH * (f + 1)],
                                                    vst[64 * b:64 * b + NI, w, 2, HH * f:HH * (f + 1), :].rearrange("p h e -> p (h e)"),
                                                    start=True, stop=True)
                    last.then_inc(s["state_psum"], 1)
                    scores(1)
                    pe.wait_ge(s["out_taken"], i + 1)
                    for t in range(2, 8):
                        text_out(t - 2)
                        scores(t)
                    text_out(6)
                    text_out(7)
                    pe.wait_ge(s["sbd_taken"], 1 + i + 1)
                    pe.wait_ge(s["si_taken"], 1 + i + 1)
                    for b in range(2):
                        for f in range(2):
                            nc.tensor.matmul(bank[3 + b][:, HH * VE * f:HH * VE * (f + 1)],
                                             qst[:, w, f, b * L + NI:(b + 1) * L], sbd[:, b, f, :],
                                             start=False, stop=f == 1, skip_group_check=True)
                    for b in range(2):
                        for hd in range(NH):
                            last = nc.tensor.matmul(bank[5][64 * b:64 * b + 64, VE * hd:VE * (hd + 1)],
                                                    si[64 * b:64 * b + 64, NI * hd:NI * hd + 64],
                                                    vst[64 * b:64 * b + 64, w, 2, hd, :],
                                                    start=hd == 0, stop=hd == NH - 1, skip_group_check=True)
                    last.then_inc(s["out_psum"], 1)

            pe.sem_inc(s["uhT_psum"], 6)
            pe.sem_inc(s["proj_psum"], 2)
            pe.sem_inc(s["x2T_psum"], 6)
            pe.sem_inc(s["logit_psum"], 2)
            for src, ready, psum, taken, dst, used, done, wgt, cols in (
                    (uh, "uh_ready", "uhT_psum", "uhT_taken", oT, "proj_taken", "proj_psum", wp, D),
                    (x2, "x2_ready", "x2T_psum", "x2T_taken", x2T, "logit_taken", "logit_psum", gw, NE + 1)):
                with pe.Fori(0, PAIRS // 2) as it:
                    for w in range(2):
                        i = it * 2 + w
                        pe.wait_ge(s[ready], i + 1)

                        def rows_out(k):
                            n, b = 3 * i + k, (w + k) % 2
                            pe.wait_ge(s[taken], n + 1)
                            for f in range(2):
                                last = nc.tensor.transpose(bank[b][0:DH, 128 * f:128 * (f + 1)],
                                                           src[:, w, k, DH * f:DH * (f + 1)], C("ident"))
                            last.then_inc(s[psum], 1)

                        def rows_in(k):
                            n, b = 3 * i + k, (w + k) % 2
                            pe.wait_ge(s[taken], 2 + n + 1)
                            pe.wait_ge(s[used], n + 1)
                            nc.tensor.matmul(bank[2 + b][:, 0:cols], dst[0:DH, b, 0:128], wgt[0:DH, 0, :], start=True, stop=False)
                            nc.tensor.matmul(bank[2 + b][:, 0:cols], dst[0:DH + 1, b, 128:256], wgt[0:DH + 1, 1, :], start=False,
                                             stop=True).then_inc(s[done], 1)

                        rows_out(0)
                        rows_out(1)
                        rows_in(0)
                        rows_out(2)
                        rows_in(1)
                        rows_in(2)
            pe.wait_ge(s["choices_ready"], 1)
            nc.tensor.matmul(bank[4][:, 0:2 * SLOTS * NE], beforeb[:, :], ohb[:, :, :].rearrange("p s e -> p (s e)"),
                             start=True, stop=True)
            nc.tensor.matmul(bank[5][:, 0:2 * SLOTS * NE], onesb[:, :], ohb[:, :, :].rearrange("p s e -> p (s e)"),
                             start=True, stop=True).then_inc(s["ranks_psum"], 1)

            pe.sem_inc(s["l1_psum"], 2)
            pe.sem_inc(s["hT_psum"], 2)
            pe.sem_inc(s["xgT_psum"], 1)
            pe.sem_inc(s["y_psum"], 1)

            def token_transpose(t, w, count):
                pe.wait_ge(s[f"xg_in{w}"], 16 * count)
                pe.wait_ge(s["xgT_taken"], t + 0) if isinstance(t, int) and t > 0 else None
                if not isinstance(t, int):
                    pe.wait_ge(s["xgT_taken"], t)
                for f in range(2):
                    last = nc.tensor.transpose(bank[0][0:DH, 128 * f:128 * (f + 1)], xg[:, w, 2 + DH * f:2 + DH * (f + 1)],
                                               C("ident"))
                last.then_inc(s["xgT_psum"], 1)

            def layer1(t, w):
                e = pe.value_load(eid[0:1, ds(t, 1)], min_val=0, max_val=NE - 1)
                pe.wait_ge(s["xgT_taken"], t + 1)
                pe.wait_ge(s["hid_ready"], t + 1)
                for f in range(2):
                    for q in range(2):
                        m = DH + q
                        last = nc.tensor.matmul(bank[1 + 2 * w + f][:, 0:384], xgT[0:m, w, 128 * q:128 * (q + 1)],
                                                w1[0:m, q, ds(e * FF + 384 * f, 384)], start=q == 0, stop=q == 1)
                last.then_inc(s["l1_psum"], 1)

            pe.wait_ge(s["w1_in"], 16)
            pe.wait_ge(s["w2_in"], 16)
            pe.wait_ge(s["eid_ready"], 1)
            token_transpose(0, 0, 1)
            token_transpose(1, 1, 1)
            layer1(0, 0)
            with pe.Fori(0, TILES // 4) as it:
                for j in range(4):
                    t, w = it * 4 + j, j % 2
                    layer1(t + 1, 1 - w)
                    e0 = pe.value_load(eid[0:1, ds(t, 1)], min_val=0, max_val=NE - 1)
                    pe.wait_ge(s["hid_ready"], 2 + t + 1)
                    for f in range(2):
                        pe.wait_ge(s["hT_taken"], 2 * t + f + 1)
                        for q in range(3):
                            last = nc.tensor.transpose(bank[5 + f][:, 128 * q:128 * (q + 1)],
                                                       hid[:, w, 384 * f + 128 * q:384 * f + 128 * (q + 1)], C("ident"))
                        last.then_inc(s["hT_psum"] if f else s["hT_half"], 1)
                    token_transpose(t + 2, w, 2 * it + j // 2 + 2)
                    for c in range(FC):
                        if c % 3 == 0:
                            pe.wait_ge(s["hT_taken"], 2 + 2 * t + c // 3 + 1)
                        if c == 0:
                            pe.wait_ge(s["y1_ready"], t + 1)
                        last = nc.tensor.matmul(bank[7][:, 0:D], hT[:, w, 128 * c:128 * (c + 1)], w2[:, c, ds(e0 * D, D)],
                                                start=c == 0, stop=c == FC - 1)
                    last.then_inc(s["y_psum"], 1)

        @block.vector
        def _(dve):
            ch = Chain(dve, s["dve_chain"])
            V = nc.vector
            dve.wait_ge(s["constants_in"], 16)
            dve.wait_ge(s["tokens_in"], 16)
            ch.done(V.tensor_scalar(tokneg, tok_i, 0, 64.0, ALU.is_lt, ALU.mult))
            ch.sync()
            ch.done(V.tensor_tensor(tok_f, tokneg, tok_i, ALU.add))
            ch.sync()
            V.tensor_scalar(tok_f, tok_f, 69.0, C("tok", 70), ALU.min, ALU.is_equal).then_inc(s["onehot_ready"], 1)
            dve.wait_ge(s["small_in"], 16 * SMALL)
            for f in range(2):
                V.tensor_scalar(wqk[:, f, :], wraw[:, f, 0:4 * DH], lnwb[:, f:f + 1], None, ALU.mult)
                V.tensor_scalar(wtok[:, f, 0:D], wraw[:, f, 4 * DH:4 * DH + D], lnwb[:, f:f + 1], None, ALU.mult)
                V.tensor_copy(wtok[:, f, D:TW], wraw[:, f, 4 * DH + D:])
                V.tensor_scalar(wp[0:DH, f, :], wp_raw[:, f, :], mnwb[:, 0:1], None, ALU.mult)
            V.tensor_scalar(temp[:, 1:2], temp[:, 0:1], 0.1, 2.0, ALU.max, ALU.min)
            dve.wait_ge(s["attn_bias_sums"], 1)
            V.tensor_tensor(bqk[:, :], bank[3][0:DH, 100:104], bqk0[:, :], ALU.add)
            V.tensor_tensor(bv[:, :], bank[7][:, D:2 * D], bv0[:, :], ALU.add)
            V.tensor_tensor(wp[DH:DH + 1, 1, :], bank[7][DH:DH + 1, 0:D], bproj[DH:DH + 1, :],
                            ALU.add).then_inc(s["attn_weights_ready"], 1)
            wq = [wpatch[:, NK * q:NK * (q + 1), :] for q in range(SHIFTS)]
            V.tensor_copy(weff[:, :, D], C("mult", KP))
            for q in range(SHIFTS):
                dve.wait_ge(s["beta_sums"], q + 1)
                ch.done(V.tensor_tensor(wq[q], wq[q], gb[:, NK * q:NK * (q + 1)].unsqueeze(2).to_broadcast([KP, NK, D]), ALU.mult))
                if q >= 2:
                    ch.sync()
                    ch.done(V.tensor_tensor(wq[q - 1], wq[q - 1], wq[q - 2], ALU.add))
            ch.sync()
            V.tensor_tensor(weff[:, :, 0:D], wq[SHIFTS - 2], wq[SHIFTS - 1], ALU.add).then_inc(s["weff_ready"], 1)
            ch.done(V.tensor_tensor(tokb, bank[6][:, 0:D], tb, ALU.add))
            text = [3 * (b // 2) + b % 2 for b in range(B)]
            for b in range(B):
                dve.wait_ge(s["text_psum"], b + 1)
                V.scalar_tensor_tensor(h[:, text[b], :], bank[4 + b % 2][:, 0:D], float(D) ** 0.5, C("pe"),
                                       ALU.mult, ALU.add).then_inc(s["text_taken"], 1)
            for g in range(PAIRS):
                dve.wait_ge(s["squares_ready"], g + 1)
                ch.done(V.tensor_tensor(xsq[:, g % 2], xsq[:, g % 2], C("mult", KP).unsqueeze(2).to_broadcast([KP, NK, 128]), ALU.mult))
                ch.sync()
                V.tensor_reduce(xss[:, 128 * g:128 * (g + 1)], xsq[:, g % 2].rearrange("p k n -> p n k"), AX.X,
                                ALU.add).then_inc(s["squares_folded"], 1)
            dve.wait_ge(s["text_taken"], B)
            for b in range(B):
                ch.done(V.bn_stats(st[:, text[b], :], h[:, text[b], :]))
            ch.sync()
            for b in range(B):
                V.bn_aggr(mv[:, text[b], :], st[:, text[b], :])
            dve.wait_ge(s["gain_sums"], 1)
            ch.done(V.tensor_copy(gsum, bank[7][:, 0:D]))
            img = lambda g: h[:, 3 * g + 2, :]
            dve.wait_ge(s["square_sums"], 1)
            ch.done(V.tensor_scalar(istat[:, 1, :], bank[3][:, 0:PAIRS], 1.0 / PDIM, None, ALU.mult))
            for n, (g0, g1) in enumerate(GROUPS):
                dve.wait_ge(s["patch_sums"], g1)
                for g in range(g0, g1):
                    ch.done(V.tensor_scalar(istat[:, 0, g:g + 1], pbank[g // 2][:, (D + 1) * (g % 2) + D:(D + 1) * (g % 2 + 1)],
                                            1.0 / PDIM, None, ALU.mult))
                ch.sync()
                ch.done(V.tensor_tensor(istat[:, 2, g0:g1], istat[:, 0, g0:g1], istat[:, 0, g0:g1], ALU.mult))
                ch.sync()
                ch.done(V.tensor_tensor(istat[:, 3, g0:g1], istat[:, 1, g0:g1], istat[:, 2, g0:g1], ALU.subtract))
                ch.sync()
                V.tensor_scalar(istat[:, 3, g0:g1], istat[:, 3, g0:g1], 0.0, None, ALU.max).then_inc(s["ivar_ready"], 1)
                ch.done(V.tensor_scalar(istat[:, 6, g0:g1], istat[:, 0, g0:g1], -1.0, None, ALU.mult))
                ch.sync()
                for g in range(g0, g1):
                    ch.done(V.scalar_tensor_tensor(img(g), gsum, istat[:, 6, g:g + 1],
                                                   pbank[g // 2][:, (D + 1) * (g % 2):(D + 1) * (g % 2) + D], ALU.mult, ALU.add))
                dve.wait_ge(s["isd_ready"], n + 1)
                ch.done(V.reciprocal(istat[:, 5, g0:g1], istat[:, 4, g0:g1]))
                ch.sync()
                for g in range(g0, g1):
                    ch.done(V.scalar_tensor_tensor(img(g), img(g), istat[:, 5, g:g + 1], tokb, ALU.mult, ALU.add))
                ch.sync()
                for g in range(g0, g1):
                    ch.done(V.bn_stats(st[:, 3 * g + 2, :], img(g)))
                ch.sync()
                for g in range(g0, g1):
                    last = V.bn_aggr(mv[:, 3 * g + 2, :], st[:, 3 * g + 2, :])
                last.then_inc(s["stats_ready"], 1)
            dve.wait_ge(s["sd_ready"], 1)
            ch.done(V.reciprocal(ln[:, 1, :], ln[:, 0, :]))
            ch.sync()
            ch.done(V.tensor_tensor(ln[:, 2, :], mv[:, :, 1], ln[:, 1, :], ALU.mult))
            ch.sync()
            V.tensor_tensor(ln[:, 2, :], ln[:, 2, :], ln[:, 1, :], ALU.mult).then_inc(s["varx_ready"], 1)
            dve.wait_ge(s["sd_ready"], 2)
            ch.done(V.reciprocal(ln[:, 4, :], ln[:, 3, :]))
            ch.sync()
            V.tensor_scalar(ln[:, 5, :], ln[:, 3, :], 0.5, None, ALU.mult)
            V.tensor_tensor(ln[:, 4, :], ln[:, 4, :], ln[:, 1, :], ALU.mult).then_inc(s["ln_ready"], 1)

            dve.sem_inc(s["qk_done"], 6)
            dve.sem_inc(s["tok_taken"], 2)
            dve.sem_inc(s["par_taken"], 1)
            dve.wait_ge(s["ln_ready"], 1)
            dve.wait_ge(s["attn_weights_ready"], 1)

            def norm_rows(i, w):
                dve.wait_ge(s["xnT_psum"], 3 * i + 3)
                for k in range(3):
                    n = 3 * i + k
                    V.tensor_scalar(xn[:, w, k, :], h[:, ds(n, 1), :].rearrange("p a n -> p (a n)"), mv[:, ds(n, 1), 0],
                                    ln[:, 4, ds(n, 1)], ALU.subtract, ALU.mult).then_inc(s["xn_ready"], 1)

            def finish_products(i, w, final=False):
                if not final:
                    norm_rows(i + 1, 1 - w)
                for k in range(3):
                    n, b = 3 * i + k, (w + k) % 2
                    dve.wait_ge(s["tok_psum"], 6 + n + 1)
                    dve.wait_ge(s["th_ready"], 2 + n + 1)
                    V.tensor_tensor(vx[:, ds(n, 1), :, :].rearrange("p a h e -> p (a h) e"),
                                    bank[4 + b][:, 0:D].rearrange("p (h e) -> p h e", h=NH),
                                    bv[:, :].rearrange("p (h e) -> p h e", h=NH), ALU.add)
                    dve.wait_ge(s["sgT_psum"], n + 1)
                    V.scalar_tensor_tensor(sg[:, b, :], th[:, b, :], 1.0, bank[4 + b][:, D:TW], ALU.add,
                                           ALU.mult).then_inc(s["tok_taken"], 1)

                def qk_finish(c):
                    m = 4 * i + c
                    dve.wait_ge(s["qk_taken"], 2 + m + 1)
                    V.scalar_tensor_tensor(qk[:, c, ds(i * PC, PC)], ek[:, c % 2, :], 1.0, rk[:, c % 2, :], ALU.min,
                                           ALU.add).then_inc(s["qk_done"], 1)

                def gate_take(k):
                    n = 3 * i + k
                    dve.wait_ge(s["par_psum"], 2 + n + 1)
                    V.tensor_scalar(par[:, ds(n, 1), :].rearrange("p a n -> p (a n)"), bank[7][:, 0:5 * NH],
                                    ln[:, 5, ds(n, 1)], None, ALU.mult).then_inc(s["par_taken"], 1)

                qk_finish(0)
                qk_finish(1)
                gate_take(0)
                qk_finish(2)
                gate_take(1)
                qk_finish(3)
                gate_take(2)

            norm_rows(0, 0)
            with dve.Fori(0, PAIRS // 2 - 1) as it:
                finish_products(it * 2, 0)
                finish_products(it * 2 + 1, 1)
            finish_products(PAIRS - 2, 0)
            finish_products(PAIRS - 1, 1, final=True)

            dve.wait_ge(s["gate_tanh"], 1)
            ch.done(V.tensor_scalar(gt[:, 0, :], gt[:, 0, :], 1.0, None, ALU.add))
            V.tensor_tensor(gt[:, 1, :], gt[:, 1, :], gt[:, 3, :], ALU.subtract).then_inc(s["phase_ready"], 1)
            ch.sync()
            ch.done(V.scalar_tensor_tensor(gt[:, 0, :], gt[:, 2, :], 1.0, gt[:, 0, :], ALU.add, ALU.mult))
            dve.wait_ge(s["sin_ready"], 1)
            ch.done(V.tensor_tensor(gt[:, 4, :], gt[:, 3, :], gt[:, 3, :], ALU.mult))
            ch.sync()
            ch.done(V.tensor_scalar(gt[:, 4, :], gt[:, 4, :], -2.0, 1.0, ALU.mult, ALU.add))
            ch.done(V.tensor_scalar(temp[:, 1:2], temp[:, 1:2], 0.5, None, ALU.mult))
            ch.sync()
            V.tensor_tensor(gt[:, 0, :], gt[:, 0, :], gt[:, 4, :], ALU.mult).then_inc(s["inter_ready"], 1)
            dve.wait_ge(s["gate_ready"], 1)
            ch.done(V.tensor_scalar(gt[:, 4, :], gt[:, 2, :], 0.5, 1.5, ALU.mult, ALU.add))
            ch.done(V.memset(si[:, NH * NI:], 0.0))
            ch.done(V.memset(vst[:, :, :, :, HD:VE], 1.0))
            ch.sync()

            dve.sem_inc(s["si_taken"], 1)
            dve.sem_inc(s["scores_taken"], 2)
            dve.sem_inc(s["sbd_taken"], 1)
            dve.sem_inc(s["out_taken"], 1)
            def expand(i, f):
                for k in range(HH):
                    last = V.tensor_scalar(qbd[:, f, k, :], qk[:, f, ds(i * PC, PC)], C("hmask", DH)[:, k:k + 1],
                                           None, ALU.mult)
                last.then_inc(s["qbd_ready"], 1)

            def gate_values(i, w):
                dve.wait_ge(s["out_psum"], i + 1)
                V.tensor_tensor(vst[:, w, :, :, 0:HD].rearrange("p s h e -> p (s h) e"),
                                vx[:, ds(3 * i, 3), :, :].rearrange("p s h e -> p (s h) e"),
                                gt[:, 4, ds(3 * NH * i, 3 * NH)].unsqueeze(2).to_broadcast([128, 3 * NH, HD]),
                                ALU.mult).then_inc(s["vg_ready"], 1)

            def rows_of(i):
                return [u[:, ds(3 * i + k, 1), :].rearrange("p a (h e) -> p (a h) e", h=NH) for k in range(3)]

            def centre(i):
                dve.wait_ge(s["out_taken"], 1 + i + 1)
                for k in range(3):
                    last = V.tensor_reduce(lnr[:, 0, ds(3 * NH * i + NH * k, NH)], rows_of(i)[k], AX.X, ALU.add)
                last.then_inc(s["head_sums"], 1)
                dve.wait_ge(s["head_sums"], i + 1)
                for k in range(3):
                    last = V.scalar_tensor_tensor(rows_of(i)[k], lnr[:, 0, ds(3 * NH * i + NH * k, NH)].unsqueeze(2).to_broadcast([128, NH, HD]),
                                                  -1.0 / HD, rows_of(i)[k], ALU.mult, ALU.add)
                last.then_inc(s["uc_ready"], 1)

            def attention_masks(i, w, first=False, final=False):
                ch.k = 0
                ch.at(i)

                def mask(t):
                    tri = t % 2
                    dve.wait_ge(s["scores_psum"], 2 + 8 * i + t + 1)
                    dve.wait_ge(s["text_out_done"], 8 * i + t + 1)
                    V.tensor_tensor(sm[:, tri, :].rearrange("p (h n) -> p h n", h=3),
                                    bank[tri][:, 0:384].rearrange("p (h n) -> p h n", h=3),
                                    C("causal").unsqueeze(1).to_broadcast([128, 3, 128]), ALU.mult).then_inc(s["scores_taken"], 1)

                mask(0)
                mask(1)
                dve.wait_ge(s["state_psum"], 1 + i + 1)
                for b in range(2):
                    last = V.tensor_tensor(sbd[:, b], bank[7 - b][0:DH, 0:2 * HH * VE].rearrange("p (c n) -> p c n", c=2),
                                           C("blk", DH).unsqueeze(1).to_broadcast([DH, 2, HH * VE]), ALU.mult)
                last.then_inc(s["sbd_taken"], 1)
                mask(2)
                if not first:
                    centre(i - 1)
                mask(3)
                mask(4)
                mask(5)
                dve.wait_ge(s["img_scores_psum"], i + 1)
                V.tensor_tensor(si[:, 0:NH * NI].rearrange("p (h n) -> p h n", h=NH),
                                bank[2][:, 0:NH * NI].rearrange("p (h n) -> p h n", h=NH),
                                C("icausal").unsqueeze(1).to_broadcast([128, NH, NI]), ALU.mult).then_inc(s["si_taken"], 1)
                mask(6)
                mask(7)
                if not final:
                    expand(i + 1, 0)
                    expand(i + 1, 1)
                    gate_values(i + 1, 1 - w)
                dve.wait_ge(s["out_psum"], 2 + i + 1)
                o = [bank[3 + k][:, 0:NH * VE].rearrange("p (h e) -> p h e", h=NH) for k in range(3)]
                for k in range(3):
                    last = V.tensor_scalar(rden[:, k, :], o[k][:, :, HD], 1e-6, None, ALU.add)
                ch.done(last)
                ch.sync()
                ch.done(V.reciprocal(rden[:, :, :], rden[:, :, :]))
                ch.sync()
                for k in range(3):
                    last = V.tensor_tensor(rows_of(i)[k], o[k][:, :, 0:HD],
                                           rden[:, k, :].unsqueeze(2).to_broadcast([128, NH, HD]), ALU.mult)
                last.then_inc(s["out_taken"], 1)

            expand(0, 0)
            expand(0, 1)
            gate_values(0, 0)
            ch.enter(2)
            attention_masks(0, 0, first=True)
            with dve.Fori(0, PAIRS // 2 - 1) as it:
                attention_masks(it * 2 + 1, 1)
                attention_masks(it * 2 + 2, 0)
            attention_masks(PAIRS - 1, 1, final=True)
            centre(PAIRS - 1)
            ch.leave(PAIRS)

            dve.wait_ge(s["usq_ready"], PAIRS)
            V.tensor_reduce(lnr[:, 1, :], usq.rearrange("p s (h e) -> p (s h) e", h=NH), AX.X, ALU.add).then_inc(s["hvar_ready"], 1)
            dve.wait_ge(s["hvar_ready"], 1)
            ch.done(V.memset(oT[DH:DH + 1], 1.0))
            ch.done(V.memset(x2T[DH:DH + 1], 1.0))
            ch.sync()
            dve.wait_ge(s["hsd_ready"], 1)
            ch.done(V.reciprocal(lnr[:, 2, :], lnr[:, 2, :]))
            ch.sync()
            dve.sem_inc(s["proj_taken"], 2)
            dve.sem_inc(s["logit_taken"], 2)

            def head_norm(i, w):
                dve.wait_ge(s["uhT_psum"], 3 * i + 3)
                uv = u[:, ds(3 * i, 3), :]
                for k in range(3):
                    last = V.tensor_tensor(uh[:, w, k].rearrange("p (h e) -> p h e", h=NH),
                                           u[:, ds(3 * i + k, 1), :].rearrange("p a (h e) -> p (a h) e", h=NH),
                                           lnr[:, 2, ds(3 * NH * i + NH * k, NH)].unsqueeze(2).to_broadcast([128, NH, HD]), ALU.mult)
                last.then_inc(s["uh_ready"], 1)

            def residual(i):
                for k in range(3):
                    hr = h[:, ds(3 * i + k, 1), :].rearrange("p a n -> p (a n)")
                    dve.wait_ge(s["proj_psum"], 2 + 3 * i + k + 1)
                    V.tensor_tensor(hr, hr, bank[2 + (i_par(i) + k) % 2][:, 0:D], ALU.add).then_inc(s["proj_taken"], 1)
                dve.wait_ge(s["proj_taken"], 2 + 3 * i + 3)
                for k in range(3):
                    last = V.bn_stats(st[:, ds(3 * i + k, 1), :].rearrange("p a n -> p (a n)"), h[:, ds(3 * i + k, 1), :].rearrange("p a n -> p (a n)"))
                last.then_inc(s["stats2_done"], 1)

            par_now = [0]
            i_par = lambda i: par_now[0]
            head_norm(0, 0)
            with dve.Fori(0, PAIRS // 2 - 1) as it:
                for w in range(2):
                    par_now[0] = w
                    head_norm(it * 2 + w + 1, 1 - w)
                    residual(it * 2 + w)
            for i in (PAIRS - 2, PAIRS - 1):
                par_now[0] = i % 2
                if i == PAIRS - 2:
                    head_norm(i + 1, 1)
                residual(i)
            dve.wait_ge(s["stats2_done"], PAIRS)
            for n in range(SLOTS):
                last = V.bn_aggr(mv[:, n, :], st[:, n, :])
            last.then_inc(s["means2_ready"], 1)
            dve.wait_ge(s["sd2_ready"], 1)
            ch.done(V.reciprocal(ln[:, 1, :], ln[:, 0, :]))
            ch.sync()

            def token_norm(i, w):
                dve.wait_ge(s["x2T_psum"], 3 * i + 3)
                dve.wait_ge(s["x2_copied"], i + 1)
                for k in range(3):
                    last = V.tensor_scalar(x2[:, w, k], h[:, ds(3 * i + k, 1), :].rearrange("p a n -> p (a n)"), mv[:, ds(3 * i + k, 1), 0],
                                           ln[:, 1, ds(3 * i + k, 1)], ALU.subtract, ALU.mult)
                last.then_inc(s["x2_ready"], 1)

            def choose(i):
                for k in range(3):
                    dve.wait_ge(s["logit_psum"], 2 + 3 * i + k + 1)
                    V.tensor_copy(lg[:, ds(3 * i + k, 1), :].rearrange("p a n -> p (a n)"),
                                  bank[2 + (par_now[0] + k) % 2][:, 0:NE + 1]).then_inc(s["logit_taken"], 1)

            token_norm(0, 0)
            with dve.Fori(0, PAIRS // 2 - 1) as it:
                for w in range(2):
                    par_now[0] = w
                    token_norm(it * 2 + w + 1, 1 - w)
                    choose(it * 2 + w)
            for i in (PAIRS - 2, PAIRS - 1):
                par_now[0] = i % 2
                if i == PAIRS - 2:
                    token_norm(i + 1, 1)
                choose(i)
            dve.wait_ge(s["logit_taken"], 2 + SLOTS)
            for n in range(SLOTS):
                ch.done(V.max(m8[:, n, :], lg[:, n, 0:NE]))
            ch.sync()
            for n in range(SLOTS):
                ch.done(V.max_index(ix[:, n, :], m8[:, n, :], lg[:, n, 0:NE]))
            ch.sync()
            V.tensor_scalar(vtok[:, :], lg[:, :, NE], -3.0, 3.0, ALU.max, ALU.min).then_inc(s["v_ready"], 1)
            V.tensor_tensor(wk[:, 0, :], m8[:, :, 1], m8[:, :, 0], ALU.subtract).then_inc(s["gap_ready"], 1)
            for k in range(2):
                ch.done(V.tensor_copy(ixf[:, k, :], ix[:, :, k]))
            V.tensor_copy(beforeb[:, :], C("before"))
            ch.done(V.memset(onesb[:, :], 1.0))
            ch.sync()
            ch.done(V.tensor_tensor(ohf[:, :, :], ixf[:, :, :].rearrange("p k s -> p (k s)").unsqueeze(2).to_broadcast([128, 2 * SLOTS, NE]),
                                    C("iota8").unsqueeze(1).to_broadcast([128, 2 * SLOTS, NE]), ALU.is_equal))
            ch.sync()
            for k in range(2):
                last = V.tensor_tensor(ohb[:, k * SLOTS:(k + 1) * SLOTS, :], ohf[:, k * SLOTS:(k + 1) * SLOTS, :],
                                       C("valid").unsqueeze(2).to_broadcast([128, SLOTS, NE]), ALU.mult)
            last.then_inc(s["choices_ready"], 1)
            dve.wait_ge(s["ratio_ready"], 1)
            ch.done(V.tensor_scalar(wk[:, 0, :], wk[:, 1, :], 1.0, None, ALU.add))
            ch.sync()
            ch.done(V.reciprocal(wk[:, 0, :], wk[:, 0, :]))
            ch.sync()
            dve.wait_ge(s["x2_copied"], 2 + PAIRS)
            V.tensor_copy(rows[:, 0, :, 0], wk[:, 0, :])
            V.tensor_tensor(rows[:, 1, :, 0], wk[:, 0, :], wk[:, 1, :], ALU.mult)
            V.tensor_copy(rows[:, :, :, 1], C("place").rearrange("p (k s) -> p k s", k=2))
            dve.wait_ge(s["ranks_psum"], 1)
            ch.done(V.tensor_copy(tot[:, :, :], bank[5][:, 0:2 * SLOTS * NE].rearrange("p (s e) -> p e s", e=NE)))
            ch.sync()
            for e in range(NE):
                ch.done(V.tensor_tensor_scan(inc[:, e, :], ones[:, 0:2 * SLOTS], tot[:, e, :], 0.0, ALU.mult, ALU.add))
            ch.sync()
            ch.done(V.tensor_tensor(ohf[:, :, :].rearrange("p s e -> p (s e)").rearrange("p (e s) -> p e s", e=NE),
                                    inc[:, :, 2 * SLOTS - 1:2 * SLOTS].to_broadcast([128, NE, 2 * SLOTS]),
                                    C("steps").unsqueeze(1).to_broadcast([128, NE, 2 * SLOTS]), ALU.is_gt))
            ch.sync()
            ch.done(V.tensor_reduce(cnt[:, 0, :], ohf[:, :, :].rearrange("p s e -> p (s e)").rearrange("p (e s) -> p e s", e=NE), AX.X, ALU.add))
            ch.sync()
            ch.done(V.tensor_tensor_scan(cnt[:, 1, :], ones[:, 0:NE], cnt[:, 0, :], 0.0, ALU.mult, ALU.add))
            ch.sync()
            ch.done(V.tensor_tensor(cnt[:, 2, :], cnt[:, 1, :], cnt[:, 0, :], ALU.subtract))
            ch.done(V.tensor_tensor(inc[:, :, :], inc[:, :, :], tot[:, :, :], ALU.subtract))
            ch.done(V.tensor_tensor(ecmp[:, :, :], cnt[0:1, 1, :].unsqueeze(1).to_broadcast([1, TILES + 2, NE]),
                                    C("tile8", 1).rearrange("p (t e) -> p t e", e=NE), ALU.is_le))
            ch.sync()
            ch.done(V.tensor_scalar(cnt[:, 3, :], cnt[:, 2, :], 128.0, None, ALU.mult))
            ch.done(V.tensor_reduce(eidf[:, :], ecmp[:, :, :], AX.X, ALU.add))
            ch.sync()
            V.tensor_scalar(eid[:, :], eidf[:, :], NE - 1.0, None, ALU.min).then_inc(s["eid_ready"], 1)
            ch.done(V.tensor_tensor(inc[:, :, :], inc[:, :, :], cnt[:, 3, :].unsqueeze(2).to_broadcast([128, NE, 2 * SLOTS]), ALU.add))
            ch.sync()
            ch.done(V.tensor_tensor(ohf[:, :, :], bank[4][:, 0:2 * SLOTS * NE].rearrange("p (s e) -> p s e", e=NE),
                                    inc[:, :, :].rearrange("p e s -> p s e"), ALU.add))
            ch.sync()
            ch.done(V.tensor_tensor(ohf[:, :, :], ohf[:, :, :], ohb[:, :, :], ALU.mult))
            ch.sync()
            ch.done(V.tensor_reduce(pos[:, :], ohf[:, :, :], AX.X, ALU.add))
            ch.sync()
            V.tensor_tensor(sidx[:, :], pos[:, :], C("trash"), ALU.add).then_inc(s["places_ready"], 1)
            ch.done(V.memset(ga[:, :, 0], 0.0))
            ch.done(V.memset(ga[:, :, 1], -1.0))
            ch.done(V.memset(gtok[:, :, :], 0.0))
            ch.done(V.memset(xgT[DH:DH + 1], 1.0))
            for k in range(3):
                ch.done(V.tensor_tensor(spec[:, k, :], spec[:, k, :], spec[:, 3, :], ALU.mult))
            ch.sync()
            dve.wait_ge(s["v_in"], 32)
            ch.done(V.scalar_tensor_tensor(ga[:, 0:L, 0], vv[:, :], -2.0, C("sign", 32)[:, 0:L], ALU.add, ALU.mult))
            ch.sync()
            ch.done(V.tensor_copy(gs[:, 0, :], ga[:, 0, :]))
            ch.sync()

            def recurrence(first, steps):
                for g in range(steps):
                    now = gs[:, ds(first + g, 1), :].rearrange("p a c -> p (a c)")
                    nxt = gs[:, ds(first + g + 1, 1), :].rearrange("p a c -> p (a c)")
                    ch.done(V.scalar_tensor_tensor(gq[:, 2:4], now, 1.0, now, ALU.mult, ALU.mult, accum_out=gq[:, 0:1]))
                    ch.sync()
                    ch.done(V.reciprocal(gq[:, 1:2], gq[:, 0:1]))
                    ch.sync()
                    ch.done(V.scalar_tensor_tensor(nxt, now, gq[:, 1:2], ga[:, ds(first + g + 1, 1), :].rearrange("p a c -> p (a c)"),
                                                   ALU.mult, ALU.add))
                    ch.sync()

            ch.enter(3 * 4)
            with dve.Fori(0, GFIRST // 4) as it:
                ch.at(it)
                recurrence(it * 4, 4)
            ch.leave(GFIRST // 4)

            def green():
                dve.wait_ge(s["recurrence_done"], 1)
                dve.wait_ge(s["ge_in"], 16)
                ch.done(V.tensor_tensor(gg[:, 1, :], ge[:, :, 0], C("sign", B)[:, 0:L], ALU.mult))
                ch.sync()
                ch.done(V.tensor_tensor(gg[:, 0, :], gg[:, 0, :], gg[:, 1, ::-1], ALU.add))
                ch.done(V.tensor_tensor(gg[:, 2, :], gs[0:B, 0:L, 1], ge[:, ::-1, 1], ALU.add))
                ch.sync()
                ch.done(V.scalar_tensor_tensor(gg[:, 0, :], vv[0:B, :], -2.0, gg[:, 0, :], ALU.add, ALU.subtract))
                ch.done(V.tensor_scalar(gg[:, 2, :], gg[:, 2, :], 1.0, None, ALU.add))
                ch.sync()
                ch.done(V.tensor_tensor(gg[:, 1, :], gg[:, 0, :], gg[:, 0, :], ALU.mult))
                ch.done(V.tensor_tensor(gg[:, 3, :], gg[:, 2, :], gg[:, 2, :], ALU.mult))
                ch.sync()
                ch.done(V.tensor_tensor(gg[:, 1, :], gg[:, 1, :], gg[:, 3, :], ALU.add))
                ch.sync()
                ch.done(V.reciprocal(gg[:, 1, :], gg[:, 1, :]))
                ch.sync()
                for k in range(2):
                    ch.done(V.scalar_tensor_tensor(gg[:, 2 * k, :], gg[:, 2 * k, :], -1.0, gg[:, 1, :], ALU.mult, ALU.mult))
                ch.sync()
                for k in range(2):
                    last = V.tensor_scalar(g2[:, :, k], gg[:, 2 * k, :], -10.0, 10.0, ALU.max, ALU.min)
                last.then_inc(s["green_ready"], 1)

            def add_features(n, count):
                hr = [h[:, ds(n + m, 1), :].rearrange("p a n -> p (a n)") for m in range(count)]
                dve.wait_ge(s["gtok_in"], 64)
                for c in range(2):
                    for m in range(count):
                        ch.done(V.scalar_tensor_tensor(hr[m], spec[:, c, :], gtok[:, ds(n + m, 1), c], hr[m], ALU.mult, ALU.add))
                    ch.sync()
                for m in range(count):
                    ch.done(V.tensor_tensor(hr[m], hr[m], spec[:, 2, :], ALU.add))

            dve.sem_inc(s["hT_taken"], 2)
            dve.sem_inc(s["y1_ready"], 1)

            def take_tokens(t, w, j):
                dve.wait_ge(s["xgT_psum"], 1 + t + 1)
                V.tensor_copy(meta_w[:, j:j + 1], xg[:, w, 0:1])
                V.tensor_copy(meta_i[:, j:j + 1], xg[:, w, 1:2])
                V.tensor_copy(xgT[0:DH, w, :], bank[0][0:DH, 0:256]).then_inc(s["xgT_taken"], 1)

            dve.wait_ge(s["eid_ready"], 1)
            dve.wait_ge(s["b2_in"], 16)
            take_tokens(0, 0, 0)
            take_tokens(1, 1, 1)

            def tile_steps(t, j, beside):
                w = j % 2
                e = dve.value_load(eid[0:1, ds(t, 1)], min_val=0, max_val=NE - 1)
                for f in range(2):
                    if f:
                        dve.wait_ge(s["hT_psum"], 2 + t + 1)
                    else:
                        dve.wait_ge(s["hT_half"], t + 1)
                        dve.wait_ge(s["y_psum"], t + 1)
                    V.tensor_copy(hT[:, w, 384 * f:384 * (f + 1)], bank[5 + f][:, 0:384]).then_inc(s["hT_taken"], 1)
                dve.wait_ge(s["turn_taken"], t + 1)
                take_tokens(t + 2, w, (j + 2) % 4)
                beside()
                dve.wait_ge(s["y_psum"], 1 + t + 1)
                dve.wait_ge(s["y2_ready"], t + 1)
                V.tensor_tensor(y1[:, w, :], bank[7][:, 0:D], b2b[:, ds(e * D, D)], ALU.add).then_inc(s["y1_ready"], 1)

            ch.enter(4 * 3 * GSTEP)
            with dve.Fori(0, GTILES // 4) as it:
                ch.at(it)
                for j in range(4):
                    t = it * 4 + j
                    tile_steps(t, j, lambda: recurrence(t * GSTEP + GFIRST, GSTEP))
            ch.leave(GTILES // 4)
            V.tensor_tensor(gg[:, 0, :], gs[0:B, 0:L, 0], C("sign", B)[:, 0:L], ALU.mult).then_inc(s["recurrence_done"], 1)
            LATE = SLOTS - (TILES - GTILES - 4)
            tile_steps(GTILES, 0, lambda: None)
            tile_steps(GTILES + 1, 1, green)
            tile_steps(GTILES + 2, 2, lambda: None)
            tile_steps(GTILES + 3, 3, lambda: add_features(0, LATE))
            ch.enter(4 * 3)
            with dve.Fori(GTILES // 4 + 1, TILES // 4) as it:
                ch.at(it - (GTILES // 4 + 1))
                for j in range(4):
                    t = it * 4 + j
                    tile_steps(t, j, lambda: add_features(t - (GTILES + 4 - LATE), 1))
            ch.leave(TILES // 4 - GTILES // 4 - 1)

            ch.sync()
            dve.wait_ge(s["planes_in"], 16 * 8)
            hv = h[:, :, :].rearrange("p (i j) n -> p j i n", j=3)
            pin = plane_in.rearrange("p k (i j) n -> p k j i n", j=3)
            parts = [(0, 128, 0), (0, 128, 1), (0, NI, 2), (64, 64 + NI, 2)]
            for k in range(2):
                for lo, hi, j in parts:
                    last = V.tensor_tensor(hv[lo:hi, j], hv[lo:hi, j], pin[lo:hi, k, j], ALU.add)
                    if k == 0:
                        ch.done(last)
                ch.sync()
            last.then_inc(s["total_ready"], 1)


def laid_out(inp):
    import numpy as np

    f = {k: np.asarray(v) for k, v in inp.items()}
    arr = {}
    x = f["x"]
    pad = np.pad(x, ((0, 0), (0, 0), (1, 1), (1, 1)))
    win = np.stack([pad[:, :, PATCH * p:PATCH * p + WIN, :] for p in range(SIDE)], 2)
    win = np.stack([win[..., PATCH * p:PATCH * p + WIN] for p in range(SIDE)], 3)
    win = win.reshape(B, CH, SIDE, SIDE, WIN, NK, 2).transpose(6, 1, 4, 5, 0, 2, 3).reshape(KP, NK, B, NI)
    arr["xwin"] = np.pad(win, ((0, 0), (0, 0), (0, 0), (0, 64 - NI))).reshape(KP, NK, PT)

    def windowed(t):
        n = t.shape[1]
        t = t.reshape(PATCH, PATCH, SHIFTS, CH, n)
        o = np.zeros((2, CH, WIN, SHIFTS, NK, n), t.dtype)
        for sft, (dr, dc) in enumerate(((1, 1), (1, 0), (1, 2), (0, 1), (2, 1))):
            for par in range(2):
                js = [j for j in range(PATCH) if (j + dc) % 2 == par]
                ks = [(j + dc) // 2 for j in js]
                o[par, :, dr:dr + PATCH, sft, ks[0]:ks[-1] + 1] = t[:, js, sft].transpose(2, 0, 1, 3)
        return o.reshape(KP, SHIFTS * NK, n)

    arr["wpatch"] = windowed(f["L0_tok_W"])
    arr["patch_gb"] = np.concatenate([windowed(f[k][:, None])[..., 0] for k in ("L0_tok_gamma", "L0_tok_beta")], 1)
    arr["tokens"] = f["x_txt"].reshape(B * NT)
    cw, sw, qw = f["L0_txt_color_W"], f["L0_txt_shape_W"], f["L0_txt_quantity_W"]
    t = np.arange(64)
    arr["table"] = np.concatenate([np.concatenate([cw[t // 16], sw[t % 16 // 4], qw[t % 4]], 1), f["L0_txt_special_W"]], 0)
    rep = lambda v: np.ascontiguousarray(np.broadcast_to(v, (128,) + v.shape))
    halved = lambda w: w.reshape(2, DH, -1).transpose(1, 0, 2)
    arr["tok_b"] = rep(f["L0_tok_b"])
    arr["wattn"] = np.concatenate([halved(f["L0_attn_Wqkv"]), halved(f["L0_attn_Wb1"])], 2)
    arr["lnwb"] = np.concatenate([f["L0_attn_ln_w"].reshape(2, DH).T, f["L0_attn_ln_b"].reshape(2, DH).T], 1)
    arr["bqk"] = f["L0_attn_bqkv"][0:4 * DH].reshape(4, DH).T
    arr["bv"] = rep(f["L0_attn_bqkv"][4 * DH:])
    arr["wb2"] = f["L0_attn_Wb2"]
    arr["temp"] = rep(f["L0_attn_temperature"])
    arr["wproj"] = halved(f["L0_attn_Wproj"])
    arr["mnwb"] = np.stack([np.tile(f["L0_attn_mn_w"], HH), np.tile(f["L0_attn_mn_b"], HH)], 1)
    arr["bproj"] = rep(f["L0_attn_bproj"])

    arr["gate_w"] = np.zeros((DH + 1, 2, NE + 1), np.float32)
    arr["gate_w"][0:DH] = halved(np.concatenate([f["L0_ffn_gate_w"], f["L0_ffn_v_w"][:, None]], 1))
    arr["gate_w"][DH, 1, 0:NE] = f["L0_ffn_gate_b"]
    arr["gate_w"][DH, 1, NE] = f["L0_ffn_v_b"]
    arr["w1"] = np.zeros((DH + 1, 2, NE * FF), np.float32)
    arr["w1"][0:DH] = f["L0_ffn_w1"].reshape(NE, 2, DH, FF).transpose(2, 1, 0, 3).reshape(DH, 2, NE * FF)
    arr["w1"][DH, 1] = f["L0_ffn_b1"].reshape(NE * FF)
    arr["w2"] = f["L0_ffn_w2"].reshape(NE, FC, 128, D).transpose(2, 1, 0, 3).reshape(128, FC, NE * D)
    arr["b2"] = rep(f["L0_ffn_b2"].reshape(NE * D))
    arr["spec"] = rep(np.stack([f["L0_ffn_out_w"][0], f["L0_ffn_out_w"][1], f["L0_ffn_out_b"], f["L0_ffn_bk_scale"]], 0))

    c = {}
    p = np.arange(128)
    pos = np.arange(NT, dtype=np.float32)[:, None]
    inv = np.exp(-(np.arange(0, D, 2, dtype=np.float32) / np.float32(D)) * np.float32(np.log(10000.0))).astype(np.float32)
    ang = pos * inv
    c["pe"] = np.stack([np.sin(ang), np.cos(ang)], -1).reshape(NT, D)
    c["ident"] = np.eye(128)
    c["causal"] = p[:, None] <= p[None, :]
    c["icausal"] = (p[:, None] % 64) <= np.arange(NI)[None, :]
    c["before"] = p[:, None] < p[None, :]
    c["blk"] = (p[:, None] // HD) == (np.arange(HH * VE)[None, :] // VE)
    c["hmask"] = (p[:, None] // HD) == np.arange(HH)[None, :]
    ones = np.ones((PDIM, 1), np.float32)
    mult = windowed(ones)[..., 0].reshape(KP, SHIFTS, NK).sum(1)
    c["mult"] = np.concatenate([mult, np.zeros((128 - KP, NK))], 0)
    c["iota8"] = np.tile(np.arange(NE), (128, 1))
    valid = np.array([[k % 3 < 2 or q % 64 < NI for k in range(SLOTS)] for q in range(128)])
    c["valid"] = valid
    image = np.array([k // 3 for k in range(SLOTS)])
    c["trash"] = np.concatenate([np.where(valid, 0, SROWS + (k * PAIRS + image[None, :]) * 128 + p[:, None]) for k in range(2)], 1)
    seq = np.array([[2 * (k // 3) + (k % 3 if k % 3 < 2 else q // 64) for k in range(SLOTS)] for q in range(128)])
    tok = np.array([[NI + q if k % 3 < 2 else q % 64 for k in range(SLOTS)] for q in range(128)])
    c["place"] = np.concatenate([np.where(valid, k * PLANE + seq * L + tok, 0) for k in range(2)], 1)
    c["tile8"] = np.tile(np.repeat(np.arange(TILES + 2), NE), (128, 1))
    c["tok"] = p[:, None]
    c["steps"] = np.tile(128 * np.arange(2 * SLOTS), (128, 1))
    c["fill"] = np.concatenate([np.zeros((128, 1)), 2 * PLANE + p[:, None], np.zeros((128, D))], 1)
    c["sign"] = np.tile(1 - 2 * (np.arange(GLEN) % 2), (128, 1))
    packed = np.zeros((128, NCONST), np.float32)
    for k, (lo, hi) in CW.items():
        packed[:, lo:hi] = c[k]
    arr["consts"] = packed
    return {k: np.ascontiguousarray(v) for k, v in arr.items()}


def kernel(**inputs):
    import numpy as _np
    import concourse.bacc as _bacc
    from concourse import mybir as _mybir
    from concourse.bass_utils import run_bass_kernel_spmd as _run

    nc = _bacc.Bacc("TRN2", target_bir_lowering=False, num_devices=1)
    arrays = {f"in_{k}_dram": v for k, v in laid_out(inputs).items()}
    args = {k[3:-5]: nc.dram_tensor(k, v.shape, _mybir.dt.from_np(v.dtype), kind="ExternalInput").ap()
            for k, v in arrays.items()}
    out = nc.dram_tensor("out_0_dram", (B, L, D), _mybir.dt.float32, kind="ExternalOutput").ap()
    early_fusion_block(nc, args, out)
    r = _run(nc, [arrays], core_ids=[0])
    return r.results[0]["out_0_dram"]
```

```python
import concourse.bass as bass
from concourse import mybir
from contextlib import ExitStack

B, CH, IMG, PATCH = 16, 3, 96, 16
SIDE = IMG // PATCH
NI = SIDE * SIDE
NT = 128
L = NI + NT
D = 192
DH = D // 2
NH, HD = 12, 16
HH = NH // 2
VE = HD + 1
RANK = 128
TW = D + RANK
NE, FF = 8, 768
FC = FF // 128
SHIFTS = 5
PDIM = PATCH * PATCH * CH * SHIFTS
WIN = PATCH + 2
KP = 2 * CH * WIN
NK = WIN // 2
PAIRS = B // 2
SLOTS = 3 * PAIRS
PC = 2 * L
PT = 128 * PAIRS
TILES = NE + (2 * B * L - NE) // 128
SROWS = TILES * 128
ROW = D + 2
PLANE = B * L
AHEAD = 4
UB = 9
DEPTH = 4
GFIRST = 48
GSTEP = 3
GTILES = (L - GFIRST) // (4 * GSTEP) * 4
GREST = L - GFIRST - GTILES * GSTEP
FSLOTS = SLOTS // (TILES - GTILES - 4)
assert FSLOTS * (TILES - GTILES - 4) == SLOTS
GLEN = L + 1
EPS = 1e-5

CW, NCONST = {}, 0
for _name, _n in (("pe", D), ("ident", 128), ("causal", 128), ("icausal", NI), ("before", 128), ("blk", HH * VE),
                  ("hmask", HH), ("mult", NK), ("iota8", NE), ("valid", SLOTS), ("trash", 2 * SLOTS),
                  ("place", 2 * SLOTS), ("tile8", (TILES + 2) * NE), ("tok", 1), ("steps", 2 * SLOTS), ("fill", ROW), ("sign", GLEN)):
    CW[_name] = (NCONST, NCONST + _n)
    NCONST += _n


class Chain:

    def __init__(self, eng, sem):
        self.eng, self.sem, self.base, self.k, self.i, self.per = eng, sem, 0, 0, None, 0

    def done(self, ins):
        ins.then_inc(self.sem, 1)
        self.k += 1

    def enter(self, per):
        self.base, self.k, self.i, self.per = self.base + self.k, 0, 0, per

    def leave(self, trips):
        assert self.k == self.per, (self.k, self.per)
        self.base, self.k, self.i = self.base + self.per * trips, 0, None

    def at(self, i):
        self.i = i

    def sync(self):
        value = self.base + self.k
        self.eng.wait_ge(self.sem, value if self.i is None else self.i * self.per + value)


def early_fusion_block(nc, a, out):
    F, BF = mybir.dt.float32, mybir.dt.bfloat16
    I32, U32 = mybir.dt.int32, mybir.dt.uint32
    ALU, ACT, AX = mybir.AluOpType, mybir.ActivationFunctionType, mybir.AxisListType
    ds = bass.ds

    sorted_rows = nc.dram_tensor("sorted_rows", (SROWS + 2 * PAIRS * 128, ROW), F, kind="Internal").ap()
    planes = nc.dram_tensor("planes", (2 * PLANE + 128, D), F, kind="Internal").ap()
    v_dram = nc.dram_tensor("v_dram", (B, L), F, kind="Internal").ap()
    g_dram = nc.dram_tensor("g_dram", (B, L, 2), F, kind="Internal").ap()

    ctx = ExitStack()
    with ctx:
        def sb(name, shape, dt=F):
            return ctx.enter_context(nc.sbuf_tensor(name, shape, dt))

        cst = sb("cst", [128, NCONST])

        def C(name, p=128):
            return cst[0:p, CW[name][0]:CW[name][1]]

        arena1 = sb("arena1", [128, NE * 2 * FF])
        xwin = arena1[0:KP, 0:NK * PT].rearrange("p (k n) -> p k n", k=NK)
        w1 = arena1[0:DH + 1, :].rearrange("p (h n) -> p h n", h=2)
        plane_in = arena1[:, 0:2 * SLOTS * D].rearrange("p (k s n) -> p k s n", k=2, n=D)
        arena2 = sb("arena2", [128, 4 * B * L])
        wpatch = arena2[0:KP, 0:SHIFTS * NK * D].rearrange("p (k n) -> p k n", n=D)
        qk = arena2[0:DH, :].rearrange("p (c n) -> p c n", c=4)
        w2 = arena2[:, 0:NE * FC * D].rearrange("p (f n) -> p f n", f=FC)
        rows = sb("rows", [128, 2, SLOTS, ROW])
        u = rows[:, 0, :, 2:ROW]
        p0 = rows[:, :, :, :].rearrange("p k s n -> p (k s n)")
        XS = NK * 128
        xsq = p0[0:KP, 0:2 * XS].rearrange("p (u k n) -> p u k n", u=2, k=NK)
        xss = p0[0:KP, 2 * XS + 2 * B * NT:2 * XS + 2 * B * NT + PT]
        tok_f = p0[0:70, 2 * XS:2 * XS + B * NT]
        tokneg = p0[0:70, 2 * XS + B * NT:2 * XS + 2 * B * NT]

        h = sb("h", [128, SLOTS, D])
        vx = sb("vx", [128, SLOTS, NH, HD])
        vflat = vx[:, :, :, :].rearrange("p s h e -> p (s h e)")
        usq = vx[:, :, :, :].rearrange("p s h e -> p s (h e)")
        tok_i = vflat[0:70, 0:B * NT].bitcast(I32)

        used = {}

        def carve(phase, p, n, start=0):
            at = used.get(phase, start)
            used[phase] = at + n
            assert at + n <= NE * 2 * FF, (phase, at + n)
            return arena1[0:p, at:at + n]

        weff = carve("patch", KP, NK * (D + 1), NK * PT).rearrange("p (k n) -> p k n", k=NK)
        gb = carve("patch", KP, 2 * SHIFTS * NK)
        gsum = carve("patch", 128, D)
        tokb = carve("patch", 128, D)
        tb = carve("patch", 128, D)
        table = carve("patch", 70, D)
        istat = carve("patch", 128, 8 * PAIRS).rearrange("p (k g) -> p k g", k=8)

        xn = carve("attn", 128, 6 * D).rearrange("p (u s n) -> p u s n", u=2, s=3)
        xnT = carve("attn", DH, 4 * PC).rearrange("p (u h n) -> p u h n", u=2, h=2)
        ek = carve("attn", DH, 2 * PC).rearrange("p (u n) -> p u n", u=2)
        rk = carve("attn", DH, 2 * PC).rearrange("p (u n) -> p u n", u=2)
        th = carve("attn", 128, 2 * RANK).rearrange("p (u n) -> p u n", u=2)
        sg = carve("attn", 128, 2 * RANK).rearrange("p (u n) -> p u n", u=2)
        sgT = carve("attn", 128, 256).rearrange("p (u n) -> p u n", u=2)
        ximg = carve("attn", DH, 4 * 128).rearrange("p (u h n) -> p u h n", u=2, h=2)
        kimg = carve("attn", DH, 4 * 128).rearrange("p (u h n) -> p u h n", u=2, h=2)
        kst = carve("attn", DH, 4 * PC).rearrange("p (u h n) -> p u h n", u=2, h=2)
        qst = carve("attn", DH, 4 * PC).rearrange("p (u h n) -> p u h n", u=2, h=2)
        qbd = carve("attn", DH, 2 * HH * PC).rearrange("p (u h n) -> p u h n", u=2, h=HH)
        used["attn2"] = 0
        sm = carve("attn2", 128, 2 * 384).rearrange("p (u n) -> p u n", u=2)
        si = carve("attn2", 128, NH * NI + 64)
        kft = carve("attn2", 128, D)
        sbd = carve("attn2", DH, 4 * HH * VE).rearrange("p (b h n) -> p b h n", b=2, h=2)
        vst = carve("attn2", 128, 6 * NH * VE).rearrange("p (u s h e) -> p u s h e", u=2, s=3, h=NH)
        vr = carve("attn2", 128, 2 * NH * VE).rearrange("p (u e) -> p u e", e=VE)
        osum = carve("attn2", 128, 2 * NH * VE).rearrange("p (u e) -> p u e", e=VE)
        assert used["attn2"] <= 6 * D + 8 * PC + 6 * RANK + 512

        ones = sb("ones", [128, 128])
        eps_t = sb("eps_t", [128, 1])
        st = sb("st", [128, SLOTS, 6])
        mv = sb("mv", [128, SLOTS, 2])
        ln = sb("ln", [128, 6, SLOTS])
        place_a = sb("place_a", [128, SLOTS * NH * 10])
        place_b = sb("place_b", [128, 2 * (4 * DH + TW)])
        place_c = sb("place_c", [128, 2 * (4 * DH + TW)])

        def within(place, start, p, n):
            assert start + n <= place.shape[1]
            return place[0:p, start:start + n]

        wraw = within(place_b, 0, DH, 2 * (4 * DH + TW)).rearrange("p (h n) -> p h n", h=2)
        wqk = within(place_c, 0, DH, 8 * DH).rearrange("p (h n) -> p h n", h=2)
        wtok = within(place_c, 8 * DH, DH, 2 * TW).rearrange("p (h n) -> p h n", h=2)
        second = rows[:, 1, :, :].rearrange("p s n -> p (s n)")
        smp = second[:, 0:DEPTH * 3 * 192].bitcast(BF).rearrange("p (k u n) -> p k u n", k=3, u=DEPTH)
        sr = second[:, DEPTH * 3 * 192:DEPTH * (3 * 192 + 384)].rearrange("p (u n) -> p u n", u=DEPTH)
        vp = within(place_b, 0, 128, 2 * 2 * NH * 3 * VE // 2).bitcast(BF).rearrange("p (w u q e) -> p w u q e", w=2, q=3, e=VE)
        lnwb = sb("lnwb", [DH, 4])
        bqk0 = sb("bqk0", [DH, 4])
        bqk = sb("bqk", [DH, 4])
        bv0 = sb("bv0", [128, D])
        bv = sb("bv", [128, D])
        wb2 = sb("wb2", [RANK, 5 * NH])
        temp = sb("temp", [128, 2])
        wp_raw = sb("wp_raw", [DH, 2, D])
        wp = sb("wp", [DH + 1, 2, D])
        mnwb = sb("mnwb", [DH, 2])
        bproj = sb("bproj", [128, D])
        gw = sb("gw", [DH + 1, 2, NE + 1])
        par = within(place_a, 0, 128, SLOTS * NH * 5).rearrange("p (s n) -> p s n", s=SLOTS)
        gt = within(place_a, SLOTS * NH * 5, 128, SLOTS * NH * 5).rearrange("p (k n) -> p k n", k=5)
        rden = sb("rden", [128, 3, NH])
        lnr = sb("lnr", [128, 3, SLOTS * NH])
        vat = [0]

        def carve_v(p, n):
            vat[0] += n
            assert vat[0] <= SLOTS * D
            return vflat[0:p, vat[0] - n:vat[0]]

        uh = carve_v(128, 6 * D).rearrange("p (u s n) -> p u s n", u=2, s=3)
        x2 = carve_v(128, 6 * D).rearrange("p (u s n) -> p u s n", u=2, s=3)
        oT = carve_v(DH + 1, 512).rearrange("p (u n) -> p u n", u=2)
        x2T = carve_v(DH + 1, 512).rearrange("p (u n) -> p u n", u=2)
        vat[0] = 0
        hid = carve_v(128, 2 * FF).rearrange("p (u n) -> p u n", u=2)
        hT = carve_v(128, 2 * FF).rearrange("p (u n) -> p u n", u=2)
        xgT = carve_v(DH + 1, 512).rearrange("p (u n) -> p u n", u=2)
        b2b = within(place_a, 0, 128, NE * D)
        xg = rows[:, 0, 0:AHEAD, :]
        y1 = within(place_a, NE * D, 128, 2 * D).rearrange("p (u n) -> p u n", u=2)
        y2 = within(place_a, NE * D + 2 * D, 128, 2 * D).rearrange("p (u n) -> p u n", u=2)
        meta_w = sb("meta_w", [128, 4])
        meta_i = sb("meta_i", [128, 4], I32)
        spec = sb("spec", [128, 4, D])
        tail2 = NE * FC * D
        lg = within(arena2, tail2, 128, SLOTS * (NE + 1)).rearrange("p (s n) -> p s n", s=SLOTS)
        m8 = within(arena2, tail2 + SLOTS * 9, 128, SLOTS * 8).rearrange("p (s n) -> p s n", s=SLOTS)
        ix = within(arena2, tail2 + SLOTS * 17, 128, SLOTS * 8).bitcast(U32).rearrange("p (s n) -> p s n", s=SLOTS)
        ixf = sb("ixf", [128, 2, SLOTS])
        wk = sb("wk", [128, 2, SLOTS])
        beforeb = sb("beforeb", [128, 128], BF)
        onesb = sb("onesb", [128, 128], BF)
        ohf = within(place_b, 0, 128, 2 * SLOTS * NE).rearrange("p (s e) -> p s e", e=NE)
        ohb = sb("ohb", [128, 2 * SLOTS, NE], BF)
        tot = within(place_b, 2 * SLOTS * NE, 128, 2 * SLOTS * NE).rearrange("p (e s) -> p e s", e=NE)
        inc = within(place_b, 4 * SLOTS * NE, 128, 2 * SLOTS * NE).rearrange("p (e s) -> p e s", e=NE)
        cnt = sb("cnt", [128, 4, NE])
        pos = sb("pos", [128, 2 * SLOTS])
        sidx = sb("sidx", [128, 2 * SLOTS], I32)
        ecmp = within(place_c, 0, 1, (TILES + 2) * NE).rearrange("p (t e) -> p t e", e=NE)
        eidf = sb("eidf", [1, TILES + 2])
        eid = sb("eid", [1, TILES + 2], I32)
        vtok = sb("vtok", [128, SLOTS])
        ga = within(place_c, 0, 32, 2 * GLEN).rearrange("p (t c) -> p t c", c=2)
        gs = within(place_c, 2 * GLEN, 32, 2 * GLEN).rearrange("p (t c) -> p t c", c=2)
        ge = within(place_c, 4 * GLEN, B, 2 * L).rearrange("p (t c) -> p t c", c=2)
        vv = within(place_c, 4 * GLEN + 2 * L, 32, L)
        gq = sb("gq", [32, 4])
        gg = within(place_b, 0, B, 4 * L).rearrange("p (k n) -> p k n", k=4)
        g2 = within(place_b, 4 * L, B, 2 * L).rearrange("p (n k) -> p n k", k=2)
        pool_turn = sb("pool_turn", [1, TILES])
        gtok = sb("gtok", [128, SLOTS, 2])

        bank = [ctx.enter_context(nc.psum_tensor(f"bank{n}", [128, 512], F)) for n in range(8)]
        pbank = [bank[0], bank[1], bank[2], bank[5]]

        class Sems(dict):
            def __missing__(self, name):
                self[name] = ctx.enter_context(nc.semaphore(name))
                return self[name]

        s = Sems()
        ctx.enter_context(nc.allow_non_contiguous_dma(reason="one value of every token"))
        block = ctx.enter_context(nc.Block())
        SMALL = 14
        GROUPS = ((0, PAIRS - 2), (PAIRS - 2, PAIRS))

        @block.sync
        def _(sp):
            sp.dma_start(cst[:, :], a["consts"]).then_inc(s["constants_in"], 16)
            sp.dma_start(tok_i, a["tokens"].partition_broadcast(70)).then_inc(s["tokens_in"], 16)
            sp.wait_ge(s["small_in"], 16 * SMALL)
            for q in range(SHIFTS):
                sp.dma_start(wpatch[:, NK * q:NK * (q + 1), :],
                             a["wpatch"][:, NK * q:NK * (q + 1), :]).then_inc(s[f"patch_weights_in{q}"], 16)
            sp.dma_start(xwin, a["xwin"]).then_inc(s["windows_in"], 16)
            sp.wait_ge(s["constants_in"], 16)
            sp.wait_ge(s["windows_in"], 16)
            sp.dma_start(sorted_rows[0:SROWS + 128 * AHEAD].rearrange("(t p) n -> p t n", p=128),
                         C("fill").unsqueeze(1).to_broadcast([128, TILES + AHEAD, ROW])).then_inc(s["list_filled"], 16)
            sp.wait_ge(s["out_taken"], 1 + PAIRS)
            sp.dma_start(w1, a["w1"]).then_inc(s["w1_in"], 16)
            sp.dma_start(w2, a["w2"]).then_inc(s["w2_in"], 16)
            sp.dma_start(b2b, a["b2"]).then_inc(s["b2_in"], 16)
            sp.wait_ge(s["v_ready"], 1)
            vt = vtok[:, :].rearrange("p (i k) -> p k i", k=3)
            vd = v_dram.rearrange("(i b) l -> b l i", b=2)
            for b in range(2):
                sp.dma_start(vd[b, NI:L], vt[:, b]).then_inc(s["v_out"], 16)
                sp.dma_start(vd[b, 0:NI], vt[64 * b:64 * b + NI, 2]).then_inc(s["v_out"], 16)
            sp.wait_ge(s["v_out"], 64)
            sp.dma_start(vv[0:B, :], v_dram).then_inc(s["v_in"], 16)
            sp.dma_start(vv[B:2 * B, :], v_dram[:, ::-1]).then_inc(s["v_in"], 16)

            sp.wait_ge(s["list_written"], 16 * 2 * SLOTS)
            for t in range(AHEAD):
                sp.dma_start(xg[:, t, :], sorted_rows[128 * t:128 * (t + 1)]).then_inc(s[f"xg_in{t}"], 16)

            def load_tile(t, w):
                sp.wait_ge(s["xgT_taken"], t + 1)
                sp.dma_start(xg[:, w, :], sorted_rows[ds(128 * (t + AHEAD), 128), :]).then_inc(s[f"xg_in{w}"], 16)

            with sp.Fori(0, GTILES // 4) as it:
                for j in range(4):
                    load_tile(it * 4 + j, j)
            load_tile(GTILES, 0)
            load_tile(GTILES + 1, 1)
            sp.wait_ge(s["recurrence_done"], 1)
            sp.dma_start(ge[:, :, :], gs[B:2 * B, 0:L, :]).then_inc(s["ge_in"], 16)
            load_tile(GTILES + 2, 2)
            sp.wait_ge(s["green_ready"], 1)
            sp.dma_start(g_dram, g2[:, :, :]).then_inc(s["g_out"], 16)
            load_tile(GTILES + 3, 3)
            sp.wait_ge(s["g_out"], 16)
            gd = g_dram.rearrange("(i b) l c -> b l i c", b=2)
            gv = gtok[:, :, :].rearrange("p (i k) c -> p k i c", k=3)
            for b in range(2):
                sp.dma_start(gv[:, b], gd[b, NI:L]).then_inc(s["gtok_in"], 16)
                sp.dma_start(gv[64 * b:64 * b + NI, 2], gd[b, 0:NI]).then_inc(s["gtok_in"], 16)
            with sp.Fori(GTILES // 4 + 1, TILES // 4) as it:
                for j in range(4):
                    load_tile(it * 4 + j, j)
            sp.wait_ge(s["l1_psum"], 2 + TILES + 1)
            for k in range(2):
                sp.wait_ge(s[f"plane_written{k}"], 8 * TILES)
            pd = planes[0:2 * PLANE].rearrange("(k i b l) n -> k b l i n", k=2, b=2, l=L)
            pv_ = plane_in.rearrange("p k (i j) n -> p k j i n", j=3)
            for n in (3, 0, 1, 2):
                for k in range(2):
                    if n < 2:
                        sp.dma_start(pv_[:, k, n], pd[k, n, NI:L]).then_inc(s[f"plane_in{n}"], 16)
                    else:
                        lo = 64 * (n - 2)
                        sp.dma_start(pv_[lo:lo + NI, k, 2], pd[k, n - 2, 0:NI]).then_inc(s[f"plane_in{n}"], 16)
            od = out.rearrange("(i b) l n -> b l i n", b=2)
            hv = h[:, :, :].rearrange("p (i j) n -> p j i n", j=3)
            for n in range(4):
                if n < 3:
                    sp.wait_ge(s["total_ready"], n + 1)
                else:
                    sp.wait_ge(s["last_total"], 1)
                if n < 2:
                    sp.dma_start(od[n, NI:L], hv[:, n]).then_inc(s["out_written"], 16)
                else:
                    lo = 64 * (n - 2)
                    sp.dma_start(od[n - 2, 0:NI], hv[lo:lo + NI, 2]).then_inc(s["out_written"], 16)
            sp.wait_ge(s["out_written"], 64)

        @block.gpsimd
        def _(pool):
            nc.gpsimd.memset(ones[:, :], 1.0)
            nc.gpsimd.memset(eps_t[:, :], EPS).then_inc(s["filled"], 1)
            P = nc.gpsimd
            pool.wait_ge(s["constants_in"], 16)
            for g in range(PAIRS):
                pool.wait_ge(s["squares_ready"], g + 1)
                P.tensor_tensor(xsq[:, g % 2], xsq[:, g % 2], C("mult", KP).unsqueeze(2).to_broadcast([KP, NK, 128]),
                                ALU.mult).then_inc(s["squares_weighted"], 1)
            pool.sem_inc(s["low_ready"], DEPTH)

            def value_rest(i, w):
                pool.wait_ge(s["value_high_ready"], i + 1)
                P.tensor_tensor(vr[:, :, :], vst[:, w, 0:2].rearrange("p s h e -> p (s h) e"), vp[:, w, :, 0, :],
                                ALU.subtract).then_inc(s["value_rest_ready"], 1)

            def value_low(i, w):
                pool.wait_ge(s["value_middle_ready"], i + 1)
                P.tensor_tensor(vp[:, w, :, 2, :], vr[:, :, :], vp[:, w, :, 1, :], ALU.subtract).then_inc(s["value_parts_ready"], 1)

            def low_parts(i, w, final=False):
                for t in range(8):
                    pool.wait_ge(s["middle_ready"], 8 * i + t + 1)
                    P.tensor_tensor(smp[:, 2, t % DEPTH], sr[:, t % DEPTH], smp[:, 1, t % DEPTH], ALU.subtract).then_inc(s["low_ready"], 1)
                    if not final:
                        if t == 5:
                            value_rest(i + 1, 1 - w)
                        if t == 6:
                            value_low(i + 1, 1 - w)

            value_rest(0, 0)
            value_low(0, 0)
            with pool.Fori(0, PAIRS // 2 - 1) as it:
                low_parts(it * 2, 0)
                low_parts(it * 2 + 1, 1)
            low_parts(PAIRS - 2, 0)
            low_parts(PAIRS - 1, 1, final=True)
            pool.sem_inc(s["first_copied"], 2)
            with pool.Fori(0, PAIRS // 2) as it:
                for w in range(2):
                    i = it * 2 + w
                    pool.wait_ge(s["x2_ready"], i + 1)
                    P.tensor_copy(rows[:, 0, ds(3 * i, 3), 2:ROW], x2[:, w]).then_inc(s["first_copied"], 1)
            pool.wait_ge(s["first_copied"], 2 + PAIRS)
            pool.wait_ge(s["list_filled"], 16)
            pool.wait_ge(s["places_ready"], 1)
            for k in range(2):
                for n in range(SLOTS):
                    pool.indirect_dma_start(out=sorted_rows,
                                            out_offset=bass.IndirectOffsetOnAxis(ap=sidx[:, k * SLOTS + n:k * SLOTS + n + 1].bitcast(U32), axis=0),
                                            in_=rows[:, k, n, :], in_offset=None).then_inc(s["list_written"], 16)
            pool.sem_inc(s["turn_taken"], 1)

            def write_tiles(it, first):
                for j in range(4):
                    t = it * 4 + j
                    pool.wait_ge(s["y2_ready"], 2 + t + 1)
                    if not (first and j == 0):
                        pool.wait_ge(s[f"plane_written{(j + 1) % 2}"], 32 * it + 16 * ((j + 1) // 2))
                    P.tensor_copy(pool_turn[:, ds(t, 1)], eps_t[0:1, :]).then_inc(s["turn_taken"], 1)
                    pool.indirect_dma_start(out=planes,
                                            out_offset=bass.IndirectOffsetOnAxis(ap=meta_i[:, j:j + 1].bitcast(U32), axis=0),
                                            in_=y2[:, j % 2, :], in_offset=None).then_inc(s[f"plane_written{j % 2}"], 16)

            write_tiles(0, True)
            with pool.Fori(1, TILES // 4) as it:
                write_tiles(it, False)
            lo, hi = 64, 64 + NI
            odd_images = h[:, :, :].rearrange("p (i j) n -> p j i n", j=3)[lo:hi, 2]
            pin = plane_in.rearrange("p k (i j) n -> p k j i n", j=3)[lo:hi, :, 2]
            pool.wait_ge(s["features_added"], 1)
            pool.wait_ge(s["plane_in3"], 32)
            P.tensor_tensor(odd_images, odd_images, pin[:, 0], ALU.add).then_inc(s["first_added"], 1)
            pool.wait_ge(s["first_added"], 1)
            P.tensor_tensor(odd_images, odd_images, pin[:, 1], ALU.add).then_inc(s["last_total"], 1)

        @block.scalar
        def _(act):
            for dst, src in ((gb, "patch_gb"), (table, "table"), (tb, "tok_b"), (wraw[:, :, :], "wattn"),
                             (lnwb[:, :], "lnwb"), (bqk0[:, :], "bqk"), (bv0[:, :], "bv"), (wb2[:, :], "wb2"),
                             (wp_raw[:, :, :], "wproj"), (mnwb[:, :], "mnwb"), (bproj[:, :], "bproj"),
                             (temp[:, 0:1], "temp"), (gw[:, :, :], "gate_w"),
                             (spec[:, :, :], "spec")):
                act.dma_start(dst, a[src]).then_inc(s["small_in"], 16)
            act.wait_ge(s["windows_in"], 16)
            act.wait_ge(s["onehot_ready"], 1)
            for g in range(PAIRS):
                if g >= 2:
                    act.wait_ge(s["squares_folded"], g - 1)
                nc.scalar.activation(xsq[:, g % 2], xwin[:, :, 128 * g:128 * (g + 1)], ACT.Square).then_inc(s["squares_ready"], 1)
            act.wait_ge(s["filled"], 1)
            for n, (g0, g1) in enumerate(GROUPS):
                act.wait_ge(s["ivar_ready"], n + 1)
                nc.scalar.activation(istat[:, 4, g0:g1], istat[:, 3, g0:g1], ACT.Sqrt, bias=eps_t[:, :]).then_inc(s["isd_ready"], 1)
            act.wait_ge(s["stats_ready"], len(GROUPS))
            nc.scalar.activation(ln[:, 0, :], mv[:, :, 1], ACT.Sqrt, bias=eps_t[:, :]).then_inc(s["sd_ready"], 1)
            act.wait_ge(s["varx_ready"], 1)
            nc.scalar.activation(ln[:, 3, :], ln[:, 2, :], ACT.Sqrt, bias=eps_t[:, :]).then_inc(s["sd_ready"], 1)

            A = nc.scalar
            act.sem_inc(s["xnT_taken"], 2)
            act.sem_inc(s["qk_taken"], 2)
            act.sem_inc(s["th_ready"], 2)
            act.sem_inc(s["sgT_taken"], 1)
            act.wait_ge(s["ln_ready"], 1)
            act.wait_ge(s["attn_weights_ready"], 1)

            def rows_take(i, w, k):
                n, b = 3 * i + k, (w + k) % 2
                act.wait_ge(s["xnT_psum"], 6 + n + 1)
                if k == 0:
                    act.wait_ge(s["tok_psum"], 3 * i + 3)
                    act.wait_ge(s["qk_done"], 4 * i + 2)
                src = bank[b][0:DH, 0:256].rearrange("p (h n) -> p h n", h=2)
                if k < 2:
                    A.activation(xnT[:, w, :, k * L + NI:(k + 1) * L], src, ACT.Copy).then_inc(s["xnT_taken"], 1)
                else:
                    A.activation(ximg[:, w], src, ACT.Copy)
                    for f in range(2):
                        last = A.activation(xnT[:, w, f, :].rearrange("p (b n) -> p b n", b=2)[:, :, 0:NI],
                                            src[:, f, :].rearrange("p (b n) -> p b n", b=2)[:, :, 0:NI], ACT.Copy)
                    last.then_inc(s["xnT_taken"], 1)

            def take_products(i, w, final=False):
                for k in range(3):
                    n, b = 3 * i + k, (w + k) % 2
                    act.wait_ge(s["tok_psum"], 6 + n + 1)
                    act.wait_ge(s["tok_taken"], n + 1)
                    A.activation(th[:, b, :], bank[4 + b][:, D:TW], ACT.Tanh,
                                 scale=ln[:, 5, ds(n, 1)]).then_inc(s["th_ready"], 1)
                for c in range(4):
                    m = 4 * i + c
                    act.wait_ge(s["qk_psum"], m + 1)
                    act.wait_ge(s["qk_done"], 4 + m + 1)
                    A.activation(ek[:, c % 2, :], bank[2 + c % 2][0:DH, 0:PC], ACT.Exp, bias=bqk[:, c:c + 1])
                    A.activation(rk[:, c % 2, :], bank[2 + c % 2][0:DH, 0:PC], ACT.Relu,
                                 bias=bqk[:, c:c + 1]).then_inc(s["qk_taken"], 1)
                    if c < 3:
                        n = 3 * i + c
                        act.wait_ge(s["sgT_psum"], 2 + n + 1)
                        act.wait_ge(s["par_psum"], n + 1)
                        A.activation(sgT[:, (w + c) % 2, :], bank[6][:, 0:128], ACT.Copy).then_inc(s["sgT_taken"], 1)
                        if not final:
                            rows_take(i + 1, 1 - w, c)

            for k in range(3):
                rows_take(0, 0, k)
            with act.Fori(0, PAIRS // 2 - 1) as it:
                take_products(it * 2, 0)
                take_products(it * 2 + 1, 1)
            take_products(PAIRS - 2, 0)
            take_products(PAIRS - 1, 1, final=True)

            act.wait_ge(s["par_taken"], 1 + SLOTS)
            pv = par[:, :, :].rearrange("p s (h k) -> p (s h) k", k=5)
            for k in range(4):
                last = A.activation(gt[:, k, :], pv[:, :, k], ACT.Tanh, scale=0.5 if k % 2 == 0 else 1.0)
            last.then_inc(s["gate_tanh"], 1)
            act.wait_ge(s["phase_ready"], 1)
            HALF_PI = 1.5707962
            A.activation(gt[:, 3, :], gt[:, 1, :], ACT.Sin, scale=HALF_PI).then_inc(s["sin_ready"], 1)
            act.wait_ge(s["inter_ready"], 1)
            A.activation(gt[:, 1, :], gt[:, 0, :], ACT.Tanh, scale=0.25).then_inc(s["inter_tanh"], 1)
            act.wait_ge(s["inter_tanh"], 1)
            A.activation(gt[:, 2, :], gt[:, 1, :], ACT.Tanh, scale=temp[:, 1:2]).then_inc(s["gate_ready"], 1)

            act.sem_inc(s["kft_taken"], 1)
            act.sem_inc(s["high_ready"], 2)
            act.wait_ge(s["qk_done"], 6 + 4 * PAIRS)

            def stage_keys(i, w):
                act.wait_ge(s["out_psum"], i + 1)
                src = qk[:, :, ds(i * PC, PC)]
                A.activation(kst[:, w], src[:, 2:4, :], ACT.Copy)
                for f in range(2):
                    A.activation(kimg[:, w, f, :].rearrange("p (b n) -> p b n", b=2),
                                 src[:, 2 + f, :].rearrange("p (b n) -> p b n", b=2)[:, :, 0:64], ACT.Copy)

            def stage_queries(i, w):
                A.activation(qst[:, w], qk[:, 0:2, ds(i * PC, PC)], ACT.Copy).then_inc(s["staged"], 1)

            def squares(i):
                act.wait_ge(s["uc_ready"], i + 1)
                A.activation(usq[:, ds(3 * i, 3), :], u[:, ds(3 * i, 3), :], ACT.Square).then_inc(s["usq_ready"], 1)

            def head_deviations(i0, i1):
                act.wait_ge(s["hvar_ready"], 1 if i0 == 0 else 2)
                A.activation(lnr[:, 2, 3 * NH * i0:3 * NH * i1], lnr[:, 1, 3 * NH * i0:3 * NH * i1], ACT.Sqrt, scale=1.0 / HD,
                             bias=eps_t[:, :]).then_inc(s["hsd_ready"], 1)

            def score_high(i, t):
                act.wait_ge(s["scores_taken"], 2 + 8 * i + t + 1)
                act.wait_ge(s["text_out_done"], 8 * i + t + 1)
                A.activation(smp[:, 0, t % DEPTH], sm[:, t % 2], ACT.Copy).then_inc(s["high_ready"], 1)

            def score_middle(i, t):
                act.wait_ge(s["rest_ready"], 2 + 8 * i + t + 1)
                A.activation(smp[:, 1, t % DEPTH], sr[:, t % DEPTH], ACT.Copy).then_inc(s["middle_ready"], 1)

            def value_high(i, w):
                act.wait_ge(s["vg_ready"], i + 1)
                A.activation(vp[:, w, :, 0, :], vst[:, w, 0:2].rearrange("p s h e -> p (s h) e"), ACT.Copy).then_inc(s["value_high_ready"], 1)

            def value_middle(i, w):
                act.wait_ge(s["value_rest_ready"], i + 1)
                A.activation(vp[:, w, :, 1, :], vr[:, :, :], ACT.Copy).then_inc(s["value_middle_ready"], 1)

            def attention_copies(i, w, first=False, final=False):
                act.wait_ge(s["kft_psum"], i + 1)
                act.wait_ge(s["state_psum"], i + 1)
                A.activation(kft, bank[6][:, 0:D], ACT.Copy).then_inc(s["kft_taken"], 1)
                score_high(i, 0)
                for t in range(8):
                    if t < 7:
                        score_high(i, t + 1)
                    score_middle(i, t)
                    if t == 2 and not first:
                        squares(i - 1)
                    if not final:
                        if t == 1:
                            stage_keys(i + 1, 1 - w)
                        if t == 3:
                            stage_queries(i + 1, 1 - w)
                        if t == 5:
                            value_high(i + 1, 1 - w)
                        if t == 6:
                            value_middle(i + 1, 1 - w)

            stage_keys(0, 0)
            stage_queries(0, 0)
            value_high(0, 0)
            value_middle(0, 0)
            attention_copies(0, 0, first=True)
            with act.Fori(0, PAIRS // 2 - 1) as it:
                attention_copies(it * 2 + 1, 1)
                attention_copies(it * 2 + 2, 0)
            attention_copies(PAIRS - 1, 1, final=True)
            head_deviations(0, PAIRS - 1)
            squares(PAIRS - 1)

            head_deviations(PAIRS - 1, PAIRS)
            act.sem_inc(s["uhT_taken"], 2)
            act.sem_inc(s["x2T_taken"], 2)
            act.sem_inc(s["second_copied"], 2)
            for psum, taken, used, dst in (("uhT_psum", "uhT_taken", "proj_psum", oT), ("x2T_psum", "x2T_taken", "logit_psum", x2T)):
                if dst is x2T:
                    act.wait_ge(s["means2_ready"], 1)
                    A.activation(ln[:, 0, :], mv[:, :, 1], ACT.Sqrt, bias=eps_t[:, :]).then_inc(s["sd2_ready"], 1)
                with act.Fori(0, PAIRS // 2) as it:
                    for j in range(6):
                        n = it * 6 + j
                        act.wait_ge(s[psum], 6 + n + 1)
                        act.wait_ge(s[used], n + 1)
                        A.activation(dst[0:DH, j % 2, :], bank[j % 2][0:DH, 0:256], ACT.Copy).then_inc(s[taken], 1)
                        if dst is x2T and j % 3 == 2:
                            i = it * 2 + j // 3
                            A.activation(rows[:, 1, ds(3 * i, 3), 2:ROW], x2[:, j // 3], ACT.Copy).then_inc(s["second_copied"], 1)
            act.wait_ge(s["gap_ready"], 1)
            A.activation(wk[:, 1, :], wk[:, 0, :], ACT.Exp).then_inc(s["ratio_ready"], 1)

            act.sem_inc(s["hid_ready"], 2)
            act.sem_inc(s["y2_ready"], 2)

            def gelu(t, w):
                for f in range(2):
                    act.wait_ge(s["l1_psum"], 2 + t + 1)
                    act.wait_ge(s["hT_psum"], t + 1)
                    ins = A.activation(hid[:, w, 384 * f:384 * (f + 1)], bank[1 + 2 * w + f][:, 0:384], ACT.Gelu_apprx_tanh)
                ins.then_inc(s["hid_ready"], 1)

            gelu(0, 0)
            with act.Fori(0, TILES // 4) as it:
                for j in range(4):
                    t = it * 4 + j
                    gelu(t + 1, (j + 1) % 2)
                    act.wait_ge(s["y1_ready"], 1 + t + 1)
                    act.wait_ge(s["turn_taken"], t + 1)
                    A.activation(y2[:, j % 2, :], y1[:, j % 2, :], ACT.Copy, scale=meta_w[:, j:j + 1]).then_inc(s["y2_ready"], 1)

        @block.tensor
        def _(pe):
            def keep_clock(at, count):
                for _ in range(count):
                    nc.tensor.matmul(at[:, 0:384], ones[:, :], cst[:, 0:384], start=True, stop=True)

            pe.wait_ge(s["constants_in"], 16)
            pe.wait_ge(s["small_in"], 16 * SMALL)
            pe.wait_ge(s["filled"], 1)
            for c in range(4):
                for f in range(2):
                    last = nc.tensor.matmul(bank[3][0:DH, 100 + c:101 + c], wraw[:, f, DH * c:DH * (c + 1)],
                                            lnwb[:, 2 + f:3 + f], start=f == 0, stop=f == 1)
            for f in range(2):
                last = nc.tensor.matmul(bank[7][:, D:2 * D], lnwb[:, 2 + f:3 + f].to_broadcast([DH, 128]),
                                        wraw[:, f, 4 * DH:4 * DH + D], start=f == 0, stop=f == 1)
            for f in range(2):
                last = nc.tensor.matmul(bank[7][:, 0:D], mnwb[:, 1:2].to_broadcast([DH, 128]), wp_raw[:, f, :],
                                        start=f == 0, stop=f == 1)
            last.then_inc(s["attn_bias_sums"], 1)
            for c in range(SHIFTS * NK):
                if c % NK == 0:
                    pe.wait_ge(s[f"patch_weights_in{c // NK}"], 16)
                last = nc.tensor.matmul(bank[6][:, 0:D], gb[:, SHIFTS * NK + c:SHIFTS * NK + c + 1].to_broadcast([KP, 128]),
                                        wpatch[:, c, :], start=c == 0, stop=c == SHIFTS * NK - 1)
                if c % NK == NK - 1:
                    last.then_inc(s["beta_sums"], 1)
            keep_clock(bank[0], 12)
            pe.wait_ge(s["onehot_ready"], 1)
            for b in range(B):
                if b >= 2:
                    pe.wait_ge(s["text_taken"], b - 1)
                nc.tensor.matmul(bank[4 + b % 2][:, 0:D], tok_f[:, NT * b:NT * (b + 1)], table, start=True,
                                 stop=True).then_inc(s["text_psum"], 1)
            pe.wait_ge(s["weff_ready"], 1)
            for k in range(NK):
                last = nc.tensor.matmul(bank[7][:, 0:D], ones[0:KP, :], weff[:, k, 0:D], start=k == 0, stop=k == NK - 1)
            last.then_inc(s["gain_sums"], 1)
            pe.wait_ge(s["windows_in"], 16)
            for g in range(PAIRS):
                if g == PAIRS - 2:
                    pe.wait_ge(s["text_taken"], B)
                    pe.wait_ge(s["squares_folded"], PAIRS)
                    for m in range(PAIRS):
                        last = nc.tensor.matmul(bank[3][:, m:m + 1], xss[:, 128 * m:128 * (m + 1)], ones[0:KP, 0:1],
                                                start=True, stop=True)
                    last.then_inc(s["square_sums"], 1)
                for k in range(NK):
                    last = nc.tensor.matmul(pbank[g // 2][:, (D + 1) * (g % 2):(D + 1) * (g % 2 + 1)],
                                            xwin[:, k, 128 * g:128 * (g + 1)], weff[:, k, :], start=k == 0, stop=k == NK - 1)
                last.then_inc(s["patch_sums"], 1)

            pe.sem_inc(s["xnT_psum"], 6)
            pe.sem_inc(s["tok_psum"], 6)
            pe.sem_inc(s["sgT_psum"], 2)
            pe.sem_inc(s["par_psum"], 2)
            keep_clock(bank[6], 10)

            def row_transpose(i, w, k):
                n, b = 3 * i + k, (w + k) % 2
                pe.wait_ge(s["xn_ready"], n + 1)
                pe.wait_ge(s["xnT_taken"], n + 1)
                for f in range(2):
                    last = nc.tensor.transpose(bank[b][0:DH, 128 * f:128 * (f + 1)],
                                               xn[:, w, k, DH * f:DH * (f + 1)], C("ident"))
                last.then_inc(s["xnT_psum"], 1)

            def products(i, w, final=False):
                def token_product(k):
                    n, b = 3 * i + k, 4 + (w + k) % 2
                    pe.wait_ge(s["xnT_taken"], 2 + n + 1)
                    pe.wait_ge(s["tok_taken"], n + 1)
                    for f in range(2):
                        lhsT = xnT[:, w, f, k * L + NI:(k + 1) * L] if k < 2 else ximg[:, w, f, :]
                        last = nc.tensor.matmul(bank[b][:, 0:TW], lhsT, wtok[:, f, :], start=f == 0, stop=f == 1)
                    last.then_inc(s["tok_psum"], 1)

                def qk_product(c):
                    m = 4 * i + c
                    pe.wait_ge(s["xnT_taken"], 2 + 3 * i + 3)
                    pe.wait_ge(s["qk_taken"], m + 1)
                    for f in range(2):
                        last = nc.tensor.matmul(bank[2 + c % 2][0:DH, 0:PC], wqk[:, f, DH * c:DH * (c + 1)],
                                                xnT[:, w, f, :], start=f == 0, stop=f == 1)
                    last.then_inc(s["qk_psum"], 1)

                def hidden_transpose(k):
                    n = 3 * i + k
                    pe.wait_ge(s["tok_taken"], 2 + n + 1)
                    pe.wait_ge(s["sgT_taken"], n + 1)
                    nc.tensor.transpose(bank[6][:, 0:128], sg[:, (w + k) % 2, :], C("ident")).then_inc(s["sgT_psum"], 1)

                def gate_product(k):
                    n = 3 * i + k
                    pe.wait_ge(s["sgT_taken"], 1 + n + 1)
                    pe.wait_ge(s["par_taken"], n + 1)
                    nc.tensor.matmul(bank[7][:, 0:5 * NH], sgT[:, (w + k) % 2, :], wb2[:, :], start=True,
                                     stop=True).then_inc(s["par_psum"], 1)

                def next_rows(k):
                    if not final:
                        row_transpose(i + 1, 1 - w, k)

                token_product(0)
                token_product(1)
                qk_product(0)
                token_product(2)
                hidden_transpose(0)
                next_rows(0)
                qk_product(1)
                hidden_transpose(1)
                next_rows(1)
                gate_product(0)
                qk_product(2)
                hidden_transpose(2)
                next_rows(2)
                gate_product(1)
                qk_product(3)
                gate_product(2)

            for k in range(3):
                row_transpose(0, 0, k)
            with pe.Fori(0, PAIRS // 2 - 1) as it:
                products(it * 2, 0)
                products(it * 2 + 1, 1)
            products(PAIRS - 2, 0)
            products(PAIRS - 1, 1, final=True)

            pe.sem_inc(s["scores_psum"], 2)
            pe.sem_inc(s["state_psum"], 1)
            pe.sem_inc(s["text_out_done"], DEPTH)
            pe.sem_inc(s["out_psum"], 2)
            with pe.Fori(0, PAIRS // 2) as it:
                for par_i in range(2):
                    i, w = it * 2 + par_i, par_i
                    pe.wait_ge(s["staged"], i + 1)
                    pe.wait_ge(s["kft_taken"], i + 1)
                    for f in range(2):
                        last = nc.tensor.transpose(bank[6][:, DH * f:DH * (f + 1)], kimg[:, w, f, :],
                                                   C("ident", DH)[:, 0:DH])
                    last.then_inc(s["kft_psum"], 1)

                    def scores(t):
                        f, b, tri = t // 4, t // 2 % 2, t % 2
                        if b == 0 and tri == 0:
                            pe.wait_ge(s["qbd_ready"], 2 * i + f + 1)
                        pe.wait_ge(s["scores_taken"], 8 * i + t + 1)
                        nc.tensor.matmul(bank[tri][:, 0:384], kst[:, w, f, b * L + NI:(b + 1) * L],
                                         qbd[:, f, 3 * tri:3 * tri + 3, b * L + NI:(b + 1) * L],
                                         start=True, stop=True).then_inc(s["scores_psum"], 1)

                    def image_scores(f):
                        if f == 0:
                            pe.wait_ge(s["out_taken"], i + 1)
                            pe.wait_ge(s["si_taken"], i + 1)
                        for b2 in range(2):
                            last = nc.tensor.matmul(bank[2][64 * b2:64 * b2 + 64, HH * NI * f:HH * NI * (f + 1)],
                                                    kimg[:, w, f, 64 * b2:64 * b2 + 64],
                                                    qbd[:, f, :, b2 * L:b2 * L + NI], start=True, stop=True)
                        last.then_inc(s["img_scores_psum"], 1)

                    def text_out(t):
                        f, b, tri = t // 4, t // 2 % 2, t % 2
                        pe.wait_ge(s["low_ready"], DEPTH + 8 * i + t + 1)
                        for k in range(3):
                            unit = NH * b + HH * f + 3 * tri + k
                            at, col = bank[3 + unit // UB], 3 * VE * (unit % UB)
                            begins = (t, k) in ((0, 0), (2, 0))
                            for q in range(3):
                                last = nc.tensor.matmul(at[:, col:col + VE * (3 - q)], smp[:, q, t % DEPTH, 128 * k:128 * (k + 1)],
                                                        vp[:, w, unit, 0:3 - q, :].rearrange("p q e -> p (q e)"),
                                                        start=begins and q == 0, stop=False, skip_group_check=True)
                        last.then_inc(s["text_out_done"], 1)

                    scores(0)
                    pe.wait_ge(s["kft_taken"], 1 + i + 1)
                    pe.wait_ge(s["vg_ready"], i + 1)
                    pe.wait_ge(s["sbd_taken"], i + 1)
                    for b in range(2):
                        for f in range(2):
                            last = nc.tensor.matmul(bank[7 - b][0:DH, HH * VE * f:HH * VE * (f + 1)],
                                                    kft[64 * b:64 * b + NI, DH * f:DH * (f + 1)],
                                                    vst[64 * b:64 * b + NI, w, 2, HH * f:HH * (f + 1), :].rearrange("p h e -> p (h e)"),
                                                    start=True, stop=True)
                    last.then_inc(s["state_psum"], 1)
                    scores(1)
                    pe.wait_ge(s["out_taken"], i + 1)
                    pe.wait_ge(s["value_parts_ready"], i + 1)
                    image_scores(0)
                    for t in range(2, 8):
                        scores(t)
                        if t == 4:
                            image_scores(1)
                        if t >= 3:
                            text_out(t - 3)
                    text_out(5)
                    pe.wait_ge(s["sbd_taken"], 1 + i + 1)
                    for b, h0, h1 in ((0, 0, 6), (0, 6, 9), (0, 9, 12), (1, 0, 6), (1, 6, 12)):
                        f, unit = h0 // HH, NH * b + h0
                        dst = bank[3 + unit // UB][:, 3 * VE * (unit % UB):3 * VE * (unit % UB + h1 - h0)]
                        begins = unit == 2 * UB
                        nc.tensor.matmul(dst.rearrange("p (u q) -> p u q", q=3 * VE)[:, :, 0:VE],
                                         qst[:, w, f, b * L + NI:(b + 1) * L], sbd[:, b, f, VE * (h0 - HH * f):VE * (h1 - HH * f)],
                                         start=begins, stop=not begins, skip_group_check=True)
                    pe.wait_ge(s["si_taken"], 1 + i + 1)
                    for b in range(2):
                        text_out(6 + b)
                        for hd in range(NH):
                            last = nc.tensor.matmul(bank[2][64 * b:64 * b + 64, VE * hd:VE * (hd + 1)],
                                                    si[64 * b:64 * b + 64, NI * hd:NI * hd + 64],
                                                    vst[64 * b:64 * b + 64, w, 2, hd, :],
                                                    start=hd == 0, stop=hd == NH - 1, skip_group_check=True)
                    last.then_inc(s["out_psum"], 1)

            pe.sem_inc(s["uhT_psum"], 6)
            pe.sem_inc(s["proj_psum"], 2)
            pe.sem_inc(s["x2T_psum"], 6)
            pe.sem_inc(s["logit_psum"], 2)
            for src, ready, psum, taken, dst, used, done, wgt, cols in (
                    (uh, "uh_ready", "uhT_psum", "uhT_taken", oT, "proj_taken", "proj_psum", wp, D),
                    (x2, "x2_ready", "x2T_psum", "x2T_taken", x2T, "logit_taken", "logit_psum", gw, NE + 1)):
                def rows_out(i, w, k):
                    n, b = 3 * i + k, (w + k) % 2
                    if k == 0:
                        pe.wait_ge(s[ready], i + 1)
                    pe.wait_ge(s[taken], n + 1)
                    for f in range(2):
                        last = nc.tensor.transpose(bank[b][0:DH, 128 * f:128 * (f + 1)],
                                                   src[:, w, k, DH * f:DH * (f + 1)], C("ident"))
                    last.then_inc(s[psum], 1)

                def rows_in(i, w, k):
                    n, b = 3 * i + k, (w + k) % 2
                    pe.wait_ge(s[taken], 2 + n + 1)
                    pe.wait_ge(s[used], n + 1)
                    nc.tensor.matmul(bank[2 + b][:, 0:cols], dst[0:DH, b, 0:128], wgt[0:DH, 0, :], start=True, stop=False)
                    nc.tensor.matmul(bank[2 + b][:, 0:cols], dst[0:DH + 1, b, 128:256], wgt[0:DH + 1, 1, :], start=False,
                                     stop=True).then_inc(s[done], 1)

                def through(i, w, final=False):
                    rows_in(i, w, 0)
                    rows_out(i, w, 2)
                    rows_in(i, w, 1)
                    if not final:
                        rows_out(i + 1, 1 - w, 0)
                    rows_in(i, w, 2)
                    if not final:
                        rows_out(i + 1, 1 - w, 1)

                rows_out(0, 0, 0)
                rows_out(0, 0, 1)
                with pe.Fori(0, PAIRS // 2 - 1) as it:
                    through(it * 2, 0)
                    through(it * 2 + 1, 1)
                through(PAIRS - 2, 0)
                through(PAIRS - 1, 1, final=True)
            pe.wait_ge(s["choices_ready"], 1)
            nc.tensor.matmul(bank[4][:, 0:2 * SLOTS * NE], beforeb[:, :], ohb[:, :, :].rearrange("p s e -> p (s e)"),
                             start=True, stop=True)
            nc.tensor.matmul(bank[5][:, 0:2 * SLOTS * NE], onesb[:, :], ohb[:, :, :].rearrange("p s e -> p (s e)"),
                             start=True, stop=True).then_inc(s["ranks_psum"], 1)

            pe.sem_inc(s["l1_psum"], 2)
            pe.sem_inc(s["hT_psum"], 2)
            pe.sem_inc(s["xgT_psum"], 1)
            pe.sem_inc(s["y_psum"], 1)

            def token_transpose(t, j, loads, first=False):
                pe.wait_ge(s[f"xg_in{j}"], 16 * loads)
                if not first:
                    pe.wait_ge(s["xgT_taken"], t)
                for f in range(2):
                    last = nc.tensor.transpose(bank[0][0:DH, 128 * f:128 * (f + 1)], xg[:, j, 2 + DH * f:2 + DH * (f + 1)],
                                               C("ident"))
                last.then_inc(s["xgT_psum"], 1)

            def layer1(t, w):
                e = pe.value_load(eid[0:1, ds(t, 1)], min_val=0, max_val=NE - 1)
                pe.wait_ge(s["xgT_taken"], t + 1)
                pe.wait_ge(s["hid_ready"], t + 1)
                for f in range(2):
                    for q in range(2):
                        m = DH + q
                        last = nc.tensor.matmul(bank[1 + 2 * w + f][:, 0:384], xgT[0:m, w, 128 * q:128 * (q + 1)],
                                                w1[0:m, q, ds(e * FF + 384 * f, 384)], start=q == 0, stop=q == 1)
                last.then_inc(s["l1_psum"], 1)

            pe.wait_ge(s["w1_in"], 16)
            pe.wait_ge(s["w2_in"], 16)
            pe.wait_ge(s["eid_ready"], 1)
            token_transpose(0, 0, 1, first=True)
            token_transpose(1, 1, 1)
            layer1(0, 0)
            with pe.Fori(0, TILES // 4) as it:
                for j in range(4):
                    t, w = it * 4 + j, j % 2
                    e0 = pe.value_load(eid[0:1, ds(t, 1)], min_val=0, max_val=NE - 1)
                    pe.wait_ge(s["hid_ready"], 2 + t + 1)
                    for f in range(2):
                        pe.wait_ge(s["hT_taken"], 2 * t + f + 1)
                        for q in range(3):
                            last = nc.tensor.transpose(bank[5 + f][:, 128 * q:128 * (q + 1)],
                                                       hid[:, w, 384 * f + 128 * q:384 * f + 128 * (q + 1)], C("ident"))
                        last.then_inc(s["hT_psum"] if f else s["hT_half"], 1)
                    token_transpose(t + 2, (j + 2) % 4, it + (j + 2) // 4 + 1)
                    layer1(t + 1, 1 - w)
                    for c in range(FC):
                        if c % 3 == 0:
                            pe.wait_ge(s["hT_taken"], 2 + 2 * t + c // 3 + 1)
                        if c == 0:
                            pe.wait_ge(s["y1_ready"], t + 1)
                        last = nc.tensor.matmul(bank[7][:, 0:D], hT[:, w, 128 * c:128 * (c + 1)], w2[:, c, ds(e0 * D, D)],
                                                start=c == 0, stop=c == FC - 1)
                    last.then_inc(s["y_psum"], 1)

        @block.vector
        def _(dve):
            ch = Chain(dve, s["dve_chain"])
            V = nc.vector
            dve.wait_ge(s["constants_in"], 16)
            dve.wait_ge(s["tokens_in"], 16)
            ch.done(V.tensor_scalar(tokneg, tok_i, 0, 64.0, ALU.is_lt, ALU.mult))
            ch.sync()
            ch.done(V.tensor_tensor(tok_f, tokneg, tok_i, ALU.add))
            ch.sync()
            V.tensor_scalar(tok_f, tok_f, 69.0, C("tok", 70), ALU.min, ALU.is_equal).then_inc(s["onehot_ready"], 1)
            dve.wait_ge(s["small_in"], 16 * SMALL)
            for f in range(2):
                V.tensor_scalar(wqk[:, f, :], wraw[:, f, 0:4 * DH], lnwb[:, f:f + 1], None, ALU.mult)
                V.tensor_scalar(wtok[:, f, 0:D], wraw[:, f, 4 * DH:4 * DH + D], lnwb[:, f:f + 1], None, ALU.mult)
                V.tensor_copy(wtok[:, f, D:TW], wraw[:, f, 4 * DH + D:])
                V.tensor_scalar(wp[0:DH, f, :], wp_raw[:, f, :], mnwb[:, 0:1], None, ALU.mult)
            V.tensor_scalar(temp[:, 1:2], temp[:, 0:1], 0.1, 2.0, ALU.max, ALU.min)
            dve.wait_ge(s["attn_bias_sums"], 1)
            V.tensor_tensor(bqk[:, :], bank[3][0:DH, 100:104], bqk0[:, :], ALU.add)
            V.tensor_tensor(bv[:, :], bank[7][:, D:2 * D], bv0[:, :], ALU.add)
            V.tensor_tensor(wp[DH:DH + 1, 1, :], bank[7][DH:DH + 1, 0:D], bproj[DH:DH + 1, :],
                            ALU.add).then_inc(s["attn_weights_ready"], 1)
            wq = [wpatch[:, NK * q:NK * (q + 1), :] for q in range(SHIFTS)]
            V.tensor_copy(weff[:, :, D], C("mult", KP))
            for q in range(SHIFTS):
                dve.wait_ge(s["beta_sums"], q + 1)
                ch.done(V.tensor_tensor(wq[q], wq[q], gb[:, NK * q:NK * (q + 1)].unsqueeze(2).to_broadcast([KP, NK, D]), ALU.mult))
                if q >= 2:
                    ch.sync()
                    ch.done(V.tensor_tensor(wq[q - 1], wq[q - 1], wq[q - 2], ALU.add))
            ch.sync()
            V.tensor_tensor(weff[:, :, 0:D], wq[SHIFTS - 2], wq[SHIFTS - 1], ALU.add).then_inc(s["weff_ready"], 1)
            ch.done(V.tensor_tensor(tokb, bank[6][:, 0:D], tb, ALU.add))
            text = [3 * (b // 2) + b % 2 for b in range(B)]
            for b in range(B):
                dve.wait_ge(s["text_psum"], b + 1)
                V.scalar_tensor_tensor(h[:, text[b], :], bank[4 + b % 2][:, 0:D], float(D) ** 0.5, C("pe"),
                                       ALU.mult, ALU.add).then_inc(s["text_taken"], 1)
            for g in range(PAIRS):
                dve.wait_ge(s["squares_weighted"], g + 1)
                V.tensor_reduce(xss[:, 128 * g:128 * (g + 1)], xsq[:, g % 2].rearrange("p k n -> p n k"), AX.X,
                                ALU.add).then_inc(s["squares_folded"], 1)
            dve.wait_ge(s["text_taken"], B)
            for b in range(B):
                ch.done(V.bn_stats(st[:, text[b], :], h[:, text[b], :]))
            ch.sync()
            for b in range(B):
                V.bn_aggr(mv[:, text[b], :], st[:, text[b], :])
            dve.wait_ge(s["gain_sums"], 1)
            ch.done(V.tensor_copy(gsum, bank[7][:, 0:D]))
            img = lambda g: h[:, 3 * g + 2, :]
            dve.wait_ge(s["square_sums"], 1)
            ch.done(V.tensor_scalar(istat[:, 1, :], bank[3][:, 0:PAIRS], 1.0 / PDIM, None, ALU.mult))
            for n, (g0, g1) in enumerate(GROUPS):
                dve.wait_ge(s["patch_sums"], g1)
                for g in range(g0, g1):
                    ch.done(V.tensor_scalar(istat[:, 0, g:g + 1], pbank[g // 2][:, (D + 1) * (g % 2) + D:(D + 1) * (g % 2 + 1)],
                                            1.0 / PDIM, None, ALU.mult))
                ch.sync()
                ch.done(V.tensor_tensor(istat[:, 2, g0:g1], istat[:, 0, g0:g1], istat[:, 0, g0:g1], ALU.mult))
                ch.sync()
                ch.done(V.tensor_tensor(istat[:, 3, g0:g1], istat[:, 1, g0:g1], istat[:, 2, g0:g1], ALU.subtract))
                ch.sync()
                V.tensor_scalar(istat[:, 3, g0:g1], istat[:, 3, g0:g1], 0.0, None, ALU.max).then_inc(s["ivar_ready"], 1)
                ch.done(V.tensor_scalar(istat[:, 6, g0:g1], istat[:, 0, g0:g1], -1.0, None, ALU.mult))
                ch.sync()
                for g in range(g0, g1):
                    ch.done(V.scalar_tensor_tensor(img(g), gsum, istat[:, 6, g:g + 1],
                                                   pbank[g // 2][:, (D + 1) * (g % 2):(D + 1) * (g % 2) + D], ALU.mult, ALU.add))
                dve.wait_ge(s["isd_ready"], n + 1)
                ch.done(V.reciprocal(istat[:, 5, g0:g1], istat[:, 4, g0:g1]))
                ch.sync()
                for g in range(g0, g1):
                    ch.done(V.scalar_tensor_tensor(img(g), img(g), istat[:, 5, g:g + 1], tokb, ALU.mult, ALU.add))
                ch.sync()
                for g in range(g0, g1):
                    ch.done(V.bn_stats(st[:, 3 * g + 2, :], img(g)))
                ch.sync()
                for g in range(g0, g1):
                    last = V.bn_aggr(mv[:, 3 * g + 2, :], st[:, 3 * g + 2, :])
                last.then_inc(s["stats_ready"], 1)
            dve.wait_ge(s["sd_ready"], 1)
            ch.done(V.reciprocal(ln[:, 1, :], ln[:, 0, :]))
            ch.sync()
            ch.done(V.tensor_tensor(ln[:, 2, :], mv[:, :, 1], ln[:, 1, :], ALU.mult))
            ch.sync()
            V.tensor_tensor(ln[:, 2, :], ln[:, 2, :], ln[:, 1, :], ALU.mult).then_inc(s["varx_ready"], 1)
            dve.wait_ge(s["sd_ready"], 2)
            ch.done(V.reciprocal(ln[:, 4, :], ln[:, 3, :]))
            ch.sync()
            V.tensor_scalar(ln[:, 5, :], ln[:, 3, :], 0.5, None, ALU.mult)
            V.tensor_tensor(ln[:, 4, :], ln[:, 4, :], ln[:, 1, :], ALU.mult).then_inc(s["ln_ready"], 1)

            dve.sem_inc(s["qk_done"], 6)
            dve.sem_inc(s["tok_taken"], 2)
            dve.sem_inc(s["par_taken"], 1)
            dve.wait_ge(s["ln_ready"], 1)
            dve.wait_ge(s["attn_weights_ready"], 1)

            def norm_rows(i, w):
                dve.wait_ge(s["xnT_psum"], 3 * i + 3)
                for k in range(3):
                    n = 3 * i + k
                    V.tensor_scalar(xn[:, w, k, :], h[:, ds(n, 1), :].rearrange("p a n -> p (a n)"), mv[:, ds(n, 1), 0],
                                    ln[:, 4, ds(n, 1)], ALU.subtract, ALU.mult).then_inc(s["xn_ready"], 1)

            def finish_products(i, w, final=False):
                if not final:
                    norm_rows(i + 1, 1 - w)
                for k in range(3):
                    n, b = 3 * i + k, (w + k) % 2
                    dve.wait_ge(s["tok_psum"], 6 + n + 1)
                    dve.wait_ge(s["th_ready"], 2 + n + 1)
                    V.tensor_tensor(vx[:, ds(n, 1), :, :].rearrange("p a h e -> p (a h) e"),
                                    bank[4 + b][:, 0:D].rearrange("p (h e) -> p h e", h=NH),
                                    bv[:, :].rearrange("p (h e) -> p h e", h=NH), ALU.add)
                    dve.wait_ge(s["sgT_psum"], n + 1)
                    V.scalar_tensor_tensor(sg[:, b, :], th[:, b, :], 1.0, bank[4 + b][:, D:TW], ALU.add,
                                           ALU.mult).then_inc(s["tok_taken"], 1)

                def qk_finish(c):
                    m = 4 * i + c
                    dve.wait_ge(s["qk_taken"], 2 + m + 1)
                    V.scalar_tensor_tensor(qk[:, c, ds(i * PC, PC)], ek[:, c % 2, :], 1.0, rk[:, c % 2, :], ALU.min,
                                           ALU.add).then_inc(s["qk_done"], 1)

                def gate_take(k):
                    n = 3 * i + k
                    dve.wait_ge(s["par_psum"], 2 + n + 1)
                    V.tensor_scalar(par[:, ds(n, 1), :].rearrange("p a n -> p (a n)"), bank[7][:, 0:5 * NH],
                                    ln[:, 5, ds(n, 1)], None, ALU.mult).then_inc(s["par_taken"], 1)

                qk_finish(0)
                qk_finish(1)
                gate_take(0)
                qk_finish(2)
                gate_take(1)
                qk_finish(3)
                gate_take(2)

            norm_rows(0, 0)
            with dve.Fori(0, PAIRS // 2 - 1) as it:
                finish_products(it * 2, 0)
                finish_products(it * 2 + 1, 1)
            finish_products(PAIRS - 2, 0)
            finish_products(PAIRS - 1, 1, final=True)

            dve.wait_ge(s["gate_tanh"], 1)
            ch.done(V.tensor_scalar(gt[:, 0, :], gt[:, 0, :], 1.0, None, ALU.add))
            V.tensor_tensor(gt[:, 1, :], gt[:, 1, :], gt[:, 3, :], ALU.subtract).then_inc(s["phase_ready"], 1)
            ch.sync()
            ch.done(V.scalar_tensor_tensor(gt[:, 0, :], gt[:, 2, :], 1.0, gt[:, 0, :], ALU.add, ALU.mult))
            dve.wait_ge(s["sin_ready"], 1)
            ch.done(V.tensor_tensor(gt[:, 4, :], gt[:, 3, :], gt[:, 3, :], ALU.mult))
            ch.sync()
            ch.done(V.tensor_scalar(gt[:, 4, :], gt[:, 4, :], -2.0, 1.0, ALU.mult, ALU.add))
            ch.done(V.tensor_scalar(temp[:, 1:2], temp[:, 1:2], 0.5, None, ALU.mult))
            ch.sync()
            V.tensor_tensor(gt[:, 0, :], gt[:, 0, :], gt[:, 4, :], ALU.mult).then_inc(s["inter_ready"], 1)
            dve.wait_ge(s["gate_ready"], 1)
            ch.done(V.tensor_scalar(gt[:, 4, :], gt[:, 2, :], 0.5, 1.5, ALU.mult, ALU.add))
            ch.done(V.memset(si[:, NH * NI:], 0.0))
            ch.done(V.memset(vst[:, :, :, :, HD:VE], 1.0))
            ch.sync()

            dve.sem_inc(s["si_taken"], 1)
            dve.sem_inc(s["scores_taken"], 2)
            dve.sem_inc(s["rest_ready"], 2)
            dve.sem_inc(s["sbd_taken"], 1)
            dve.sem_inc(s["out_taken"], 1)
            def expand(i, f):
                for k in range(HH):
                    last = V.tensor_scalar(qbd[:, f, k, :], qk[:, f, ds(i * PC, PC)], C("hmask", DH)[:, k:k + 1],
                                           None, ALU.mult)
                last.then_inc(s["qbd_ready"], 1)

            def gate_values(i, w):
                dve.wait_ge(s["out_psum"], i + 1)
                V.tensor_tensor(vst[:, w, :, :, 0:HD].rearrange("p s h e -> p (s h) e"),
                                vx[:, ds(3 * i, 3), :, :].rearrange("p s h e -> p (s h) e"),
                                gt[:, 4, ds(3 * NH * i, 3 * NH)].unsqueeze(2).to_broadcast([128, 3 * NH, HD]),
                                ALU.mult).then_inc(s["vg_ready"], 1)

            def rows_of(i):
                return [u[:, ds(3 * i + k, 1), :].rearrange("p a (h e) -> p (a h) e", h=NH) for k in range(3)]

            def centre(i):
                dve.wait_ge(s["out_taken"], 1 + i + 1)
                for k in range(3):
                    last = V.tensor_reduce(lnr[:, 0, ds(3 * NH * i + NH * k, NH)], rows_of(i)[k], AX.X, ALU.add)
                last.then_inc(s["head_sums"], 1)
                dve.wait_ge(s["head_sums"], i + 1)
                for k in range(3):
                    last = V.scalar_tensor_tensor(rows_of(i)[k], lnr[:, 0, ds(3 * NH * i + NH * k, NH)].unsqueeze(2).to_broadcast([128, NH, HD]),
                                                  -1.0 / HD, rows_of(i)[k], ALU.mult, ALU.add)
                last.then_inc(s["uc_ready"], 1)

            def attention_masks(i, w, first=False, final=False):
                ch.k = 0
                ch.at(i)

                def mask(t):
                    tri = t % 2
                    dve.wait_ge(s["scores_psum"], 2 + 8 * i + t + 1)
                    dve.wait_ge(s["rest_ready"], 8 * i + t + 1)
                    V.tensor_tensor(sm[:, tri, :].rearrange("p (h n) -> p h n", h=3),
                                    bank[tri][:, 0:384].rearrange("p (h n) -> p h n", h=3),
                                    C("causal").unsqueeze(1).to_broadcast([128, 3, 128]), ALU.mult).then_inc(s["scores_taken"], 1)

                def rest(t):
                    dve.wait_ge(s["high_ready"], 2 + 8 * i + t + 1)
                    dve.wait_ge(s["low_ready"], 8 * i + t + 1)
                    dve.wait_ge(s["scores_taken"], 2 + 8 * i + t + 1)
                    V.tensor_tensor(sr[:, t % DEPTH], sm[:, t % 2], smp[:, 0, t % DEPTH], ALU.subtract).then_inc(s["rest_ready"], 1)

                mask(0)
                mask(1)
                rest(0)
                dve.wait_ge(s["state_psum"], 1 + i + 1)
                for b in range(2):
                    last = V.tensor_tensor(sbd[:, b], bank[7 - b][0:DH, 0:2 * HH * VE].rearrange("p (c n) -> p c n", c=2),
                                           C("blk", DH).unsqueeze(1).to_broadcast([DH, 2, HH * VE]), ALU.mult)
                last.then_inc(s["sbd_taken"], 1)
                for t in range(2, 8):
                    mask(t)
                    rest(t - 1)
                    if t == 3 and not first:
                        centre(i - 1)
                    if t == 5 and not final:
                        gate_values(i + 1, 1 - w)
                    if t == 6:
                        dve.wait_ge(s["img_scores_psum"], 2 * i + 2)
                        V.tensor_tensor(si[:, 0:NH * NI].rearrange("p (h n) -> p h n", h=NH),
                                        bank[2][:, 0:NH * NI].rearrange("p (h n) -> p h n", h=NH),
                                        C("icausal").unsqueeze(1).to_broadcast([128, NH, NI]), ALU.mult).then_inc(s["si_taken"], 1)
                rest(7)
                if not final:
                    expand(i + 1, 0)
                    expand(i + 1, 1)
                else:
                    head_variances(0, PAIRS - 1)
                dve.wait_ge(s["out_psum"], 2 + i + 1)
                for g in range(3):
                    u0, u1 = UB * g, min(UB * (g + 1), 2 * NH)
                    last = V.tensor_reduce(osum[:, u0:u1, :],
                                           bank[3 + g][:, 0:3 * VE * (u1 - u0)].rearrange("p (u q e) -> p u e q", q=3, e=VE), AX.X, ALU.add)
                V.tensor_scalar(rden[:, 2, :], bank[2][:, 0:NH * VE].rearrange("p (h e) -> p h e", h=NH)[:, :, HD], 1e-6, None, ALU.add)
                ch.done(last)
                ch.sync()
                ch.done(V.tensor_scalar(rden[:, 0:2, :].rearrange("p k h -> p (k h)"), osum[:, :, HD], 1e-6, None, ALU.add))
                ch.sync()
                ch.done(V.reciprocal(rden[:, :, :], rden[:, :, :]))
                ch.sync()
                o = [osum[:, NH * k:NH * (k + 1), :] for k in range(2)] + [bank[2][:, 0:NH * VE].rearrange("p (h e) -> p h e", h=NH)]
                for k in range(3):
                    last = V.tensor_tensor(rows_of(i)[k], o[k][:, :, 0:HD],
                                           rden[:, k, :].unsqueeze(2).to_broadcast([128, NH, HD]), ALU.mult)
                last.then_inc(s["out_taken"], 1)

            def head_variances(i0, i1):
                n = 1 if i0 == 0 else 2
                lo, hi = 3 * NH * i0, 3 * NH * i1
                dve.wait_ge(s["usq_ready"], i1)
                V.tensor_reduce(lnr[:, 1, lo:hi], usq[:, 3 * i0:3 * i1, :].rearrange("p s (h e) -> p (s h) e", h=NH), AX.X,
                                ALU.add).then_inc(s["hvar_ready"], 1)
                dve.wait_ge(s["hsd_ready"], n)
                V.reciprocal(lnr[:, 2, lo:hi], lnr[:, 2, lo:hi]).then_inc(s["head_scales"], 1)

            expand(0, 0)
            expand(0, 1)
            gate_values(0, 0)
            ch.enter(3)
            attention_masks(0, 0, first=True)
            with dve.Fori(0, PAIRS // 2 - 1) as it:
                attention_masks(it * 2 + 1, 1)
                attention_masks(it * 2 + 2, 0)
            attention_masks(PAIRS - 1, 1, final=True)
            centre(PAIRS - 1)
            ch.leave(PAIRS)

            head_variances(PAIRS - 1, PAIRS)
            dve.wait_ge(s["head_scales"], 2)
            ch.done(V.memset(oT[DH:DH + 1], 1.0))
            ch.done(V.memset(x2T[DH:DH + 1], 1.0))
            ch.sync()
            dve.sem_inc(s["proj_taken"], 2)
            dve.sem_inc(s["logit_taken"], 2)

            def head_norm(i, w):
                dve.wait_ge(s["uhT_psum"], 3 * i + 3)
                for k in range(3):
                    last = V.tensor_tensor(uh[:, w, k].rearrange("p (h e) -> p h e", h=NH),
                                           u[:, ds(3 * i + k, 1), :].rearrange("p a (h e) -> p (a h) e", h=NH),
                                           lnr[:, 2, ds(3 * NH * i + NH * k, NH)].unsqueeze(2).to_broadcast([128, NH, HD]), ALU.mult)
                last.then_inc(s["uh_ready"], 1)

            def residual(i, w):
                for k in range(3):
                    hr = h[:, ds(3 * i + k, 1), :].rearrange("p a n -> p (a n)")
                    dve.wait_ge(s["proj_psum"], 2 + 3 * i + k + 1)
                    V.tensor_tensor(hr, hr, bank[2 + (w + k) % 2][:, 0:D], ALU.add).then_inc(s["proj_taken"], 1)

            def residual_stats(i):
                dve.wait_ge(s["proj_taken"], 2 + 3 * i + 3)
                for k in range(3):
                    last = V.bn_stats(st[:, ds(3 * i + k, 1), :].rearrange("p a n -> p (a n)"), h[:, ds(3 * i + k, 1), :].rearrange("p a n -> p (a n)"))
                last.then_inc(s["stats2_done"], 1)

            EARLY = 3 * (PAIRS - 2)
            head_norm(0, 0)
            head_norm(1, 1)
            with dve.Fori(0, PAIRS // 2 - 1) as it:
                for w in range(2):
                    residual(it * 2 + w, w)
                    head_norm(it * 2 + w + 2, w)
                    residual_stats(it * 2 + w)
            dve.wait_ge(s["stats2_done"], PAIRS - 2)
            for n in range(EARLY):
                V.bn_aggr(mv[:, n, :], st[:, n, :])
            for w in range(2):
                residual(PAIRS - 2 + w, w)
                residual_stats(PAIRS - 2 + w)
            dve.wait_ge(s["stats2_done"], PAIRS)
            for n in range(EARLY, SLOTS):
                last = V.bn_aggr(mv[:, n, :], st[:, n, :])
            last.then_inc(s["means2_ready"], 1)
            dve.wait_ge(s["sd2_ready"], 1)
            ch.done(V.reciprocal(ln[:, 1, :], ln[:, 0, :]))
            ch.sync()

            def token_norm(i, w):
                dve.wait_ge(s["x2T_psum"], 3 * i + 3)
                dve.wait_ge(s["first_copied"], i + 1)
                dve.wait_ge(s["second_copied"], i + 1)
                for k in range(3):
                    last = V.tensor_scalar(x2[:, w, k], h[:, ds(3 * i + k, 1), :].rearrange("p a n -> p (a n)"), mv[:, ds(3 * i + k, 1), 0],
                                           ln[:, 1, ds(3 * i + k, 1)], ALU.subtract, ALU.mult)
                last.then_inc(s["x2_ready"], 1)

            def choose(i, w):
                for k in range(3):
                    dve.wait_ge(s["logit_psum"], 2 + 3 * i + k + 1)
                    V.tensor_copy(lg[:, ds(3 * i + k, 1), :].rearrange("p a n -> p (a n)"),
                                  bank[2 + (w + k) % 2][:, 0:NE + 1]).then_inc(s["logit_taken"], 1)

            def best(n0, n1):
                for n in range(n0, n1):
                    ch.done(V.max(m8[:, n, :], lg[:, n, 0:NE]))
                ch.sync()
                for n in range(n0, n1):
                    ch.done(V.max_index(ix[:, n, :], m8[:, n, :], lg[:, n, 0:NE]))
                ch.sync()

            token_norm(0, 0)
            token_norm(1, 1)
            with dve.Fori(0, PAIRS // 2 - 1) as it:
                for w in range(2):
                    choose(it * 2 + w, w)
                    token_norm(it * 2 + w + 2, w)
            dve.wait_ge(s["logit_taken"], 2 + EARLY)
            best(0, EARLY)
            for w in range(2):
                choose(PAIRS - 2 + w, w)
            dve.wait_ge(s["logit_taken"], 2 + SLOTS)
            best(EARLY, SLOTS)
            V.tensor_scalar(vtok[:, :], lg[:, :, NE], -3.0, 3.0, ALU.max, ALU.min).then_inc(s["v_ready"], 1)
            V.tensor_tensor(wk[:, 0, :], m8[:, :, 1], m8[:, :, 0], ALU.subtract).then_inc(s["gap_ready"], 1)
            for k in range(2):
                ch.done(V.tensor_copy(ixf[:, k, :], ix[:, :, k]))
            V.tensor_copy(beforeb[:, :], C("before"))
            ch.done(V.memset(onesb[:, :], 1.0))
            ch.sync()
            ch.done(V.tensor_tensor(ohf[:, :, :], ixf[:, :, :].rearrange("p k s -> p (k s)").unsqueeze(2).to_broadcast([128, 2 * SLOTS, NE]),
                                    C("iota8").unsqueeze(1).to_broadcast([128, 2 * SLOTS, NE]), ALU.is_equal))
            ch.sync()
            for k in range(2):
                last = V.tensor_tensor(ohb[:, k * SLOTS:(k + 1) * SLOTS, :], ohf[:, k * SLOTS:(k + 1) * SLOTS, :],
                                       C("valid").unsqueeze(2).to_broadcast([128, SLOTS, NE]), ALU.mult)
            last.then_inc(s["choices_ready"], 1)
            dve.wait_ge(s["ratio_ready"], 1)
            ch.done(V.tensor_scalar(wk[:, 0, :], wk[:, 1, :], 1.0, None, ALU.add))
            ch.sync()
            ch.done(V.reciprocal(wk[:, 0, :], wk[:, 0, :]))
            ch.sync()
            dve.wait_ge(s["first_copied"], 2 + PAIRS)
            dve.wait_ge(s["second_copied"], 2 + PAIRS)
            V.tensor_copy(rows[:, 0, :, 0], wk[:, 0, :])
            V.tensor_tensor(rows[:, 1, :, 0], wk[:, 0, :], wk[:, 1, :], ALU.mult)
            V.tensor_copy(rows[:, :, :, 1], C("place").rearrange("p (k s) -> p k s", k=2))
            dve.wait_ge(s["ranks_psum"], 1)
            ch.done(V.tensor_copy(tot[:, :, :], bank[5][:, 0:2 * SLOTS * NE].rearrange("p (s e) -> p e s", e=NE)))
            ch.sync()
            for e in range(NE):
                ch.done(V.tensor_tensor_scan(inc[:, e, :], ones[:, 0:2 * SLOTS], tot[:, e, :], 0.0, ALU.mult, ALU.add))
            ch.sync()
            ch.done(V.tensor_tensor(ohf[:, :, :].rearrange("p s e -> p (s e)").rearrange("p (e s) -> p e s", e=NE),
                                    inc[:, :, 2 * SLOTS - 1:2 * SLOTS].to_broadcast([128, NE, 2 * SLOTS]),
                                    C("steps").unsqueeze(1).to_broadcast([128, NE, 2 * SLOTS]), ALU.is_gt))
            ch.sync()
            ch.done(V.tensor_reduce(cnt[:, 0, :], ohf[:, :, :].rearrange("p s e -> p (s e)").rearrange("p (e s) -> p e s", e=NE), AX.X, ALU.add))
            ch.sync()
            ch.done(V.tensor_tensor_scan(cnt[:, 1, :], ones[:, 0:NE], cnt[:, 0, :], 0.0, ALU.mult, ALU.add))
            ch.sync()
            ch.done(V.tensor_tensor(cnt[:, 2, :], cnt[:, 1, :], cnt[:, 0, :], ALU.subtract))
            ch.sync()
            ch.done(V.tensor_scalar(cnt[:, 3, :], cnt[:, 2, :], 128.0, None, ALU.mult))
            ch.sync()
            ch.done(V.tensor_tensor(inc[:, :, :], inc[:, :, :], cnt[:, 3, :].unsqueeze(2).to_broadcast([128, NE, 2 * SLOTS]), ALU.add))
            ch.sync()
            ch.done(V.tensor_tensor(ohf[:, :, :], bank[4][:, 0:2 * SLOTS * NE].rearrange("p (s e) -> p s e", e=NE),
                                    inc[:, :, :].rearrange("p e s -> p s e"), ALU.add))
            ch.sync()
            ch.done(V.tensor_tensor(ohf[:, :, :], ohf[:, :, :], ohb[:, :, :], ALU.mult))
            ch.sync()
            ch.done(V.tensor_reduce(pos[:, :], ohf[:, :, :], AX.X, ALU.add))
            ch.sync()
            V.tensor_tensor(sidx[:, :], pos[:, :], C("trash"), ALU.add).then_inc(s["places_ready"], 1)
            ch.done(V.tensor_tensor(ecmp[:, :, :], cnt[0:1, 1, :].unsqueeze(1).to_broadcast([1, TILES + 2, NE]),
                                    C("tile8", 1).rearrange("p (t e) -> p t e", e=NE), ALU.is_le))
            ch.sync()
            ch.done(V.tensor_reduce(eidf[:, :], ecmp[:, :, :], AX.X, ALU.add))
            ch.sync()
            V.tensor_scalar(eid[:, :], eidf[:, :], NE - 1.0, None, ALU.min).then_inc(s["eid_ready"], 1)
            ch.done(V.memset(ga[:, :, 0], 0.0))
            ch.done(V.memset(ga[:, :, 1], -1.0))
            ch.done(V.memset(gtok[:, :, :], 0.0))
            ch.done(V.memset(xgT[DH:DH + 1], 1.0))
            for k in range(3):
                ch.done(V.tensor_tensor(spec[:, k, :], spec[:, k, :], spec[:, 3, :], ALU.mult))
            ch.sync()
            dve.wait_ge(s["v_in"], 32)
            ch.done(V.scalar_tensor_tensor(ga[:, 0:L, 0], vv[:, :], -2.0, C("sign", 32)[:, 0:L], ALU.add, ALU.mult))
            ch.sync()
            ch.done(V.tensor_copy(gs[:, 0, :], ga[:, 0, :]))
            ch.sync()

            def recurrence(first, steps):
                for g in range(steps):
                    now = gs[:, ds(first + g, 1), :].rearrange("p a c -> p (a c)")
                    nxt = gs[:, ds(first + g + 1, 1), :].rearrange("p a c -> p (a c)")
                    ch.done(V.scalar_tensor_tensor(gq[:, 2:4], now, 1.0, now, ALU.mult, ALU.mult, accum_out=gq[:, 0:1]))
                    ch.sync()
                    ch.done(V.reciprocal(gq[:, 1:2], gq[:, 0:1]))
                    ch.sync()
                    ch.done(V.scalar_tensor_tensor(nxt, now, gq[:, 1:2], ga[:, ds(first + g + 1, 1), :].rearrange("p a c -> p (a c)"),
                                                   ALU.mult, ALU.add))
                    ch.sync()

            ch.enter(3 * 4)
            with dve.Fori(0, GFIRST // 4) as it:
                ch.at(it)
                recurrence(it * 4, 4)
            ch.leave(GFIRST // 4)

            def green():
                dve.wait_ge(s["recurrence_done"], 1)
                dve.wait_ge(s["ge_in"], 16)
                ch.done(V.tensor_tensor(gg[:, 1, :], ge[:, :, 0], C("sign", B)[:, 0:L], ALU.mult))
                ch.sync()
                ch.done(V.tensor_tensor(gg[:, 0, :], gg[:, 0, :], gg[:, 1, ::-1], ALU.add))
                ch.done(V.tensor_tensor(gg[:, 2, :], gs[0:B, 0:L, 1], ge[:, ::-1, 1], ALU.add))
                ch.sync()
                ch.done(V.scalar_tensor_tensor(gg[:, 0, :], vv[0:B, :], -2.0, gg[:, 0, :], ALU.add, ALU.subtract))
                ch.done(V.tensor_scalar(gg[:, 2, :], gg[:, 2, :], 1.0, None, ALU.add))
                ch.sync()
                ch.done(V.tensor_tensor(gg[:, 1, :], gg[:, 0, :], gg[:, 0, :], ALU.mult))
                ch.done(V.tensor_tensor(gg[:, 3, :], gg[:, 2, :], gg[:, 2, :], ALU.mult))
                ch.sync()
                ch.done(V.tensor_tensor(gg[:, 1, :], gg[:, 1, :], gg[:, 3, :], ALU.add))
                ch.sync()
                ch.done(V.reciprocal(gg[:, 1, :], gg[:, 1, :]))
                ch.sync()
                for k in range(2):
                    ch.done(V.scalar_tensor_tensor(gg[:, 2 * k, :], gg[:, 2 * k, :], -1.0, gg[:, 1, :], ALU.mult, ALU.mult))
                ch.sync()
                for k in range(2):
                    last = V.tensor_scalar(g2[:, :, k], gg[:, 2 * k, :], -10.0, 10.0, ALU.max, ALU.min)
                last.then_inc(s["green_ready"], 1)

            def add_features(n, count):
                hr = [h[:, ds(n + m, 1), :].rearrange("p a n -> p (a n)") for m in range(count)]
                dve.wait_ge(s["gtok_in"], 64)
                for c in range(2):
                    for m in range(count):
                        ch.done(V.scalar_tensor_tensor(hr[m], spec[:, c, :], gtok[:, ds(n + m, 1), c], hr[m], ALU.mult, ALU.add))
                    ch.sync()
                for m in range(count):
                    ch.done(V.tensor_tensor(hr[m], hr[m], spec[:, 2, :], ALU.add))

            dve.sem_inc(s["hT_taken"], 2)
            dve.sem_inc(s["y1_ready"], 1)

            def take_tokens(t, j):
                dve.wait_ge(s["xgT_psum"], 1 + t + 1)
                V.tensor_copy(meta_w[:, j:j + 1], xg[:, j, 0:1])
                V.tensor_copy(meta_i[:, j:j + 1], xg[:, j, 1:2])
                V.tensor_copy(xgT[0:DH, j % 2, :], bank[0][0:DH, 0:256]).then_inc(s["xgT_taken"], 1)

            dve.wait_ge(s["eid_ready"], 1)
            dve.wait_ge(s["b2_in"], 16)
            take_tokens(0, 0)
            take_tokens(1, 1)

            def tile_steps(t, j, beside):
                w = j % 2
                e = dve.value_load(eid[0:1, ds(t, 1)], min_val=0, max_val=NE - 1)
                for f in range(2):
                    if f:
                        dve.wait_ge(s["hT_psum"], 2 + t + 1)
                    else:
                        dve.wait_ge(s["hT_half"], t + 1)
                        dve.wait_ge(s["y_psum"], t + 1)
                    V.tensor_copy(hT[:, w, 384 * f:384 * (f + 1)], bank[5 + f][:, 0:384]).then_inc(s["hT_taken"], 1)
                dve.wait_ge(s["turn_taken"], t + 1)
                take_tokens(t + 2, (j + 2) % 4)
                beside()
                dve.wait_ge(s["y_psum"], 1 + t + 1)
                dve.wait_ge(s["y2_ready"], t + 1)
                V.tensor_tensor(y1[:, w, :], bank[7][:, 0:D], b2b[:, ds(e * D, D)], ALU.add).then_inc(s["y1_ready"], 1)

            ch.enter(4 * 3 * GSTEP)
            with dve.Fori(0, GTILES // 4) as it:
                ch.at(it)
                for j in range(4):
                    t = it * 4 + j
                    tile_steps(t, j, lambda: recurrence(t * GSTEP + GFIRST, GSTEP))
            ch.leave(GTILES // 4)
            HALF = GREST // 2
            tile_steps(GTILES, 0, lambda: recurrence(L - GREST, HALF))
            tile_steps(GTILES + 1, 1, lambda: recurrence(L - GREST + HALF, GREST - HALF))
            V.tensor_tensor(gg[:, 0, :], gs[0:B, 0:L, 0], C("sign", B)[:, 0:L], ALU.mult).then_inc(s["recurrence_done"], 1)
            tile_steps(GTILES + 2, 2, green)
            tile_steps(GTILES + 3, 3, lambda: None)
            ch.enter(4 * 3 * FSLOTS)
            with dve.Fori(GTILES // 4 + 1, TILES // 4) as it:
                ch.at(it - (GTILES // 4 + 1))
                for j in range(4):
                    t = it * 4 + j
                    tile_steps(t, j, lambda: add_features((t - (GTILES + 4)) * FSLOTS, FSLOTS))
            ch.leave(TILES // 4 - GTILES // 4 - 1)

            ch.sync()
            V.tensor_copy(gq[:, 0:1], gq[:, 1:2]).then_inc(s["features_added"], 1)
            hv = h[:, :, :].rearrange("p (i j) n -> p j i n", j=3)
            pin = plane_in.rearrange("p k (i j) n -> p k j i n", j=3)
            for n, (lo, hi, j) in enumerate(((0, 128, 0), (0, 128, 1), (0, NI, 2))):
                for k in range(2):
                    dve.wait_ge(s[f"plane_in{n}"], 32)
                    last = V.tensor_tensor(hv[lo:hi, j], hv[lo:hi, j], pin[lo:hi, k, j], ALU.add)
                    if k == 0:
                        ch.done(last)
                        ch.sync()
                last.then_inc(s["total_ready"], 1)


def laid_out(inp):
    import numpy as np

    f = {k: np.asarray(v) for k, v in inp.items()}
    arr = {}
    x = f["x"]
    pad = np.pad(x, ((0, 0), (0, 0), (1, 1), (1, 1)))
    win = np.stack([pad[:, :, PATCH * p:PATCH * p + WIN, :] for p in range(SIDE)], 2)
    win = np.stack([win[..., PATCH * p:PATCH * p + WIN] for p in range(SIDE)], 3)
    win = win.reshape(B, CH, SIDE, SIDE, WIN, NK, 2).transpose(6, 1, 4, 5, 0, 2, 3).reshape(KP, NK, B, NI)
    arr["xwin"] = np.pad(win, ((0, 0), (0, 0), (0, 0), (0, 64 - NI))).reshape(KP, NK, PT)

    def windowed(t):
        n = t.shape[1]
        t = t.reshape(PATCH, PATCH, SHIFTS, CH, n)
        o = np.zeros((2, CH, WIN, SHIFTS, NK, n), t.dtype)
        for sft, (dr, dc) in enumerate(((1, 1), (1, 0), (1, 2), (0, 1), (2, 1))):
            for par in range(2):
                js = [j for j in range(PATCH) if (j + dc) % 2 == par]
                ks = [(j + dc) // 2 for j in js]
                o[par, :, dr:dr + PATCH, sft, ks[0]:ks[-1] + 1] = t[:, js, sft].transpose(2, 0, 1, 3)
        return o.reshape(KP, SHIFTS * NK, n)

    arr["wpatch"] = windowed(f["L0_tok_W"])
    arr["patch_gb"] = np.concatenate([windowed(f[k][:, None])[..., 0] for k in ("L0_tok_gamma", "L0_tok_beta")], 1)
    arr["tokens"] = f["x_txt"].reshape(B * NT)
    cw, sw, qw = f["L0_txt_color_W"], f["L0_txt_shape_W"], f["L0_txt_quantity_W"]
    t = np.arange(64)
    arr["table"] = np.concatenate([np.concatenate([cw[t // 16], sw[t % 16 // 4], qw[t % 4]], 1), f["L0_txt_special_W"]], 0)
    rep = lambda v: np.ascontiguousarray(np.broadcast_to(v, (128,) + v.shape))
    halved = lambda w: w.reshape(2, DH, -1).transpose(1, 0, 2)
    arr["tok_b"] = rep(f["L0_tok_b"])
    arr["wattn"] = np.concatenate([halved(f["L0_attn_Wqkv"]), halved(f["L0_attn_Wb1"])], 2)
    arr["lnwb"] = np.concatenate([f["L0_attn_ln_w"].reshape(2, DH).T, f["L0_attn_ln_b"].reshape(2, DH).T], 1)
    arr["bqk"] = f["L0_attn_bqkv"][0:4 * DH].reshape(4, DH).T
    arr["bv"] = rep(f["L0_attn_bqkv"][4 * DH:])
    arr["wb2"] = f["L0_attn_Wb2"]
    arr["temp"] = rep(f["L0_attn_temperature"])
    arr["wproj"] = halved(f["L0_attn_Wproj"])
    arr["mnwb"] = np.stack([np.tile(f["L0_attn_mn_w"], HH), np.tile(f["L0_attn_mn_b"], HH)], 1)
    arr["bproj"] = rep(f["L0_attn_bproj"])

    arr["gate_w"] = np.zeros((DH + 1, 2, NE + 1), np.float32)
    arr["gate_w"][0:DH] = halved(np.concatenate([f["L0_ffn_gate_w"], f["L0_ffn_v_w"][:, None]], 1))
    arr["gate_w"][DH, 1, 0:NE] = f["L0_ffn_gate_b"]
    arr["gate_w"][DH, 1, NE] = f["L0_ffn_v_b"]
    arr["w1"] = np.zeros((DH + 1, 2, NE * FF), np.float32)
    arr["w1"][0:DH] = f["L0_ffn_w1"].reshape(NE, 2, DH, FF).transpose(2, 1, 0, 3).reshape(DH, 2, NE * FF)
    arr["w1"][DH, 1] = f["L0_ffn_b1"].reshape(NE * FF)
    arr["w2"] = f["L0_ffn_w2"].reshape(NE, FC, 128, D).transpose(2, 1, 0, 3).reshape(128, FC, NE * D)
    arr["b2"] = rep(f["L0_ffn_b2"].reshape(NE * D))
    arr["spec"] = rep(np.stack([f["L0_ffn_out_w"][0], f["L0_ffn_out_w"][1], f["L0_ffn_out_b"], f["L0_ffn_bk_scale"]], 0))

    c = {}
    p = np.arange(128)
    pos = np.arange(NT, dtype=np.float32)[:, None]
    inv = np.exp(-(np.arange(0, D, 2, dtype=np.float32) / np.float32(D)) * np.float32(np.log(10000.0))).astype(np.float32)
    ang = pos * inv
    c["pe"] = np.stack([np.sin(ang), np.cos(ang)], -1).reshape(NT, D)
    c["ident"] = np.eye(128)
    c["causal"] = p[:, None] <= p[None, :]
    c["icausal"] = (p[:, None] % 64) <= np.arange(NI)[None, :]
    c["before"] = (p[:, None] < p[None, :]) - 1.0
    c["blk"] = (p[:, None] // HD) == (np.arange(HH * VE)[None, :] // VE)
    c["hmask"] = (p[:, None] // HD) == np.arange(HH)[None, :]
    ones = np.ones((PDIM, 1), np.float32)
    mult = windowed(ones)[..., 0].reshape(KP, SHIFTS, NK).sum(1)
    c["mult"] = np.concatenate([mult, np.zeros((128 - KP, NK))], 0)
    c["iota8"] = np.tile(np.arange(NE), (128, 1))
    valid = np.array([[k % 3 < 2 or q % 64 < NI for k in range(SLOTS)] for q in range(128)])
    c["valid"] = valid
    image = np.array([k // 3 for k in range(SLOTS)])
    c["trash"] = np.concatenate([np.where(valid, 0, SROWS + (k * PAIRS + image[None, :]) * 128 + p[:, None]) for k in range(2)], 1)
    seq = np.array([[2 * (k // 3) + (k % 3 if k % 3 < 2 else q // 64) for k in range(SLOTS)] for q in range(128)])
    tok = np.array([[NI + q if k % 3 < 2 else q % 64 for k in range(SLOTS)] for q in range(128)])
    c["place"] = np.concatenate([np.where(valid, k * PLANE + seq * L + tok, 0) for k in range(2)], 1)
    c["tile8"] = np.tile(np.repeat(np.arange(TILES + 2), NE), (128, 1))
    c["tok"] = p[:, None]
    c["steps"] = np.tile(128 * np.arange(2 * SLOTS), (128, 1))
    c["fill"] = np.concatenate([np.zeros((128, 1)), 2 * PLANE + p[:, None], np.zeros((128, D))], 1)
    c["sign"] = np.tile(1 - 2 * (np.arange(GLEN) % 2), (128, 1))
    packed = np.zeros((128, NCONST), np.float32)
    for k, (lo, hi) in CW.items():
        packed[:, lo:hi] = c[k]
    arr["consts"] = packed
    return {k: np.ascontiguousarray(v) for k, v in arr.items()}


def kernel(**inputs):
    import numpy as _np
    import concourse.bacc as _bacc
    from concourse import mybir as _mybir
    from concourse.bass_utils import run_bass_kernel_spmd as _run

    nc = _bacc.Bacc("TRN2", target_bir_lowering=False, num_devices=1)
    arrays = {f"in_{k}_dram": v for k, v in laid_out(inputs).items()}
    args = {k[3:-5]: nc.dram_tensor(k, v.shape, _mybir.dt.from_np(v.dtype), kind="ExternalInput").ap()
            for k, v in arrays.items()}
    out = nc.dram_tensor("out_0_dram", (B, L, D), _mybir.dt.float32, kind="ExternalOutput").ap()
    early_fusion_block(nc, args, out)
    r = _run(nc, [arrays], core_ids=[0])
    return r.results[0]["out_0_dram"]
```
